# Optimizing a Trainium2 kernel written in Bass

```python
import numpy as np
import jax
import jax.numpy as jnp

def _softmax(x, axis=-1):
    return jax.nn.softmax(x, axis=axis)

def _gelu(x):
    return jax.nn.gelu(x, approximate=True)

def _silu(x):
    return jax.nn.silu(x)

def _sigmoid(x):
    return jax.nn.sigmoid(x)

def _layernorm(x, axis=-1, eps=1e-05):
    m = jnp.mean(x, axis=axis, keepdims=True)
    v = jnp.var(x, axis=axis, keepdims=True)
    return (x - m) / jnp.sqrt(v + eps)

def _scatter_add(tgt, idx, src, axis=0):
    return tgt.at[idx].add(src)

def _segment_sum(src, seg, n):
    return jax.ops.segment_sum(src, seg, n)
kernel_name = 'mk_recurrent_d2_jaxref_r8_dd5486'

def setup_inputs(seed: int=0):
    np.random.seed(seed)
    _w = jnp.asarray

    def _L0_attn_setup():
        import jax, jax.numpy as jnp
        import numpy as np
        B, S, HID = (2, 256, 256)
        H = 16
        HD = HID // H
        HD2 = HD // 2
        LAT = HID // 8
        BASE = 10000.0

        def _rotary_table(seq_len):
            inv_freq = 1.0 / BASE ** (jnp.arange(0, HD2, 2, dtype=jnp.float32) / HD2)
            pos = jnp.arange(seq_len, dtype=jnp.float32)
            sincos = pos[:, None] * inv_freq[None, :]
            return jnp.concatenate([jnp.sin(sincos), jnp.cos(sincos)], axis=-1)

        def _apply_rope(x, emb):
            half = HD2 // 2
            x1, x2 = (x[..., :half], x[..., half:])
            sin = emb[None, :, None, :half]
            cos = emb[None, :, None, half:]
            return jnp.concatenate([x1 * cos - x2 * sin, x1 * sin + x2 * cos], axis=-1)
        key = jax.random.key(seed)
        ks = jax.random.split(key, 9)
        s = 0.02
        return {'hidden_states': jax.random.normal(ks[0], (B, S, HID), jnp.float32), 'w_kv_d': jax.random.normal(ks[1], (HID, LAT), jnp.float32) * s, 'w_q_d': jax.random.normal(ks[2], (HID, LAT), jnp.float32) * s, 'w_k_u': jax.random.normal(ks[3], (LAT, H * HD2), jnp.float32) * s, 'w_q_u': jax.random.normal(ks[4], (LAT, H * HD2), jnp.float32) * s, 'w_v_u': jax.random.normal(ks[5], (LAT, H * HD), jnp.float32) * s, 'w_rope_k': jax.random.normal(ks[6], (HID, HID // 2), jnp.float32) * s, 'w_rope_q': jax.random.normal(ks[7], (LAT, HID // 2), jnp.float32) * s, 'w_o': jax.random.normal(ks[8], (HID, HID), jnp.float32) * s}
    _L0_attn_in = _L0_attn_setup()

    def _L0_ffn_setup():
        import jax, jax.numpy as jnp
        import numpy as np
        N_HEAD = 16
        N_EMBD = 256
        R = 8
        HEAD_DIM = N_EMBD // N_HEAD
        D_STD = HEAD_DIM - R
        THRESHOLD = 0.1
        B, T = (4, 128)
        key = jax.random.key(seed)
        k1, k2, k3, k4, k5 = jax.random.split(key, 5)
        fused_dim = 2 * N_HEAD * D_STD + N_EMBD + 2 * N_HEAD * R
        x = jax.random.normal(k1, (B, T, N_EMBD), dtype=jnp.float32)
        Wa = jax.random.normal(k2, (N_EMBD, fused_dim), dtype=jnp.float32) * 0.02
        Wp = jax.random.normal(k3, (N_EMBD, N_EMBD), dtype=jnp.float32) * 0.02
        w_std = jax.random.uniform(k4, (N_HEAD,), dtype=jnp.float32, minval=0.3, maxval=0.7)
        w_rec = jax.random.uniform(k5, (N_HEAD,), dtype=jnp.float32)
        return {'x': x, 'Wa': Wa, 'Wp': Wp, 'w_std': w_std, 'w_rec': w_rec}
    _L0_ffn_in = _L0_ffn_setup()

    def _L1_attn_setup():
        import jax, jax.numpy as jnp
        import numpy as np
        B, S, D = (2, 512, 256)
        H, DK, DV = (16, 128, 128)
        SEG = 64
        UPDATE = 'delta'
        CAUSAL = True
        key = jax.random.key(seed)
        ks = jax.random.split(key, 6)
        s = 0.02
        return {'x': jax.random.normal(ks[0], (B, S, D), jnp.float32), 'Wq': jax.random.normal(ks[1], (D, H * DK), jnp.float32) * s, 'Wk': jax.random.normal(ks[2], (D, H * DK), jnp.float32) * s, 'Wv': jax.random.normal(ks[3], (D, H * DV), jnp.float32) * s, 'Wo': jax.random.normal(ks[4], (H * DV, D), jnp.float32) * s, 'betas': jax.random.normal(ks[5], (1, H, 1, DV), jnp.float32)}
    _L1_attn_in = _L1_attn_setup()

    def _L1_ffn_setup():
        import jax, jax.numpy as jnp
        import numpy as np
        D_MODEL = 256
        NUM_TILES = 64
        D_SLICE = D_MODEL // NUM_TILES
        TILES_PER_CLUSTER = 8
        NUM_CLUSTERS = NUM_TILES // TILES_PER_CLUSTER
        GRID = 16
        LN_EPS = 1e-05
        DIMS = (np.arange(NUM_TILES)[:, None] * D_SLICE + np.arange(D_SLICE)[None, :]) % D_MODEL
        DIMS = jnp.asarray(DIMS, dtype=jnp.int32)

        def _forward(x, ln_gamma, ln_beta, spline_bases, spline_slopes, output_scale):
            B, S, D = x.shape
            N = B * S
            mu = jnp.mean(x, axis=-1, keepdims=True)
            var = jnp.mean(jnp.square(x - mu), axis=-1, keepdims=True)
            xn = (x - mu) * jax.lax.rsqrt(var + LN_EPS) * ln_gamma + ln_beta
            xf = xn.reshape(N, D)
            slope_sign = jnp.sign(jnp.mean(spline_slopes, axis=-1))
            tile_sigs = jnp.zeros((NUM_TILES, D), dtype=x.dtype)
            tile_sigs = tile_sigs.at[jnp.arange(NUM_TILES)[:, None], DIMS].set(slope_sign)
            cluster_sigs = jnp.sign(tile_sigs.reshape(NUM_CLUSTERS, TILES_PER_CLUSTER, D).mean(axis=1))
            cluster_assign = jnp.arange(NUM_TILES, dtype=jnp.int32) // TILES_PER_CLUSTER
            input_sigs = jnp.sign(xf)
            cluster_scores = input_sigs @ cluster_sigs.T
            best_cluster = jnp.argmax(cluster_scores, axis=-1)
            tile_scores = input_sigs @ tile_sigs.T
            in_cluster = cluster_assign[None, :] == best_cluster[:, None]
            tile_idx = jnp.argmax(jnp.where(in_cluster, tile_scores, -jnp.inf), axis=-1)
            tok_dims = DIMS[tile_idx]
            x_slice = jnp.take_along_axis(xf, tok_dims, axis=1)
            tok_min = x_slice.min(axis=1)
            tok_max = x_slice.max(axis=1)
            onehot = tile_idx[None, :] == jnp.arange(NUM_TILES)[:, None]
            tile_min = jnp.where(onehot, tok_min[None, :], jnp.inf).min(axis=1)
            tile_max = jnp.where(onehot, tok_max[None, :], -jnp.inf).max(axis=1)
            mn = tile_min[tile_idx][:, None]
            mx = tile_max[tile_idx][:, None]
            u = jnp.clip((x_slice - mn) / (mx - mn + 1e-08), 0.0, 1.0 - 1e-06)
            gi = jnp.clip((u * GRID).astype(jnp.int32), 0, GRID - 1)
            j = jnp.arange(D_SLICE)[None, :]
            b = spline_bases[tile_idx[:, None], j, gi]
            s = spline_slopes[tile_idx[:, None], j, gi]
            x_local = (u - gi.astype(u.dtype) / GRID) * GRID
            delta = (b + s * x_local) * output_scale[tile_idx][:, None]
            out = jnp.zeros_like(xf).at[jnp.arange(N)[:, None], tok_dims].set(delta)
            return x + out.reshape(B, S, D)
        key = jax.random.key(seed)
        k1, k2, k3, k4, k5, k6 = jax.random.split(key, 6)
        x = jax.random.normal(k1, (4, 512, D_MODEL), dtype=jnp.float32)
        ln_gamma = 1.0 + 0.1 * jax.random.normal(k2, (D_MODEL,), dtype=jnp.float32)
        ln_beta = 0.1 * jax.random.normal(k3, (D_MODEL,), dtype=jnp.float32)
        spline_bases = 0.1 * jax.random.normal(k4, (NUM_TILES, D_SLICE, GRID), dtype=jnp.float32)
        spline_slopes = 0.1 + 0.1 * jax.random.normal(k5, (NUM_TILES, D_SLICE, GRID), dtype=jnp.float32)
        output_scale = 1.0 + 0.1 * jax.random.normal(k6, (NUM_TILES,), dtype=jnp.float32)
        return {'x': x, 'ln_gamma': ln_gamma, 'ln_beta': ln_beta, 'spline_bases': spline_bases, 'spline_slopes': spline_slopes, 'output_scale': output_scale}
    _L1_ffn_in = _L1_ffn_setup()
    _d = {'L0_attn_hidden_states': _L0_attn_in['hidden_states'], 'L0_attn_w_kv_d': _L0_attn_in['w_kv_d'], 'L0_attn_w_q_d': _L0_attn_in['w_q_d'], 'L0_attn_w_k_u': _L0_attn_in['w_k_u'], 'L0_attn_w_q_u': _L0_attn_in['w_q_u'], 'L0_attn_w_v_u': _L0_attn_in['w_v_u'], 'L0_attn_w_rope_k': _L0_attn_in['w_rope_k'], 'L0_attn_w_rope_q': _L0_attn_in['w_rope_q'], 'L0_attn_w_o': _L0_attn_in['w_o'], 'L0_ffn_Wa': _L0_ffn_in['Wa'], 'L0_ffn_Wp': _L0_ffn_in['Wp'], 'L0_ffn_w_std': _L0_ffn_in['w_std'], 'L0_ffn_w_rec': _L0_ffn_in['w_rec'], 'L1_attn_Wq': _L1_attn_in['Wq'], 'L1_attn_Wk': _L1_attn_in['Wk'], 'L1_attn_Wv': _L1_attn_in['Wv'], 'L1_attn_Wo': _L1_attn_in['Wo'], 'L1_attn_betas': _L1_attn_in['betas'], 'L1_ffn_ln_gamma': _L1_ffn_in['ln_gamma'], 'L1_ffn_ln_beta': _L1_ffn_in['ln_beta'], 'L1_ffn_spline_bases': _L1_ffn_in['spline_bases'], 'L1_ffn_spline_slopes': _L1_ffn_in['spline_slopes'], 'L1_ffn_output_scale': _L1_ffn_in['output_scale']}
    _x0 = _d['L0_attn_hidden_states']
    _d['L0_attn_hidden_states'] = jax.random.normal(jax.random.fold_in(jax.random.key(seed), 1), (8, 512, 256), dtype=_x0.dtype)
    del _x0
    return _d

def reference(L0_attn_hidden_states, L0_attn_w_kv_d, L0_attn_w_q_d, L0_attn_w_k_u, L0_attn_w_q_u, L0_attn_w_v_u, L0_attn_w_rope_k, L0_attn_w_rope_q, L0_attn_w_o, L0_ffn_Wa, L0_ffn_Wp, L0_ffn_w_std, L0_ffn_w_rec, L1_attn_Wq, L1_attn_Wk, L1_attn_Wv, L1_attn_Wo, L1_attn_betas, L1_ffn_ln_gamma, L1_ffn_ln_beta, L1_ffn_spline_bases, L1_ffn_spline_slopes, L1_ffn_output_scale):

    def _L0_attn_ref(hidden_states, w_kv_d, w_q_d, w_k_u, w_q_u, w_v_u, w_rope_k, w_rope_q, w_o):
        import jax, jax.numpy as jnp
        import numpy as np
        B, S, HID = (2, 256, 256)
        H = 16
        HD = HID // H
        HD2 = HD // 2
        LAT = HID // 8
        BASE = 10000.0

        def _rotary_table(seq_len):
            inv_freq = 1.0 / BASE ** (jnp.arange(0, HD2, 2, dtype=jnp.float32) / HD2)
            pos = jnp.arange(seq_len, dtype=jnp.float32)
            sincos = pos[:, None] * inv_freq[None, :]
            return jnp.concatenate([jnp.sin(sincos), jnp.cos(sincos)], axis=-1)

        def _apply_rope(x, emb):
            half = HD2 // 2
            x1, x2 = (x[..., :half], x[..., half:])
            sin = emb[None, :, None, :half]
            cos = emb[None, :, None, half:]
            return jnp.concatenate([x1 * cos - x2 * sin, x1 * sin + x2 * cos], axis=-1)
        b, s, _ = hidden_states.shape
        kv_d = hidden_states @ w_kv_d
        q_d = hidden_states @ w_q_d
        k_p = (kv_d @ w_k_u).reshape(b, s, H, HD2)
        q_p = (q_d @ w_q_u).reshape(b, s, H, HD2)
        v = (kv_d @ w_v_u).reshape(b, s, H, HD)
        k_r = (hidden_states @ w_rope_k).reshape(b, s, H, HD2)
        q_r = (q_d @ w_rope_q).reshape(b, s, H, HD2)
        emb = _rotary_table(s)
        k_r = _apply_rope(k_r, emb)
        q_r = _apply_rope(q_r, emb)
        k = jnp.concatenate([k_p, k_r], axis=-1)
        q = jnp.concatenate([q_p, q_r], axis=-1)
        scores = jnp.einsum('bqhd,bkhd->bhqk', q, k) / jnp.sqrt(jnp.float32(HD))
        causal = jnp.tril(jnp.ones((s, s), dtype=bool))
        scores = jnp.where(causal[None, None], scores, jnp.float32(-1000000000.0))
        probs = jax.nn.softmax(scores, axis=-1)
        out = jnp.einsum('bhqk,bkhd->bqhd', probs, v).reshape(b, s, HID)
        return out @ w_o

    def _L0_ffn_ref(x, Wa, Wp, w_std, w_rec):
        import jax, jax.numpy as jnp
        import numpy as np
        N_HEAD = 16
        N_EMBD = 256
        R = 8
        HEAD_DIM = N_EMBD // N_HEAD
        D_STD = HEAD_DIM - R
        THRESHOLD = 0.1
        B, T = (4, 128)
        Bx, Tx, C = x.shape
        H, D, Ds, r = (N_HEAD, HEAD_DIM, D_STD, R)
        s_std = jnp.sqrt(jnp.clip(w_std, 1e-08, None))
        s_rec = jnp.sqrt(jnp.clip(w_rec, 1e-08, None))
        col_scale = jnp.concatenate([jnp.repeat(s_std, Ds), jnp.repeat(s_std, Ds), jnp.ones((C,), dtype=x.dtype), jnp.repeat(s_rec, r), jnp.repeat(s_rec, r)])
        Wb = Wa * col_scale[None, :]
        fused = x @ Wb
        q_std_end = H * Ds
        k_std_end = q_std_end + H * Ds
        v_end = k_std_end + C
        q_low_end = v_end + H * r

        def heads(t, d):
            return t.reshape(Bx, Tx, H, d).transpose(0, 2, 1, 3)
        Q_std = heads(fused[..., :q_std_end], Ds)
        K_std = heads(fused[..., q_std_end:k_std_end], Ds)
        V = heads(fused[..., k_std_end:v_end], D)
        Q_low = heads(fused[..., v_end:q_low_end], r)
        K_low = heads(fused[..., q_low_end:], r)
        use_ra = (w_rec > THRESHOLD)[None, :, None, None]
        q_tail = jnp.where(use_ra, K_low, Q_low)
        k_tail = jnp.where(use_ra, Q_low, K_low)
        Qf = jnp.concatenate([Q_std, q_tail], axis=-1)
        Kf = jnp.concatenate([K_std, k_tail], axis=-1)
        scale = 1.0 / jnp.sqrt(jnp.asarray(D, dtype=x.dtype))
        scores = jnp.einsum('bhtd,bhsd->bhts', Qf, Kf) * scale
        causal = jnp.tril(jnp.ones((Tx, Tx), dtype=bool))
        scores = jnp.where(causal[None, None], scores, jnp.finfo(scores.dtype).min)
        attn = jax.nn.softmax(scores, axis=-1)
        out = jnp.einsum('bhts,bhsd->bhtd', attn, V)
        y = out.transpose(0, 2, 1, 3).reshape(Bx, Tx, C)
        return y @ Wp

    def _L1_attn_ref(x, Wq, Wk, Wv, Wo, betas):
        import jax, jax.numpy as jnp
        import numpy as np
        B, S, D = (2, 512, 256)
        H, DK, DV = (16, 128, 128)
        SEG = 64
        UPDATE = 'delta'
        CAUSAL = True
        Bsz, seq, _ = x.shape
        nseg = seq // SEG
        q = (x @ Wq).reshape(Bsz, seq, H, DK).transpose(0, 2, 1, 3)
        k = (x @ Wk).reshape(Bsz, seq, H, DK).transpose(0, 2, 1, 3)
        v = (x @ Wv).reshape(Bsz, seq, H, DV).transpose(0, 2, 1, 3)
        qs = q.reshape(Bsz, H, nseg, SEG, DK).transpose(2, 0, 1, 3, 4)
        ks_ = k.reshape(Bsz, H, nseg, SEG, DK).transpose(2, 0, 1, 3, 4)
        vs = v.reshape(Bsz, H, nseg, SEG, DV).transpose(2, 0, 1, 3, 4)
        causal_mask = jnp.tril(jnp.ones((SEG, SEG), bool))
        scale = DK ** 0.5
        beta = jax.nn.sigmoid(betas)

        def step(carry, seg):
            mem, z = carry
            qq, kk, vv = seg
            sigma_q = jax.nn.elu(qq) + 1.0
            scores = jnp.einsum('bhsk,bhtk->bhst', qq, kk) / scale
            if CAUSAL:
                scores = jnp.where(causal_mask, scores, -jnp.inf)
            att_dot = jax.nn.softmax(scores, axis=-1) @ vv
            att_mem = sigma_q @ mem / (sigma_q @ z)
            sigma_k = jax.nn.elu(kk) + 1.0
            if UPDATE == 'linear':
                mem_new = mem + jnp.einsum('bhsk,bhsv->bhkv', sigma_k, vv)
            else:
                delta = vv - sigma_k @ mem / (sigma_k @ z)
                mem_new = mem + jnp.einsum('bhsk,bhsv->bhkv', sigma_k, delta)
            z_new = z + sigma_k.sum(axis=-2, keepdims=True).transpose(0, 1, 3, 2)
            att = beta * att_mem + (1.0 - beta) * att_dot
            out = att.reshape(Bsz, SEG, H * DV) @ Wo
            return ((mem_new, z_new), out)
        mem0 = jnp.zeros((Bsz, H, DK, DV), x.dtype)
        z0 = jnp.ones((Bsz, H, DK, 1), x.dtype) / DK
        _, outs = jax.lax.scan(step, (mem0, z0), (qs, ks_, vs))
        return outs.transpose(1, 0, 2, 3).reshape(Bsz, seq, D)

    def _L1_ffn_ref(x, ln_gamma, ln_beta, spline_bases, spline_slopes, output_scale):
        import jax, jax.numpy as jnp
        import numpy as np
        D_MODEL = 256
        NUM_TILES = 64
        D_SLICE = D_MODEL // NUM_TILES
        TILES_PER_CLUSTER = 8
        NUM_CLUSTERS = NUM_TILES // TILES_PER_CLUSTER
        GRID = 16
        LN_EPS = 1e-05
        DIMS = (np.arange(NUM_TILES)[:, None] * D_SLICE + np.arange(D_SLICE)[None, :]) % D_MODEL
        DIMS = jnp.asarray(DIMS, dtype=jnp.int32)

        def _forward(x, ln_gamma, ln_beta, spline_bases, spline_slopes, output_scale):
            B, S, D = x.shape
            N = B * S
            mu = jnp.mean(x, axis=-1, keepdims=True)
            var = jnp.mean(jnp.square(x - mu), axis=-1, keepdims=True)
            xn = (x - mu) * jax.lax.rsqrt(var + LN_EPS) * ln_gamma + ln_beta
            xf = xn.reshape(N, D)
            slope_sign = jnp.sign(jnp.mean(spline_slopes, axis=-1))
            tile_sigs = jnp.zeros((NUM_TILES, D), dtype=x.dtype)
            tile_sigs = tile_sigs.at[jnp.arange(NUM_TILES)[:, None], DIMS].set(slope_sign)
            cluster_sigs = jnp.sign(tile_sigs.reshape(NUM_CLUSTERS, TILES_PER_CLUSTER, D).mean(axis=1))
            cluster_assign = jnp.arange(NUM_TILES, dtype=jnp.int32) // TILES_PER_CLUSTER
            input_sigs = jnp.sign(xf)
            cluster_scores = input_sigs @ cluster_sigs.T
            best_cluster = jnp.argmax(cluster_scores, axis=-1)
            tile_scores = input_sigs @ tile_sigs.T
            in_cluster = cluster_assign[None, :] == best_cluster[:, None]
            tile_idx = jnp.argmax(jnp.where(in_cluster, tile_scores, -jnp.inf), axis=-1)
            tok_dims = DIMS[tile_idx]
            x_slice = jnp.take_along_axis(xf, tok_dims, axis=1)
            tok_min = x_slice.min(axis=1)
            tok_max = x_slice.max(axis=1)
            onehot = tile_idx[None, :] == jnp.arange(NUM_TILES)[:, None]
            tile_min = jnp.where(onehot, tok_min[None, :], jnp.inf).min(axis=1)
            tile_max = jnp.where(onehot, tok_max[None, :], -jnp.inf).max(axis=1)
            mn = tile_min[tile_idx][:, None]
            mx = tile_max[tile_idx][:, None]
            u = jnp.clip((x_slice - mn) / (mx - mn + 1e-08), 0.0, 1.0 - 1e-06)
            gi = jnp.clip((u * GRID).astype(jnp.int32), 0, GRID - 1)
            j = jnp.arange(D_SLICE)[None, :]
            b = spline_bases[tile_idx[:, None], j, gi]
            s = spline_slopes[tile_idx[:, None], j, gi]
            x_local = (u - gi.astype(u.dtype) / GRID) * GRID
            delta = (b + s * x_local) * output_scale[tile_idx][:, None]
            out = jnp.zeros_like(xf).at[jnp.arange(N)[:, None], tok_dims].set(delta)
            return x + out.reshape(B, S, D)
        return _forward(x, ln_gamma, ln_beta, spline_bases, spline_slopes, output_scale)
    x = L0_attn_hidden_states
    xn = _layernorm(x, axis=-1)
    s = _L0_attn_ref(xn, L0_attn_w_kv_d, L0_attn_w_q_d, L0_attn_w_k_u, L0_attn_w_q_u, L0_attn_w_v_u, L0_attn_w_rope_k, L0_attn_w_rope_q, L0_attn_w_o)
    g = _silu(_L0_ffn_ref(xn, L0_ffn_Wa, L0_ffn_Wp, L0_ffn_w_std, L0_ffn_w_rec))
    x = x + s * g
    xn = _layernorm(x, axis=-1)
    s = _L1_attn_ref(xn, L1_attn_Wq, L1_attn_Wk, L1_attn_Wv, L1_attn_Wo, L1_attn_betas)
    g = _silu(_L1_ffn_ref(xn, L1_ffn_ln_gamma, L1_ffn_ln_beta, L1_ffn_spline_bases, L1_ffn_spline_slopes, L1_ffn_output_scale))
    x = x + s * g
    return x

_drawn_inputs = setup_inputs


def setup_inputs(seed=0):
    import zlib

    import numpy as np

    out = dict(_drawn_inputs(seed))
    spreads = {}
    factors = {'L0_attn_w_kv_d': 8.0,
     'L0_attn_w_q_d': 8.0,
     'L0_attn_w_k_u': 8.0,
     'L0_attn_w_q_u': 8.0,
     'L0_attn_w_v_u': 8.0,
     'L0_attn_w_rope_k': 8.0,
     'L0_attn_w_rope_q': 8.0,
     'L0_attn_w_o': 8.0,
     'L0_ffn_Wa': 8.0,
     'L0_ffn_Wp': 8.0,
     'L0_ffn_w_std': 8.0,
     'L0_ffn_w_rec': 8.0,
     'L1_attn_Wq': 49.692,
     'L1_attn_Wk': 49.933,
     'L1_attn_betas': 43.528,
     'L1_ffn_ln_gamma': 64.0,
     'L1_ffn_ln_beta': 62.35,
     'L1_ffn_spline_bases': 64.0,
     'L1_ffn_spline_slopes': 64.0,
     'L1_ffn_output_scale': 64.0,
     'L1_attn_Wv': 5.898,
     'L1_attn_Wo': 5.811}
    for name, (base, spread) in spreads.items():
        noise = np.random.default_rng([zlib.crc32(name.encode()), seed]).standard_normal(out[name].shape)
        drawn = base * np.exp(spread * noise) if base else spread * noise
        out[name] = jnp.asarray(drawn.astype(out[name].dtype))
    for name, factor in factors.items():
        out[name] = (out[name] * factor).astype(out[name].dtype)
    return out
```

```python
import math
from contextlib import ExitStack

import numpy as np

import concourse.bass as bass
from concourse import mybir

F32 = mybir.dt.float32
BF16 = mybir.dt.bfloat16
ALU = mybir.AluOpType
ACT = mybir.ActivationFunctionType
AXX = mybir.AxisListType.X

P = 128
B, S, HID = 8, 512, 256
NBLK = S // P
KC = HID // P
H, HD = 16, 16
HH = HD // 2
LAT = HID // 8
HALF = 8 * HD
NHALF = H // 8
GH = 4
NG = H // GH
NPART = 3
Q_SLOT = (0, 1, 2, 0, 1, 0)
K_SLOT = (0, 0, 0, 1, 1, 2)
STACK = len(Q_SLOT) * HD
MROWS = GH * NPART
EPS = 1e-5
THRESHOLD = 0.1
BIG = 1.0e30
ATTN, FFN = 0, 1

DK = 128
SEG = 64
NSEG = S // SEG
NTILE, SLICE, GRID, PER_CLUSTER = 64, 4, 16, 8
NCLUSTER = NTILE // PER_CLUSTER


def shape_constants(phase):
    cols = {}
    parts = []

    def put(name, a):
        at = sum(x.shape[1] for x in parts)
        parts.append(a.astype(np.float32))
        cols[name] = (at, at + a.shape[1])

    r = np.arange(P)
    put("ident", np.eye(P))
    if phase == 1:
        seg = r // SEG
        ok = (seg[:, None] == seg[None, :]) & (r[None, :] <= r[:, None])
        put("mask_seg", np.where(ok, 0.0, -BIG))
        return np.concatenate(parts, axis=1), cols
    if phase == 2:
        put("grid", np.tile(np.arange(GRID), (P, SLICE)))
        put("cluster", np.tile(np.arange(NCLUSTER), (P, NBLK)))
        put("in_cluster", np.tile(np.arange(PER_CLUSTER), (P, NBLK * NCLUSTER)))
        return np.concatenate(parts, axis=1), cols
    half = HH // 2
    inv_freq = (1.0 / 10000.0 ** (np.arange(0, HH, 2, dtype=np.float32) / HH)).astype(np.float32)
    angle = (np.arange(S, dtype=np.float32)[:, None] * inv_freq[None, :]).astype(np.float32)
    sin, cos = np.sin(angle).T, np.cos(angle).T
    c, s = np.zeros((HD, S)), np.zeros((HD, S))
    c[:HH] = 1.0
    c[HH:HH + half] = cos
    c[HH + half:] = cos
    s[HH:HH + half] = -sin
    s[HH + half:] = sin
    put("rope_c", np.tile(c, (8, 1)))
    put("rope_s", np.tile(s, (8, 1)))
    put("mask_qk", np.where(r[None, :] > r[:, None], -BIG, 0.0))
    put("mask_kq", np.where(r[None, :] < r[:, None], -BIG, 0.0))
    one = np.zeros((P, GH))
    for h in range(GH):
        one[STACK + h * NPART:STACK + (h + 1) * NPART, h] = 1.0
    put("own_max", one)
    return np.concatenate(parts, axis=1), cols


def meet(eng, turn, n, arrive, seen, leave, mine=()):
    eng.drain().then_inc(arrive, 1)
    eng.wait_ge(arrive, (turn + 1) * n)
    eng.sem_inc(seen, 1)
    for s in mine:
        eng.sem_clear(s)
    eng.sem_inc(leave, 1)
    eng.wait_ge(leave, (turn + 1) * n)
    eng.sem_inc(seen, 1)


def wait_apart(eng, sem, value, seen):
    eng.wait_ge(sem, value)
    eng.sem_inc(seen, 1)


class Scope:

    def __init__(self, nc, ctx):
        self.nc, self.ctx = nc, ctx

    def sb(self, name, shape, dt=F32):
        return self.ctx.enter_context(self.nc.sbuf_tensor(name, shape, dt))

    def sem(self, name):
        return self.ctx.enter_context(self.nc.semaphore(name))


class Chain:

    def __init__(self, eng, sem):
        self.eng, self.sem, self.n = eng, sem, 0

    def __call__(self, ins):
        self.n += 1
        ins.then_inc(self.sem, 1)
        self.eng.wait_ge(self.sem, self.n)


def spread(ap, shape):
    return ap.broadcast_to(shape)


def load_layer0(nc, sc, w, cst, col, A):
    with ExitStack() as ctx:
        t = Scope(nc, ctx)
        wqu = t.sb("wqu", [LAT, P])
        wrq = t.sb("wrq", [LAT, P])
        wku = t.sb("wku", [2 * LAT, P])
        wrk = t.sb("wrk", [P, KC, P])
        wa = t.sb("wa", [P, KC, 768])
        hs = t.sb("head_scales", [P, 8, H])
        hs2 = t.sb("kept_low", [P, H, HH])
        loaded = t.sem("l0_loaded")
        cleared = t.sem("l0_cleared")
        clamped = t.sem("l0_clamped")
        rooted = t.sem("l0_rooted")
        step = t.sem("l0_step")
        N_DMA = 13
        block = ctx.enter_context(nc.Block())

        @block.sync
        def _(sp):
            for dst, src in (
                (cst[:, :], A["consts0"]),
                (w["d"][:, :, 0:LAT], A["w_q_d"].rearrange("(k p) n -> p k n", p=P)),
                (w["d"][:, :, LAT:2 * LAT], A["w_kv_d"].rearrange("(k p) n -> p k n", p=P)),
                (wqu[:, :], A["w_q_u"]),
                (wrq[:, :], A["w_rope_q"]),
                (wku[LAT:2 * LAT, :], A["w_k_u"]),
                (w["v_a"][LAT:2 * LAT, :], A["w_v_u"]),
                (wrk[:, :, :], A["w_rope_k"].rearrange("(k p) n -> p k n", p=P)),
                (wa[:, :, :], A["Wa"].rearrange("(k p) n -> p k n", p=P)),
                (w["o_a"][:, :, :], A["w_o"].rearrange("(k p) n -> p k n", p=P)),
                (w["o_f"][:, :, :], A["Wp"].rearrange("(k p) n -> p k n", p=P)),
                (hs[:, 0, :], A["w_std"].unsqueeze(0).broadcast_to([P, H])),
                (hs[:, 1, :], A["w_rec"].unsqueeze(0).broadcast_to([P, H])),
            ):
                sp.dma_start(dst, src).then_inc(loaded, 16)

        @block.gpsimd
        def _(pool):
            nc.gpsimd.memset(hs[:, 7, :], 0.5).then_inc(cleared, 1)
            pool.wait_ge(cleared, 1)
            pool.wait_ge(clamped, 2)
            nc.gpsimd.tensor_tensor(hs[:, 2, :], hs[:, 2, :], hs[:, 7, :], ALU.pow).then_inc(rooted, 1)
            nc.gpsimd.tensor_tensor(hs[:, 3, :], hs[:, 3, :], hs[:, 7, :], ALU.pow).then_inc(rooted, 1)

        @block.vector
        def _(dve):
            link = Chain(dve, step)
            for name in ("q_a", "q_b", "k_a", "kr_a", "kr_b"):
                nc.vector.memset(w[name][:], 0.0)
            dve.wait_ge(loaded, 16 * N_DMA)
            nc.vector.tensor_scalar(hs[:, 2, :], hs[:, 0, :], 1e-8, None, ALU.max).then_inc(clamped, 1)
            nc.vector.tensor_scalar(hs[:, 3, :], hs[:, 1, :], 1e-8, None, ALU.max).then_inc(clamped, 1)
            link(nc.vector.tensor_copy(w["ident_b"][:, :], cst[:, slice(*col["ident"])]))
            nc.vector.tensor_copy(w["mask_qk"][:, :], cst[:, slice(*col["mask_qk"])])
            nc.vector.tensor_copy(w["mask_kq"][:, :], cst[:, slice(*col["mask_kq"])])

            def heads(ap):
                return ap.rearrange("p (h c) -> p h c", h=H)

            half = HH // 2
            for plain, rope, dst_a, dst_b, lo, hi in (
                (wqu, wrq, w["q_a"], w["q_b"], 0, LAT),
                (wku, None, w["k_a"], None, LAT, 2 * LAT),
            ):
                nc.vector.tensor_copy(heads(dst_a[lo:hi, :])[:, :, 0:HH], heads(plain[lo:hi, :]))
                if rope is not None:
                    nc.vector.tensor_copy(heads(dst_a[lo:hi, :])[:, :, HH:HD], heads(rope[lo:hi, :]))
                    nc.vector.tensor_copy(heads(dst_b[lo:hi, :])[:, :, HH:HH + half], heads(rope[lo:hi, :])[:, :, half:HH])
                    nc.vector.tensor_copy(heads(dst_b[lo:hi, :])[:, :, HH + half:HD], heads(rope[lo:hi, :])[:, :, 0:half])
            for k in range(KC):
                src = heads(wrk[:, k, :])
                nc.vector.tensor_copy(heads(w["kr_a"][:, k, :])[:, :, HH:HD], src)
                nc.vector.tensor_copy(heads(w["kr_b"][:, k, :])[:, :, HH:HH + half], src[:, :, half:HH])
                nc.vector.tensor_copy(heads(w["kr_b"][:, k, :])[:, :, HH + half:HD], src[:, :, 0:half])
                nc.vector.tensor_copy(w["v_f"][:, k, :], wa[:, k, 2 * P:2 * P + HID])
            dve.wait_ge(rooted, 2)
            link(nc.vector.tensor_scalar(hs[:, 4, :], hs[:, 1, :], THRESHOLD, None, ALU.is_gt))
            link(nc.vector.tensor_scalar(hs[:, 5, :], hs[:, 4, :], -1.0, 1.0, ALU.mult, ALU.add))
            link(nc.vector.tensor_tensor(hs[:, 4, :], hs[:, 4, :], hs[:, 3, :], ALU.mult))
            link(nc.vector.tensor_tensor(hs[:, 5, :], hs[:, 5, :], hs[:, 3, :], ALU.mult))
            std, swap, keep = (spread(hs[:, n, :].unsqueeze(2), [P, H, HH]) for n in (2, 4, 5))
            for k in range(KC):
                q_std, k_std, q_low, k_low = (heads(wa[:, k, at:at + P]) for at in (0, P, 2 * P + HID, 3 * P + HID))
                q_out, k_out = heads(w["q_f"][:, k, :]), heads(w["k_f"][:, k, :])
                link(nc.vector.tensor_tensor(q_out[:, :, 0:HH], q_std, std, ALU.mult))
                link(nc.vector.tensor_tensor(k_out[:, :, 0:HH], k_std, std, ALU.mult))
                for out, swapped, kept in ((q_out, k_low, q_low), (k_out, q_low, k_low)):
                    link(nc.vector.tensor_tensor(out[:, :, HH:HD], swapped, swap, ALU.mult))
                    link(nc.vector.tensor_tensor(hs2[:, :, :], kept, keep, ALU.mult))
                    link(nc.vector.tensor_tensor(out[:, :, HH:HD], out[:, :, HH:HD], hs2[:, :, :], ALU.add))


def project_layer0(nc, ps, w, cst, col, A, parts_dram, v_dram):
    with ExitStack() as ctx:
        t = Scope(nc, ctx)
        x = t.sb("p_x", [P, NBLK, HID])
        xn = t.sb("p_xn", [P, NBLK, HID])
        stats = t.sb("p_stats", [P, NBLK, 6])
        mv = t.sb("p_mv", [P, NBLK, 2])
        rstd = t.sb("p_rstd", [P, NBLK])
        power = t.sb("p_power", [P, NBLK])
        xT = t.sb("p_xT", [P, KC, S])
        dT = t.sb("p_dT", [2 * LAT, S])
        rc = t.sb("p_rc", [P, NHALF, S])
        rs = t.sb("p_rs", [P, NHALF, S])
        full = [t.sb(f"p_full{n}", [P, NHALF, S]) for n in range(4)]
        rest = [t.sb(f"p_rest{n}", [P, NHALF, S]) for n in range(4)]
        part = [t.sb(f"p_part{n}", [P, NPART, NHALF, S], BF16) for n in range(4)]
        va = [t.sb(f"p_v{n}", [P, NG, NBLK, GH, HD + 1]) for n in range(2)]

        x_in = t.sem("x_in")
        var_ready, rstd_ready = t.sem("var_ready"), t.sem("rstd_ready")
        xn_ready, xt_psum, xt_ready = t.sem("xn_ready"), t.sem("xt_psum"), t.sem("xt_ready")
        d_psum, d_ready = t.sem("d_psum"), t.sem("d_ready")
        ffn_psum, ffn_full = t.sem("ffn_psum"), t.sem("ffn_full")
        rope_psum, rope_terms, rope_full = t.sem("rope_psum"), t.sem("rope_terms"), t.sem("rope_full")
        v_psum, v_ready = t.sem("v_psum"), t.sem("v_ready")
        hi_ready, rest_ready, mid_ready, lo_ready = (t.sem(f"part_{n}") for n in ("hi", "rest", "mid", "lo"))
        stored = t.sem("parts_stored")
        dve_step, pool_step, preset = t.sem("p_dve_step"), t.sem("p_pool_step"), t.sem("p_preset")
        arrive, seen, leave = t.sem("p_arrive"), t.sem("p_seen"), t.sem("p_leave")
        N_ENG = 5
        N_STORE = 4 * NPART * NHALF + 2
        ORDER = (2, 3, 0, 1)
        block = ctx.enter_context(nc.Block())

        @block.sync
        def _(sp):
            with sp.Fori(0, B) as b:
                sp.dma_start(x[:, :, :], tokens(A["x"], b)).then_inc(x_in, 16)
                for n, tensor in enumerate(ORDER):
                    for m in range(NPART):
                        sp.wait_ge((hi_ready, mid_ready, lo_ready)[m], n + 1)
                        for f in range(NHALF):
                            rows = parts_dram[tensor][m, :, bass.ds(b * H + f * 8, 8), :]
                            sp.dma_start(rows.rearrange("d h n -> h d n"), part[tensor][:, m, f, :]).then_inc(stored, 16)
                for kind in (ATTN, FFN):
                    sp.wait_ge(v_ready, 2 * (kind + 1))
                    sp.dma_start(v_dram[kind][bass.ds(b * NG, NG), :, :].rearrange("g p n -> p g n"),
                                 va[kind][:, :, :, :, :].rearrange("p g k h c -> p g (k h c)")).then_inc(stored, 16)
                sp.wait_ge(stored, 16 * N_STORE)
                meet(sp, b, N_ENG, arrive, seen, leave, (x_in, stored))

        @block.gpsimd
        def _(pool):
            nc.gpsimd.memset(power[:, :], -0.5).then_inc(preset, 1)
            nc.gpsimd.memset(va[0][:], 1.0)
            nc.gpsimd.memset(va[1][:], 1.0).then_inc(preset, 1)
            pool.wait_ge(preset, 2)
            with pool.Fori(0, B) as b:
                pool.wait_ge(var_ready, 1)
                nc.gpsimd.tensor_scalar(rstd[:, :], mv[:, :, 1], EPS, None, ALU.add).then_inc(pool_step, 1)
                pool.wait_ge(pool_step, 1)
                nc.gpsimd.tensor_tensor(rstd[:, :], rstd[:, :], power[:, :], ALU.pow).then_inc(rstd_ready, 1)
                for n, tensor in enumerate(ORDER):
                    if tensor < 2:
                        pool.wait_ge(rope_terms, tensor + 1)
                        nc.gpsimd.tensor_tensor(full[tensor][:, :, :], rc[:, :, :], rs[:, :, :], ALU.add).then_inc(rope_full, 1)
                    pool.wait_ge(hi_ready, n + 1)
                    nc.gpsimd.tensor_tensor(rest[tensor][:, :, :], full[tensor][:, :, :], part[tensor][:, 0, :, :], ALU.subtract).then_inc(rest_ready, 1)
                    pool.wait_ge(mid_ready, n + 1)
                    nc.gpsimd.tensor_tensor(part[tensor][:, 2, :, :], rest[tensor][:, :, :], part[tensor][:, 1, :, :], ALU.subtract).then_inc(lo_ready, 1)
                meet(pool, b, N_ENG, arrive, seen, leave, (rstd_ready, pool_step, rope_full, rest_ready, lo_ready))

        @block.scalar
        def _(act):
            act.wait_ge(preset, 2)
            with act.Fori(0, B) as b:
                act.wait_ge(xt_psum, 1)
                nc.scalar.activation(xT[:, :, :], ps[:, 0:2, :], ACT.Copy).then_inc(xt_ready, 1)
                act.wait_ge(d_psum, 1)
                nc.scalar.activation(dT[:, :], ps[0:2 * LAT, 2, :], ACT.Copy).then_inc(d_ready, 1)
                for n, tensor in enumerate(ORDER):
                    if tensor >= 2:
                        act.wait_ge(ffn_psum, n + 1)
                        at = 4 + 2 * n
                        nc.scalar.activation(full[tensor][:, :, :], ps[:, at:at + 2, :], ACT.Copy).then_inc(ffn_full, 1)
                        act.wait_ge(ffn_full, n + 1)
                    else:
                        act.wait_ge(rope_full, tensor + 1)
                    nc.scalar.activation(part[tensor][:, 0, :, :], full[tensor][:, :, :], ACT.Copy).then_inc(hi_ready, 1)
                    act.wait_ge(rest_ready, n + 1)
                    nc.scalar.activation(part[tensor][:, 1, :, :], rest[tensor][:, :, :], ACT.Copy).then_inc(mid_ready, 1)
                for kind in (ATTN, FFN):
                    for j in range(2):
                        act.wait_ge(v_psum, 2 * kind + j + 1)
                        for i in range(2):
                            k = 2 * j + i
                            last = nc.scalar.activation(
                                va[kind][:, :, k, :, 0:HD],
                                ps[:, 2 * kind + j, i * HID:(i + 1) * HID].rearrange("p (g h c) -> p g h c", g=NG, h=GH), ACT.Copy)
                        last.then_inc(v_ready, 1)
                meet(act, b, N_ENG, arrive, seen, leave, (xt_ready, d_ready, ffn_full, hi_ready, mid_ready, v_ready))

        @block.vector
        def _(dve):
            with dve.Fori(0, B) as b:
                link = Chain(dve, dve_step)
                dve.wait_ge(x_in, 16)
                for k in range(NBLK):
                    last = nc.vector.bn_stats(stats[:, k, :], x[:, k, :])
                link(last)
                for k in range(NBLK):
                    last = nc.vector.bn_aggr(mv[:, k, :], stats[:, k, :])
                last.then_inc(var_ready, 1)
                dve.wait_ge(var_ready, 1)
                dve.wait_ge(rstd_ready, 1)
                for k in range(NBLK):
                    last = nc.vector.tensor_scalar(xn[:, k, :], x[:, k, :], mv[:, k, 0:1], rstd[:, k:k + 1], ALU.subtract, ALU.mult)
                last.then_inc(xn_ready, 1)
                for n in range(2):
                    at = 4 * n
                    dve.wait_ge(rope_psum, n + 1)
                    if n:
                        dve.wait_ge(rope_full, 1)
                    for f in range(NHALF):
                        nc.vector.tensor_tensor(rc[:, f, :], ps[:, at + f, :], cst[:, slice(*col["rope_c"])], ALU.mult)
                        last = nc.vector.tensor_tensor(rs[:, f, :], ps[:, at + 2 + f, :], cst[:, slice(*col["rope_s"])], ALU.mult)
                    last.then_inc(rope_terms, 1)
                meet(dve, b, N_ENG, arrive, seen, leave, (dve_step, var_ready, xn_ready, rope_terms))

        @block.tensor
        def _(pe):
            ident = cst[:, slice(*col["ident"])]

            def product(out, pairs):
                for n, (lhsT, rhs) in enumerate(pairs):
                    last = nc.tensor.matmul(out, lhsT, rhs, start=(n == 0), stop=(n == len(pairs) - 1))
                return last

            with pe.Fori(0, B) as b:
                pe.wait_ge(xn_ready, 1)
                for c in range(KC):
                    for k in range(NBLK):
                        last = nc.tensor.transpose(ps[:, c, k * P:(k + 1) * P], xn[:, k, c * P:(c + 1) * P], ident)
                last.then_inc(xt_psum, 1)
                pe.wait_ge(xt_ready, 1)
                product(ps[0:2 * LAT, 2, :], [(w["d"][:, c, :], xT[:, c, :]) for c in range(KC)]).then_inc(d_psum, 1)
                for n, name in enumerate(("q_f", "k_f")):
                    for f in range(NHALF):
                        last = product(ps[:, 4 + 2 * n + f, :],
                                       [(w[name][:, c, f * P:(f + 1) * P], xT[:, c, :]) for c in range(KC)])
                    last.then_inc(ffn_psum, 1)
                pe.wait_ge(d_ready, 1)
                for f in range(NHALF):
                    cols = slice(f * P, (f + 1) * P)
                    product(ps[:, f, :], [(w["q_a"][:, cols], dT[0:LAT, :])])
                    last = product(ps[:, 2 + f, :], [(w["q_b"][:, cols], dT[0:LAT, :])])
                last.then_inc(rope_psum, 1)
                pe.wait_ge(ffn_full, 2)
                for f in range(NHALF):
                    cols = slice(f * P, (f + 1) * P)
                    rope = [(w["kr_a"][:, c, cols], xT[:, c, :]) for c in range(KC)]
                    product(ps[:, 4 + f, :], [(w["k_a"][LAT:2 * LAT, cols], dT[LAT:2 * LAT, :])] + rope)
                    last = product(ps[:, 6 + f, :], [(w["kr_b"][:, c, cols], xT[:, c, :]) for c in range(KC)])
                last.then_inc(rope_psum, 1)
                pe.wait_ge(rope_terms, 1)
                for kind in (ATTN, FFN):
                    for k in range(NBLK):
                        blk = slice(k * P, (k + 1) * P)
                        if kind == ATTN:
                            pairs = [(dT[LAT:2 * LAT, blk], w["v_a"][LAT:2 * LAT, :])]
                        else:
                            pairs = [(xT[:, c, blk], w["v_f"][:, c, :]) for c in range(KC)]
                        last = product(ps[:, 2 * kind + k // 2, (k % 2) * HID:(k % 2 + 1) * HID], pairs)
                        if k % 2:
                            last.then_inc(v_psum, 1)
                meet(pe, b, N_ENG, arrive, seen, leave, (xt_psum, d_psum, ffn_psum, rope_psum, v_psum))


def attend_layer0(nc, ps, w, cst, col, parts_dram, v_dram, o_all):
    NSLOT = 4
    TURNS = B * NG * 2 // NSLOT
    N_S = NBLK * GH
    N_E = NBLK * GH // 2
    START = [sum(S - j * P for j in range(k)) for k in range(NBLK + 1)]
    with ExitStack() as ctx:
        t = Scope(nc, ctx)
        qs = [t.sb(f"a_q{n}", [P, GH, S], BF16) for n in range(NSLOT)]
        ks = [t.sb(f"a_k{n}", [P, GH, S], BF16) for n in range(NSLOT)]
        vs = [t.sb(f"a_v{n}", [P, NBLK, GH, HD + 1]) for n in range(NSLOT)]
        pt = t.sb("a_p", [P, GH, START[NBLK]])
        negm = t.sb("a_negm", [P, N_S])
        mrest = t.sb("a_mrest", [P, N_S])
        mp = t.sb("a_mp", [P, N_S, NPART], BF16)
        rden = t.sb("a_rden", [P, N_S])
        loaded = [t.sem(f"a_loaded{n}") for n in range(NSLOT)]
        preset = t.sem("a_preset")
        s_ready, s_taken = t.sem("score_ready"), t.sem("score_taken")
        m_split, mt_ready, m_placed = t.sem("max_split"), t.sem("max_turned"), t.sem("max_placed")
        st_ready, exp_done = t.sem("turned_score_ready"), t.sem("prob_ready")
        pv_ready, o_taken = t.sem("out_ready"), t.sem("out_taken")
        m_step, m_rden = t.sem("max_step"), t.sem("out_sums_inverted")
        block = ctx.enter_context(nc.Block())

        def upto(turn, r, per, c):
            return turn * (NSLOT * per) + (r * per + c)

        def placed(turn, r):
            return turn * (NSLOT // 2) + r // 2

        def mt(lo, hi):
            return ps[STACK:STACK + MROWS, 7, lo // 2:hi // 2].bitcast(BF16)

        @block.sync
        def _(sp):
            def load(turn, r):
                at, slot = placed(turn, r), r % NSLOT
                q, k = parts_dram[2 * (r % 2)], parts_dram[2 * (r % 2) + 1]
                heads = bass.ds(at * GH, GH)
                row = 0
                for m in (NPART, NPART - 1, NPART - 2):
                    sp.dma_start(qs[slot][row:row + m * HD, :, :],
                                 q[0:m, :, heads, :].rearrange("a d h n -> (a d) h n")).then_inc(loaded[slot], 16)
                    one = NPART - m
                    sp.dma_start(ks[slot][row:row + m * HD, :, :].rearrange("p h n -> p (h n)"),
                                 k[one:one + 1, :, heads, :].rearrange("a d h n -> a d (h n)").broadcast_to([m, HD, GH * S])).then_inc(loaded[slot], 16)
                    row += m * HD
                sp.dma_start(vs[slot][:, :, :, :].rearrange("p k h c -> p (k h c)"),
                             v_dram[r % 2][bass.ds(at, 1), :, :].rearrange("a p n -> (a p) n")).then_inc(loaded[slot], 16)

            for r in range(NSLOT):
                load(0, r)
            with sp.Fori(0, TURNS - 1) as turn:
                for r in range(NSLOT):
                    sp.wait_ge(pv_ready, upto(turn, r, 1, 1))
                    load(turn, r + NSLOT)

        @block.tensor
        def _(pe):
            pe.wait_ge(preset, 1)

            def score(turn, r, c):
                slot, k, h = r % NSLOT, c // GH, c % GH
                if c == 0:
                    pe.wait_ge(loaded[slot], (turn + r // NSLOT) * (16 * 7) + 16 * 7)
                if not (isinstance(turn, int) and turn == 0 and r == 0 and c < 2):
                    pe.wait_ge(s_taken, upto(turn, r, N_S, c - 1))
                bank = 4 + c % 2
                nc.tensor.matmul(ps[:, bank, 0:(k + 1) * P], qs[slot][0:STACK, h, k * P:(k + 1) * P],
                                 ks[slot][0:STACK, h, 0:(k + 1) * P], start=True, stop=False)
                nc.tensor.matmul(ps[:, bank, k * P:(k + 1) * P], w["ident_b"][:, :], w["mask_qk"][:, :],
                                 start=False, stop=True).then_inc(s_ready, 1)

            def turn_max(turn, r):
                pe.wait_ge(m_split, upto(turn, r, 1, 1))
                for k in range(NBLK):
                    last = nc.tensor.transpose(mt(k * P, (k + 1) * P), mp[:, k * GH:(k + 1) * GH, :].rearrange("p h m -> p (h m)"),
                                               w["ident_b"][:, :])
                last.then_inc(mt_ready, 1)

            def turned_score(turn, r, c):
                slot, k, pair = r % NSLOT, c // 2, c % 2
                if c == 0:
                    pe.wait_ge(m_placed, upto(turn, r, 1, 1))
                if c >= 2:
                    pe.wait_ge(exp_done, upto(turn, r, N_E, c - 1))
                for j in range(2):
                    h, bank = 2 * pair + j, 2 * (c % 2) + j
                    nc.tensor.matmul(ps[:, bank, 0:S - k * P], ks[slot][0:STACK + MROWS, h, k * P:(k + 1) * P],
                                     qs[slot][0:STACK + MROWS, h, k * P:S], start=True, stop=False)
                    last = nc.tensor.matmul(ps[:, bank, 0:P], w["ident_b"][:, :], w["mask_kq"][:, :], start=False, stop=True)
                last.then_inc(st_ready, 1)

            def values(turn, r):
                slot = r % NSLOT
                for q in range(NBLK):
                    pe.wait_ge(exp_done, upto(turn, r, N_E, 2 * (q + 1)))
                    for h in range(GH):
                        at = (q * GH + h) * (HD + 1)
                        for k in range(q + 1):
                            col0 = START[k] + (q - k) * P
                            last = nc.tensor.matmul(ps[:, 6, at:at + HD + 1], pt[:, h, col0:col0 + P], vs[slot][:, k, h, :],
                                                    start=(k == 0), stop=(k == q))
                last.then_inc(pv_ready, 1)

            def unit(turn, r, last=False):
                for c in range(N_E):
                    turned_score(turn, r, c)
                    if not last:
                        score(turn, r + 1, 2 * c)
                        score(turn, r + 1, 2 * c + 1)
                if last:
                    pe.wait_ge(o_taken, upto(turn, r, 1, 0))
                values(turn, r)
                if not last:
                    turn_max(turn, r + 1)

            for c in range(N_S):
                score(0, 0, c)
            turn_max(0, 0)
            with pe.Fori(0, TURNS - 1) as turn:
                for r in range(NSLOT):
                    unit(turn, r)
            for r in range(NSLOT):
                unit(TURNS - 1, r, last=(r == NSLOT - 1))

        @block.scalar
        def _(act):
            def place_max(turn, r):
                act.wait_ge(mt_ready, upto(turn, r, 1, 1))
                nc.scalar.activation(qs[r % NSLOT][STACK:STACK + MROWS, :, :],
                                     mt(0, S).unsqueeze(1).broadcast_to([MROWS, GH, S]), ACT.Copy).then_inc(m_placed, 1)

            def unit(turn, r, last=False):
                for c in range(N_E):
                    k, pair = c // 2, c % 2
                    act.wait_ge(st_ready, upto(turn, r, N_E, c + 1))
                    bank = 2 * (c % 2)
                    nc.scalar.activation(pt[:, 2 * pair:2 * pair + 2, START[k]:START[k + 1]],
                                         ps[:, bank:bank + 2, 0:S - k * P], ACT.Exp, scale=float(HD) ** -0.5).then_inc(exp_done, 1)
                if not last:
                    place_max(turn, r + 1)

            place_max(0, 0)
            with act.Fori(0, TURNS - 1) as turn:
                for r in range(NSLOT):
                    unit(turn, r)
            for r in range(NSLOT):
                unit(TURNS - 1, r, last=(r == NSLOT - 1))

        @block.vector
        def _(dve):
            for n in range(NSLOT):
                last = nc.vector.tensor_copy(
                    ks[n][STACK:STACK + MROWS, :, :],
                    cst[STACK:STACK + MROWS, slice(*col["own_max"])].unsqueeze(2).broadcast_to([MROWS, GH, S]))
            last.then_inc(preset, 1)

            def maxima(turn, r):
                for c in range(N_S):
                    k = c // GH
                    dve.wait_ge(s_ready, upto(turn, r, N_S, c + 1))
                    nc.vector.tensor_reduce(negm[:, c:c + 1], ps[:, 4 + c % 2, 0:(k + 1) * P], AXX, ALU.max, negate=True).then_inc(s_taken, 1)
                dve.wait_ge(s_taken, upto(turn, r, N_S, N_S))
                nc.vector.tensor_copy(mp[:, :, 0], negm[:, :]).then_inc(m_step, 1)
                dve.wait_ge(m_step, upto(turn, r, 3, 1))
                nc.vector.tensor_tensor(mrest[:, :], negm[:, :], mp[:, :, 0], ALU.subtract).then_inc(m_step, 1)
                dve.wait_ge(m_step, upto(turn, r, 3, 2))
                nc.vector.tensor_copy(mp[:, :, 1], mrest[:, :]).then_inc(m_step, 1)
                dve.wait_ge(m_step, upto(turn, r, 3, 3))
                nc.vector.tensor_tensor(mp[:, :, 2], mrest[:, :], mp[:, :, 1], ALU.subtract).then_inc(m_split, 1)

            def take_out(turn, r):
                dve.wait_ge(pv_ready, upto(turn, r, 1, 1))
                got = ps[:, 6, 0:N_S * (HD + 1)].rearrange("p (n c) -> p n c", c=HD + 1)
                nc.vector.reciprocal(rden[:, :], got[:, :, HD]).then_inc(m_rden, 1)
                dve.wait_ge(m_rden, upto(turn, r, 1, 1))
                nc.vector.tensor_tensor(
                    o_all[:, bass.ds(placed(turn, r), 1), r % 2, :].rearrange("p a (n c) -> p (a n) c", c=HD),
                    got[:, :, 0:HD], rden[:, :].unsqueeze(2).broadcast_to([P, N_S, HD]), ALU.mult).then_inc(o_taken, 1)

            maxima(0, 0)
            with dve.Fori(0, TURNS - 1) as turn:
                for r in range(NSLOT):
                    maxima(turn, r + 1)
                    take_out(turn, r)
            for r in range(NSLOT):
                if r < NSLOT - 1:
                    maxima(TURNS - 1, r + 1)
                take_out(TURNS - 1, r)


def tokens(ap, b):
    return ap[bass.ds(b, 1), :, :].rearrange("a (k p) c -> p (a k) c", p=P)


def gate_layer0(nc, ps, w, cst, col, A, o_all, x1_dram):
    with ExitStack() as ctx:
        t = Scope(nc, ctx)
        x = t.sb("g_x", [P, NBLK, HID])
        oc = [t.sb(f"g_oc{n}", [P, NBLK, NG, GH * HD]) for n in range(2)]
        oT = [t.sb(f"g_oT{n}", [P, KC, S]) for n in range(2)]
        e = t.sb("g_e", [P, 2 * S])
        r = t.sb("g_r", [P, 2 * S])
        g = t.sb("g_g", [P, 2 * S])
        x1 = t.sb("g_x1", [P, NBLK, HID])
        x1_ready, x1_out = t.sem("g_x1_ready"), t.sem("g_x1_out")
        x_in, copied, turned, turned_sb, projected = (t.sem("g_" + n) for n in ("x_in", "copied", "turned", "turned_sb", "projected"))
        clipped, exped, step = t.sem("g_clipped"), t.sem("g_exped"), t.sem("g_step")
        arrive, seen, leave = t.sem("g_arrive"), t.sem("g_seen"), t.sem("g_leave")
        N_ENG = 5
        block = ctx.enter_context(nc.Block())

        @block.sync
        def _(sp):
            with sp.Fori(0, B) as b:
                sp.dma_start(x[:, :, :], tokens(A["x"], b)).then_inc(x_in, 16)
                sp.wait_ge(x1_ready, 1)
                sp.dma_start(tokens(x1_dram, b), x1[:, :, :]).then_inc(x1_out, 16)
                sp.wait_ge(x1_out, 16)
                meet(sp, b, N_ENG, arrive, seen, leave, (x1_ready, x1_out))

        @block.gpsimd
        def _(pool):
            with pool.Fori(0, B) as b:
                for kind in (ATTN, FFN):
                    nc.gpsimd.tensor_copy(oc[kind][:, :, :, :].rearrange("p k g c -> p g k c"),
                                          o_all[:, bass.ds(b * NG, NG), kind, :].rearrange("p g (k c) -> p g k c", k=NBLK)).then_inc(copied, 1)
                meet(pool, b, N_ENG, arrive, seen, leave, (copied,))

        @block.tensor
        def _(pe):
            ident = cst[:, slice(*col["ident"])]
            with pe.Fori(0, B) as b:
                for kind in (ATTN, FFN):
                    pe.wait_ge(copied, kind + 1)
                    for c in range(KC):
                        for k in range(NBLK):
                            last = nc.tensor.transpose(ps[:, 2 * kind + c, k * P:(k + 1) * P],
                                                       oc[kind][:, k, 2 * c:2 * c + 2, :].rearrange("p g c -> p (g c)"), ident)
                    last.then_inc(turned, 1)
                for kind in (ATTN, FFN):
                    pe.wait_ge(turned_sb, kind + 1)
                    wo = w["o_a"] if kind == ATTN else w["o_f"]
                    for k in range(NBLK):
                        for c in range(KC):
                            last = nc.tensor.matmul(ps[:, 4 + 2 * kind + k // 2, (k % 2) * HID:(k % 2 + 1) * HID],
                                                    oT[kind][:, c, k * P:(k + 1) * P], wo[:, c, :], start=(c == 0), stop=(c == KC - 1))
                    last.then_inc(projected, 1)
                meet(pe, b, N_ENG, arrive, seen, leave, (turned, projected))

        @block.scalar
        def _(act):
            with act.Fori(0, B) as b:
                for kind in (ATTN, FFN):
                    act.wait_ge(turned, kind + 1)
                    nc.scalar.activation(oT[kind][:, :, :], ps[:, 2 * kind:2 * kind + 2, :], ACT.Copy).then_inc(turned_sb, 1)
                act.wait_ge(clipped, 1)
                nc.scalar.activation(e[:, :], e[:, :], ACT.Exp).then_inc(exped, 1)
                meet(act, b, N_ENG, arrive, seen, leave, (turned_sb, exped))

        @block.vector
        def _(dve):
            with dve.Fori(0, B) as b:
                link = Chain(dve, step)
                s_ps, y_ps = (ps[:, at:at + 2, :].rearrange("p k n -> p (k n)") for at in (4, 6))
                dve.wait_ge(projected, 2)
                nc.vector.tensor_scalar(e[:, :], y_ps, -1.0, 80.0, ALU.mult, ALU.min).then_inc(clipped, 1)
                dve.wait_ge(exped, 1)
                link(nc.vector.tensor_scalar(e[:, :], e[:, :], 1.0, None, ALU.add))
                link(nc.vector.reciprocal(r[:, :], e[:, :]))
                link(nc.vector.tensor_tensor(g[:, :], y_ps, r[:, :], ALU.mult))
                link(nc.vector.tensor_tensor(g[:, :], s_ps, g[:, :], ALU.mult))
                dve.wait_ge(x_in, 16)
                nc.vector.tensor_tensor(x1[:, :, :].rearrange("p k c -> p (k c)"), x[:, :, :].rearrange("p k c -> p (k c)"),
                                        g[:, :], ALU.add).then_inc(x1_ready, 1)
                meet(dve, b, N_ENG, arrive, seen, leave, (step, clipped, x_in))


def recur_layer1(nc, ps, col, A, x1_dram, s1_dram):
    NGRP = 4
    NPAIR = NSEG // 2
    WB = DK + 1
    with ExitStack() as ctx:
        t = Scope(nc, ctx)
        cst = t.sb("cst1", [P, A["consts1"].shape[1]])
        wq, wk, wv = (t.sb("m_" + n, [P, KC, NGRP * GH * DK]) for n in ("wq", "wk", "wv"))
        NJ = NGRP * GH
        wo = t.sb("m_wo", [P, NJ, HID])
        share = t.sb("m_share", [P, 2, NGRP * GH])
        se = t.sb("m_se", [P, NGRP * GH])
        ident_b = t.sb("m_ident_b", [P, P], BF16)
        mask_b = t.sb("m_mask_b", [P, P], BF16)
        xs = t.sb("m_xs", [P, NBLK, HID])
        stats = t.sb("m_stats", [P, NBLK, 6])
        mv = t.sb("m_mv", [P, NBLK, 2])
        rstd = t.sb("m_rstd", [P, NBLK])
        power = t.sb("m_power", [P, NBLK])
        xT = t.sb("m_xT", [P, KC, S])
        qT = t.sb("m_qT", [P, S])
        kT = t.sb("m_kT", [P, S])
        eq, ek = t.sb("m_eq", [P, S]), t.sb("m_ek", [P, S])
        sk = t.sb("m_sk", [P, S])
        sg = [[t.sb(f"m_sg{g}{h}", [P, NPAIR, 4, SEG]) for h in range(GH)] for g in range(2)]
        kn = [t.sb(f"m_kn{g}", [P, GH, NPAIR, DK]) for g in range(2)]
        v = [t.sb(f"m_v{g}", [P, NPAIR, GH, DK]) for g in range(2)]
        am = [t.sb(f"m_am{g}", [P, NPAIR, GH, DK]) for g in range(2)]
        at = [t.sb(f"m_at{g}", [P, GH, S]) for g in range(NGRP)]
        pr = t.sb("m_pr", [P, NPAIR, P])
        prT = t.sb("m_prT", [P, S])
        negm, psum_, prec = t.sb("m_negm", [P, NPAIR]), t.sb("m_psum", [P, NPAIR]), t.sb("m_prec", [P, NPAIR])
        mem = t.sb("m_mem", [P, GH, WB])
        rd = t.sb("m_rd", [P, GH])
        tmp = t.sb("m_tmp", [P, GH, DK])
        delta = t.sb("m_delta", [P, GH, WB])
        acc = t.sb("m_acc", [P, HID])

        w_in, preset, share_step = t.sem("w_in"), t.sem("m_preset"), t.sem("share_step")
        share_clip, share_exp, share_ready = t.sem("share_clip"), t.sem("share_exp"), t.sem("share_ready")
        stat_ready, apart, power_set = t.sem("m_stat_ready"), t.sem("m_apart"), t.sem("m_power_set")
        x_in, var_ready, eps_added, rstd_ready, xn_ready, xt_psum, xt_ready = (
            t.sem("m_" + n) for n in ("x_in", "var_ready", "eps_added", "rstd_ready", "xn_ready", "xt_psum", "xt_ready"))
        proj_ready, qk_ready, min_ready, exp_ready, sigq_ready, sigk_ready, sigk_placed = (
            t.sem(n) for n in ("proj_ready", "qk_ready", "min_ready", "exp_ready", "sigma_q_ready", "sigma_k_ready", "sigma_k_placed"))
        v_psum, v_ready, kn_psum, kn_ready = (t.sem(n) for n in ("v_psum1", "v_ready1", "kn_psum", "kn_ready"))
        sc_ready, max_raw, max_ready, p_ready, rs_ready, pn_ready = (
            t.sem(n) for n in ("sc_ready", "max_raw", "max_ready", "p_ready", "rs_ready", "pn_ready"))
        pt_psum, pt_ready, bt_psum, bt_ready = (t.sem(n) for n in ("pt_psum", "pt_ready", "bt_psum", "bt_ready"))
        d_ready, rd_ready, tmp_ready, delta_ready, read_done, u_ready, mem_ready = (
            t.sem(n) for n in ("d_ready", "rd_ready", "tmp_ready", "delta_ready", "read_done", "u_ready", "mem_ready"))
        am_psum, at_ready, out_psum, acc_ready, stored = (
            t.sem(n) for n in ("am_psum", "at_ready", "out_psum1", "acc_ready", "s_stored"))
        N_W = 6
        NUPD = NSEG - 1
        block = ctx.enter_context(nc.Block())

        class Group:

            def __init__(self, b, g):
                self.b, self.g = b + g // NGRP, g % NGRP
                self.par = g % 2
                self._b, self._g = b, g

            def upto(self, per, c):
                return self._b * (NGRP * per) + (self._g * per + c)

            def head(self, h):
                return self.g * GH + h

            @property
            def first(self):
                return isinstance(self._b, int) and self._b == 0 and self._g == 0

        def khalf(s):
            return slice(SEG * (s % 2), SEG * (s % 2) + SEG)

        def qhalf(s):
            return khalf(s + 1)

        def region(lo, hi, part=slice(0, P)):
            return ps[part, 0:2, :].rearrange("p b (h c) -> p (b h) c", h=2)[:, :, lo:hi]

        def windows(turn, last):
            for g in range(NGRP):
                n = Group(turn, g)
                yield n, (None if last and g == NGRP - 1 else Group(turn, g + 1)), (Group(turn, g - 1) if g else None)

        def run(eng, prologue, window):
            prologue()
            window(None, Group(0, 0), None)
            with eng.Fori(0, B - 1) as turn:
                for n, m, o in windows(turn, False):
                    window(n, m, o)
            for n, m, o in windows(B - 1, True):
                window(n, m, o)

        @block.sync
        def _(sp):
            sp.dma_start(cst[:, :], A["consts1"]).then_inc(w_in, 16)
            for dst, src in ((wq, A["Wq"]), (wk, A["Wk"]), (wv, A["Wv"])):
                sp.dma_start(dst[:, :, :], src.rearrange("(k p) n -> p k n", p=P)).then_inc(w_in, 16)
            sp.dma_start(wo[:, :, :], A["Wo"].rearrange("(h p) n -> p h n", p=P)).then_inc(w_in, 16)
            with nc.allow_non_contiguous_dma(reason="2048 words, once"):
                sp.dma_start(share[:, 0, :], A["betas"].rearrange("a h b p -> p (a h b)")).then_inc(w_in, 16)
            sp.dma_start(xs[:, :, :], tokens(x1_dram, 0)).then_inc(x_in, 16)
            sp.sem_inc(stored, 16)
            def store(b, g):
                sp.wait_ge(acc_ready, b * NGRP + (g + 1))
                rows = s1_dram[bass.ds(b, 1), :, :].rearrange("a (s g h r) c -> g h (a s) r c", s=NSEG, g=NGRP, h=GH)
                for h in range(GH):
                    sp.dma_start(rows[g, h], acc[h * NSEG * 4:(h + 1) * NSEG * 4, :]).then_inc(stored, 16)

            with sp.Fori(0, B - 1) as b:
                sp.wait_ge(xt_psum, b + 1)
                sp.dma_start(xs[:, :, :], tokens(x1_dram, b + 1)).then_inc(x_in, 16)
                for g in range(NGRP):
                    store(b, g)
            for g in range(NGRP):
                store(B - 1, g)
            sp.wait_ge(stored, 16 * (1 + B * NGRP * GH))

        @block.gpsimd
        def _(pool):
            nc.gpsimd.memset(power[:, :], -0.5).then_inc(power_set, 1)
            pool.wait_ge(power_set, 1)

            def inv_std(b):
                wait_apart(pool, var_ready, b + 1, apart)
                nc.gpsimd.tensor_scalar(rstd[:, :], mv[:, :, 1], EPS, None, ALU.add).then_inc(eps_added, 1)
                pool.wait_ge(eps_added, b + 1)
                nc.gpsimd.tensor_tensor(rstd[:, :], rstd[:, :], power[:, :], ALU.pow).then_inc(rstd_ready, 1)

            def place_keys(m, h):
                wait_apart(pool, sigk_ready, m.upto(GH, h + 1), apart)
                nc.gpsimd.tensor_copy(sg[m.par][h][:, :, 0:4:3, :], sk[:, :].rearrange("p (a b c) -> p a b c", a=NPAIR, b=2)).then_inc(sigk_placed, 1)

            def normalise(m, h):
                pool.wait_ge(rs_ready, m.upto(GH, h + 1))
                p = pr
                nc.gpsimd.tensor_tensor(p[:, :, :], p[:, :, :], prec[:, :].unsqueeze(2).broadcast_to([P, NPAIR, P]), ALU.mult).then_inc(pn_ready, 1)

            def window(n, m, o):
                if n is not None:
                    normalise(n, GH - 1)
                if m is not None:
                    for h in range(GH):
                        place_keys(m, h)
                        if h < GH - 1:
                            normalise(m, h)
                if n is not None and n.g == 1 and not (isinstance(n.b, int) and n.b == B - 1):
                    inv_std(n.b + 1)

            run(pool, lambda: inv_std(0), window)

        @block.tensor
        def _(pe):
            ident = cst[:, slice(*col["ident"])]

            def product(out, pairs):
                for i, (lhsT, rhs) in enumerate(pairs):
                    last = nc.tensor.matmul(out, lhsT, rhs, start=(i == 0), stop=(i == len(pairs) - 1))
                return last

            def turn_x(b, first=False):
                pe.wait_ge(xn_ready, b + 1)
                if not first:
                    pe.wait_ge(qk_ready, (b * NGRP) * (2 * GH))
                for c in range(KC):
                    for k in range(NBLK):
                        last = nc.tensor.transpose(ps[:, 2 + c, k * P:(k + 1) * P], xs[:, k, c * P:(c + 1) * P], ident)
                last.then_inc(xt_psum, 1)

            def project(m, h):
                if h == 0:
                    pe.wait_ge(xt_ready, m.b + 1)
                if not (m.first and h == 0):
                    pe.wait_ge(qk_ready, m.upto(2 * GH, 2 * h))
                cols = slice(m.head(h) * DK, (m.head(h) + 1) * DK)
                for bank, weights in ((2, wq), (3, wk)):
                    product(ps[:, bank, :], [(weights[:, c, cols], xT[:, c, :]) for c in range(KC)]).then_inc(proj_ready, 1)

            def project_v(m, k, bank):
                product(ps[:, bank, :], [(xT[:, c, k * P:(k + 1) * P], wv[:, c, m.g * GH * DK:(m.g + 1) * GH * DK])
                                         for c in range(KC)]).then_inc(v_psum, 1)

            def turn_keys(m, h):
                pe.wait_ge(sigk_ready, m.upto(GH, h + 1))
                pe.wait_ge(v_ready, m.upto(NBLK, 2 if h == 0 else NBLK))
                if h:
                    pe.wait_ge(kn_ready, m.upto(GH, h))
                for p in range(NPAIR):
                    blk = slice(p * P, (p + 1) * P)
                    last = nc.tensor.transpose(ps[:, 5, blk], sk[:, blk], ident)
                last.then_inc(kn_psum, 1)

            def score(m, h):
                pe.wait_ge(qk_ready, m.upto(2 * GH, 2 * h + 2))
                if not (m.first and h == 0):
                    pe.wait_ge(p_ready, m.upto(GH, h))
                nc.tensor.matmul(ps[:, 6, :].rearrange("p (a c) -> p a c", a=NPAIR), ident_b[:, :],
                                 mask_b[:, :].unsqueeze(1).broadcast_to([P, NPAIR, P]), start=True, stop=False, skip_group_check=True)
                for p in range(NPAIR):
                    blk = slice(p * P, (p + 1) * P)
                    last = nc.tensor.matmul(ps[:, 6, blk], qT[:, blk], kT[:, blk],
                                            start=False, stop=(p == NPAIR - 1), skip_group_check=True)
                last.then_inc(sc_ready, 1)

            def turn_probs(m, h):
                pe.wait_ge(pn_ready, m.upto(GH, h + 1))
                if not (m.first and h == 0):
                    pe.wait_ge(bt_ready, m.upto(GH, h))
                for p in range(NPAIR):
                    last = nc.tensor.transpose(ps[:, 7, p * P:(p + 1) * P], pr[:, p, :], ident)
                last.then_inc(pt_psum, 1)

            def local(m, h):
                pe.wait_ge(pt_ready, m.upto(GH, h + 1))
                pe.wait_ge(v_ready, m.upto(NBLK, NBLK))
                for p in range(NPAIR):
                    blk = slice(p * P, (p + 1) * P)
                    last = nc.tensor.matmul(ps[:, 7, blk], v[m.par][:, p, h, :], prT[:, blk], start=True, stop=True)
                last.then_inc(bt_psum, 1)

            def read_memory(n, s):
                if s == 0:
                    pe.wait_ge(sigq_ready, n.upto(GH, GH))
                    pe.wait_ge(sigk_placed, n.upto(GH, GH))
                pe.wait_ge(mem_ready, n.upto(NSEG, s + 1))
                for h in range(GH):
                    last = nc.tensor.matmul(region(0, WB)[:, h, :], sg[n.par][h][:, s // 2, 2 * (s % 2):2 * (s % 2) + 2, :].rearrange("p a c -> p (a c)"),
                                            mem[:, h, :], start=True, stop=True)
                last.then_inc(d_ready, 1)

            def write_memory(n, s):
                if s == 0:
                    pe.wait_ge(kn_ready, n.upto(GH, GH))
                pe.wait_ge(delta_ready, n.upto(NUPD, s + 1))
                pe.wait_ge(read_done, n.upto(NSEG, s + 1))
                half = khalf(s)
                for h in range(GH):
                    last = nc.tensor.matmul(region(0, WB)[:, h, :], kn[n.par][half, h, s // 2, :], delta[half, h, :], start=True, stop=True)
                last.then_inc(u_ready, 1)

            def turn_read(o, h, bank):
                pe.wait_ge(read_done, o.upto(NSEG, NSEG))
                for p in range(NPAIR):
                    last = nc.tensor.transpose(ps[:, bank, p * P:(p + 1) * P], am[o.par][:, p, h, :], ident)
                last.then_inc(am_psum, 1)

            def emit(o, j):
                if j == 0:
                    pe.wait_ge(at_ready, o.upto(GH, GH))
                heads = at[o.g][:, :, :].rearrange("p h (r j) -> p (h r) j", j=NJ)
                for i in range(j * NJ // 2, (j + 1) * NJ // 2):
                    last = nc.tensor.matmul(ps[:, 4, 0:HID], heads[:, :, i], wo[:, i, :], start=(i == 0), stop=(i == NJ - 1))
                if j:
                    last.then_inc(out_psum, 1)

            def window(n, m, o):
                for s in range(NSEG):
                    if n is not None:
                        read_memory(n, s)
                    if m is not None:
                        if s % 2 == 0:
                            project(m, s // 2)
                        elif s < 4:
                            if o is not None or (s == 1 and n is not None and not n.first):
                                if s == 1:
                                    if o is not None:
                                        pe.wait_ge(at_ready, o.upto(GH, 2))
                                    else:
                                        pe.wait_ge(acc_ready, n.upto(1, 0))
                                else:
                                    pe.wait_ge(at_ready, o.upto(GH, GH))
                            if s == 3:
                                pe.wait_ge(kn_ready, m.upto(GH, 1))
                                pe.wait_ge(v_ready, m.upto(NBLK, 2))
                            project_v(m, s - 1, 4)
                            project_v(m, s, 5)
                    if o is not None and s in (5, 7):
                        if s == 5 and m is not None:
                            pe.wait_ge(v_ready, m.upto(NBLK, NBLK))
                        emit(o, (s - 5) // 2)
                    if n is not None and s < NUPD:
                        write_memory(n, s)
                    if n is not None and s == 0:
                        turn_probs(n, GH - 1)
                    if n is not None and s == 1:
                        local(n, GH - 1)
                    if m is not None and s % 2 == 0 and s:
                        turn_probs(m, s // 2 - 1)
                    if m is not None and s % 2:
                        score(m, s // 2)
                        if s > 1:
                            local(m, s // 2 - 1)
                        turn_keys(m, s // 2)
                    if o is not None and s in (0, 2):
                        if s == 0:
                            if n is not None:
                                pe.wait_ge(kn_ready, n.upto(GH, GH))
                            if o.g:
                                pe.wait_ge(acc_ready, o.upto(1, 0))
                        else:
                            if m is not None:
                                pe.wait_ge(v_ready, m.upto(NBLK, 2))
                                pe.wait_ge(kn_ready, m.upto(GH, 1))
                            else:
                                pe.wait_ge(at_ready, o.upto(GH, 2))
                        turn_read(o, s, 5)
                        turn_read(o, s + 1, 4)
                if n is not None and n.g == 2 and m is not None and not (isinstance(n.b, int) and n.b == B - 1):
                    turn_x(n.b + 1)
                if n is not None and n.g == NGRP - 1:
                    if m is not None:
                        pe.wait_ge(kn_ready, m.upto(GH, GH))
                    pe.wait_ge(acc_ready, n.upto(1, 0))
                    turn_read(n, 0, 5)
                    turn_read(n, 1, 4)
                    pe.wait_ge(at_ready, n.upto(GH, 2))
                    turn_read(n, 2, 5)
                    turn_read(n, 3, 4)
                    emit(n, 0)
                    emit(n, 1)

            def prologue():
                pe.wait_ge(preset, 2)
                pe.wait_ge(w_in, 16 * N_W)
                turn_x(0, first=True)

            run(pe, prologue, window)

        @block.scalar
        def _(act):
            def take_x(b):
                act.wait_ge(xt_psum, b + 1)
                nc.scalar.activation(xT[:, :, :], ps[:, 2:4, :], ACT.Copy).then_inc(xt_ready, 1)

            def take_qk(m, h):
                for i, dst in enumerate((qT, kT)):
                    act.wait_ge(proj_ready, m.upto(2 * GH, 2 * h + i + 1))
                    nc.scalar.activation(dst[:, :], ps[:, 2 + i, :], ACT.Copy).then_inc(qk_ready, 1)
                for i, e in enumerate((eq, ek)):
                    act.wait_ge(min_ready, m.upto(2 * GH, 2 * h + i + 1))
                    nc.scalar.activation(e[:, :], e[:, :], ACT.Exp).then_inc(exp_ready, 1)

            def take_v(m, k, bank):
                act.wait_ge(v_psum, m.upto(NBLK, k + 1))
                nc.scalar.activation(v[m.par][:, k, :, :].rearrange("p h c -> p (h c)"), ps[:, bank, :], ACT.Copy).then_inc(v_ready, 1)

            def take_keys(m, h):
                act.wait_ge(kn_psum, m.upto(GH, h + 1))
                nc.scalar.activation(kn[m.par][:, h, :, :].rearrange("p a c -> p (a c)"), ps[:, 5, :], ACT.Copy).then_inc(kn_ready, 1)

            def probabilities(m, h):
                act.wait_ge(max_ready, m.upto(GH, h + 1))
                for p in range(NPAIR):
                    last = nc.scalar.activation(pr[:, p, :], ps[:, 6, p * P:(p + 1) * P], ACT.Exp,
                                                bias=negm[:, p:p + 1], scale=float(DK) ** -0.5, accum_out=psum_[:, p:p + 1])
                last.then_inc(p_ready, 1)

            def take_turned_probs(m, h):
                act.wait_ge(pt_psum, m.upto(GH, h + 1))
                nc.scalar.activation(prT[:, :], ps[:, 7, :], ACT.Copy).then_inc(pt_ready, 1)

            def take_local(m, h):
                act.wait_ge(bt_psum, m.upto(GH, h + 1))
                nc.scalar.activation(at[m.g][:, h, :], ps[:, 7, :], ACT.Copy, scale=share[:, 1, m.head(h):m.head(h) + 1]).then_inc(bt_ready, 1)

            def take_read(n, s):
                act.wait_ge(rd_ready, n.upto(NSEG, s + 1))
                half = qhalf(s)
                for h in range(GH):
                    last = nc.scalar.activation(am[n.par][half, s // 2, h, :], region(0, DK, half)[:, h, :], ACT.Copy, scale=rd[half, h:h + 1])
                last.then_inc(read_done, 1)

            def take_out(o):
                act.wait_ge(out_psum, o.upto(1, 1))
                act.wait_ge(stored, o.upto(16 * GH, 16))
                nc.scalar.activation(acc[:, :], ps[:, 4, 0:HID], ACT.Copy).then_inc(acc_ready, 1)

            def window(n, m, o):
                for s in range(NSEG):
                    if n is not None:
                        take_read(n, s)
                    if m is not None:
                        if s % 2 == 0:
                            take_qk(m, s // 2)
                        elif s < 4:
                            take_v(m, s - 1, 4)
                            take_v(m, s, 5)
                    if n is not None and s == 0:
                        take_turned_probs(n, GH - 1)
                    if n is not None and s == 1:
                        take_local(n, GH - 1)
                    if m is not None and s % 2 == 0 and s:
                        take_turned_probs(m, s // 2 - 1)
                    if m is not None and s % 2:
                        probabilities(m, s // 2)
                        if s > 1:
                            take_local(m, s // 2 - 1)
                        take_keys(m, s // 2)
                    if o is not None and s == 7:
                        take_out(o)
                if n is not None and n.g == 2 and m is not None and not (isinstance(n.b, int) and n.b == B - 1):
                    take_x(n.b + 1)
                if n is not None and n.g == NGRP - 1:
                    take_out(n)

            def prologue():
                act.wait_ge(share_clip, 1)
                nc.scalar.activation(se[:, :], se[:, :], ACT.Exp).then_inc(share_exp, 1)
                act.wait_ge(share_ready, 1)
                take_x(0)

            run(act, prologue, window)

        @block.vector
        def _(dve):
            def normalise_x(b):
                dve.wait_ge(rstd_ready, b + 1)
                for k in range(NBLK):
                    last = nc.vector.tensor_scalar(xs[:, k, :], xs[:, k, :], mv[:, k, 0:1], rstd[:, k:k + 1], ALU.subtract, ALU.mult)
                last.then_inc(xn_ready, 1)

            def stats_x(b):
                dve.wait_ge(x_in, b * 16 + 16)
                for k in range(NBLK):
                    last = nc.vector.bn_stats(stats[:, k, :], xs[:, k, :])
                last.then_inc(stat_ready, 1)
                wait_apart(dve, stat_ready, b + 1, apart)
                for k in range(NBLK):
                    last = nc.vector.bn_aggr(mv[:, k, :], stats[:, k, :])
                last.then_inc(var_ready, 1)
                dve.wait_ge(var_ready, b + 1)

            def pairs(x):
                return x[:, :].rearrange("p (a c) -> p a c", a=NPAIR)

            def sigma(m, h):
                for i, (x, e) in enumerate(((qT, eq), (kT, ek))):
                    dve.wait_ge(qk_ready, m.upto(2 * GH, 2 * h + i + 1))
                    nc.vector.tensor_scalar(e[:, :], x[:, :], 0.0, None, ALU.min).then_inc(min_ready, 1)
                dve.wait_ge(exp_ready, m.upto(2 * GH, 2 * h + 1))
                nc.vector.scalar_tensor_tensor(sg[m.par][h][:, :, 1:3, :].rearrange("p a b c -> p a (b c)"), pairs(qT), 1.0,
                                               pairs(eq), ALU.add, ALU.max).then_inc(sigq_ready, 1)
                dve.wait_ge(exp_ready, m.upto(2 * GH, 2 * h + 2))
                if not (m.first and h == 0):
                    dve.wait_ge(sigk_placed, m.upto(GH, h))
                nc.vector.scalar_tensor_tensor(sk[:, :], kT[:, :], 1.0, ek[:, :], ALU.add, ALU.max).then_inc(sigk_ready, 1)

            def maximum(m, h):
                dve.wait_ge(sc_ready, m.upto(GH, h + 1))
                nc.vector.tensor_reduce(negm[:, :], ps[:, 6, :].rearrange("p (a c) -> p a c", a=NPAIR), AXX, ALU.max, negate=True).then_inc(max_raw, 1)
                dve.wait_ge(max_raw, m.upto(GH, h + 1))
                nc.vector.tensor_scalar(negm[:, :], negm[:, :], float(DK) ** -0.5, None, ALU.mult).then_inc(max_ready, 1)

            def inv_sum(m, h):
                dve.wait_ge(p_ready, m.upto(GH, h + 1))
                nc.vector.reciprocal(prec[:, :], psum_[:, :]).then_inc(rs_ready, 1)

            def reset_memory(n):
                if not n.first:
                    dve.wait_ge(read_done, n.upto(NSEG, 0))
                nc.vector.memset(mem[:, :, 0:DK], 0.0)
                nc.vector.memset(mem[:, :, DK:WB], 1.0 / DK).then_inc(mem_ready, 1)

            def change(n, s):
                dve.wait_ge(d_ready, n.upto(NSEG, s + 1))
                nc.vector.reciprocal(rd[:, :], region(DK, WB)[:, :, 0]).then_inc(rd_ready, 1)
                if s == NUPD:
                    return
                half = khalf(s)
                dve.wait_ge(rd_ready, n.upto(NSEG, s + 1))
                nc.vector.tensor_tensor(tmp[half, :, :], region(0, DK, half), rd[half, :].unsqueeze(2).broadcast_to([SEG, GH, DK]), ALU.mult).then_inc(tmp_ready, 1)
                if s == 0:
                    dve.wait_ge(v_ready, n.upto(NBLK, NBLK))
                dve.wait_ge(tmp_ready, n.upto(NUPD, s + 1))
                nc.vector.tensor_tensor(delta[half, :, 0:DK], v[n.par][half, s // 2, :, :], tmp[half, :, :], ALU.subtract).then_inc(delta_ready, 1)

            def update(n, s):
                dve.wait_ge(u_ready, n.upto(NUPD, s + 1))
                dve.wait_ge(mem_ready, n.upto(NSEG, s + 1))
                nc.vector.tensor_tensor(mem[:, :, :], region(0, WB), mem[:, :, :], ALU.add).then_inc(mem_ready, 1)

            def add_read(o, h, bank):
                dve.wait_ge(am_psum, o.upto(GH, h + 1))
                dve.wait_ge(bt_ready, o.upto(GH, h + 1))
                read = ps[:, bank, :].rearrange("p (a b c) -> p a b c", a=NPAIR, b=2)
                sum_ = at[o.g][:, h, :].rearrange("p (a b c) -> p a b c", a=NPAIR, b=2)
                for i in range(2):
                    last = nc.vector.scalar_tensor_tensor(sum_[:, :, i, :], read[:, :, 1 - i, :], share[:, 0, o.head(h):o.head(h) + 1],
                                                          sum_[:, :, i, :], ALU.mult, ALU.add)
                last.then_inc(at_ready, 1)

            def window(n, m, o):
                for s in range(NSEG):
                    if n is not None:
                        change(n, s)
                        if s == 0:
                            inv_sum(n, GH - 1)
                    if m is not None and s % 2 == 0 and s:
                        inv_sum(m, s // 2 - 1)
                    if n is not None and s < NUPD:
                        update(n, s)
                    if m is not None:
                        if s % 2 == 0:
                            sigma(m, s // 2)
                        else:
                            maximum(m, s // 2)
                    if o is not None and s in (0, 2):
                        add_read(o, s, 5)
                        add_read(o, s + 1, 4)
                    if n is not None and n.g in (1, 2) and m is not None and s == 4 and not (isinstance(n.b, int) and n.b == B - 1):
                        if n.g == 1:
                            stats_x(n.b + 1)
                        else:
                            normalise_x(n.b + 1)
                if m is not None:
                    reset_memory(m)
                if n is not None and n.g == NGRP - 1:
                    for h in range(GH):
                        add_read(n, h, 5 - h % 2)

            def prologue():
                link = Chain(dve, share_step)
                nc.vector.memset(delta[:, :, DK:WB], 1.0).then_inc(preset, 1)
                dve.wait_ge(w_in, 16 * N_W)
                nc.vector.tensor_copy(ident_b[:, :], cst[:, slice(*col["ident"])])
                nc.vector.tensor_copy(mask_b[:, :], cst[:, slice(*col["mask_seg"])]).then_inc(preset, 1)
                nc.vector.tensor_scalar(se[:, :], share[:, 0, :], -1.0, 80.0, ALU.mult, ALU.min).then_inc(share_clip, 1)
                dve.wait_ge(share_exp, 1)
                link(nc.vector.tensor_scalar(se[:, :], se[:, :], 1.0, None, ALU.add))
                link(nc.vector.reciprocal(share[:, 0, :], se[:, :]))
                nc.vector.tensor_scalar(share[:, 1, :], share[:, 0, :], -1.0, 1.0, ALU.mult, ALU.add).then_inc(share_ready, 1)
                stats_x(0)
                normalise_x(0)

            run(dve, prologue, window)

def mix_layer1(nc, ps, col, A, x1_dram, s1_dram, out):
    NT = NBLK * NTILE
    TAB = 2 * SLICE * GRID + 3
    U_MAX = float(np.float32(1.0 - 1e-6))
    with ExitStack() as ctx:
        t = Scope(nc, ctx)
        cst = t.sb("cst2", [P, A["consts2"].shape[1]])
        xs, xn, xf, sg, w1, w2 = (t.sb("f_" + n, [P, NBLK, HID]) for n in ("xs", "xn", "xf", "sg", "w1", "w2"))
        s1 = t.sb("f_s1", [P, NBLK, HID])
        xn_all = t.sb("f_xn_all", [P, B, NBLK * HID])
        hot_all = t.sb("f_hot_all", [P, B, NT])
        hotT_all = t.sb("f_hotT_all", [NTILE, B, S])
        sl_all = t.sb("f_sl_all", [P, B, NBLK * SLICE])
        slopes = t.sb("f_slopes", [P, NTILE * SLICE, GRID])
        want = t.sb("f_want", [P, NTILE * SLICE])
        gamma, beta = t.sb("f_gamma", [P, HID]), t.sb("f_beta", [P, HID])
        table = t.sb("f_table", [NTILE, TAB])
        stats, mv = t.sb("f_stats", [P, NBLK, 6]), t.sb("f_mv", [P, NBLK, 2])
        rstd, power = t.sb("f_rstd", [P, NBLK]), t.sb("f_power", [P, NBLK])
        ts, hot, pen, lo, hi = (t.sb("f_" + n, [P, NT]) for n in ("ts", "hot", "pen", "lo", "hi"))
        cs, ch = t.sb("f_cs", [P, NBLK * NCLUSTER]), t.sb("f_ch", [P, NBLK * NCLUSTER])
        top = t.sb("f_top", [P, NBLK])
        ends = t.sb("f_ends", [P, 2, NBLK])
        least, most = t.sb("f_least", [P, NT]), t.sb("f_most", [P, NT])
        ends64 = t.sb("f_ends64", [P, 2, NTILE])
        hotT = t.sb("f_hotT", [NTILE, S])
        sl, dl = t.sb("f_sl", [P, NBLK * SLICE]), t.sb("f_dl", [P, NBLK * SLICE])
        tab = t.sb("f_tab", [P, NBLK, 3])
        rng = t.sb("f_rng", [P, NBLK])
        d, ge, in_, val = (t.sb("f_" + n, [P, NBLK * SLICE, GRID]) for n in ("d", "ge", "in", "val"))

        w_in, preset, want_sum, want_ready = t.sem("f_w_in"), t.sem("f_preset"), t.sem("f_want_sum"), t.sem("f_want_ready")
        x_in, var_ready, eps_added, rstd_ready = (t.sem("f_" + n) for n in ("x_in", "var_ready", "eps_added", "rstd_ready"))
        xf_ready, sign_ready, hot_ready, hot_psum, hot_turned = (t.sem("f_" + n) for n in ("xf_ready", "sign_ready", "hot_ready", "hot_psum", "hot_turned"))
        step, pstep = t.sem("f_step"), t.sem("f_pstep")
        arrive, seen, leave = t.sem("f_arrive"), t.sem("f_seen"), t.sem("f_leave")
        N_ENG = 5
        first = ExitStack()
        block = first.enter_context(nc.Block())

        def per_block(ap):
            return ap.rearrange("p (k n) -> p k n", k=NBLK)

        def cells(x):
            return x[:, :, :].rearrange("p (k j) g -> p k (j g)", k=NBLK)

        def flat(x):
            return x[:, :, :].rearrange("p k c -> p (k c)")

        @block.sync
        def _(sp):
            for dst, src in (
                (cst[:, :], A["consts2"]),
                (slopes[:, :, :].rearrange("p a g -> p (a g)"), A["slopes"].rearrange("(o t) j g -> o (t j g)", o=1).broadcast_to([P, NTILE * SLICE * GRID])),
                (gamma[:, :], A["gamma"].unsqueeze(0).broadcast_to([P, HID])),
                (beta[:, :], A["beta"].unsqueeze(0).broadcast_to([P, HID])),
                (table[:, 0:SLICE * GRID], A["bases"].rearrange("t j g -> t (j g)")),
                (table[:, SLICE * GRID:2 * SLICE * GRID], A["slopes"].rearrange("t j g -> t (j g)")),
                (table[:, 2 * SLICE * GRID:2 * SLICE * GRID + 1], A["oscale"].unsqueeze(1)),
            ):
                sp.dma_start(dst, src).then_inc(w_in, 16)
            with sp.Fori(0, B) as b:
                sp.dma_start(xs[:, :, :], tokens(x1_dram, b)).then_inc(x_in, 16)
                sp.wait_ge(x_in, 16)
                meet(sp, b, N_ENG, arrive, seen, leave, ())

        @block.gpsimd
        def _(pool):
            nc.gpsimd.memset(power[:, :], -0.5).then_inc(preset, 1)
            pool.wait_ge(preset, 1)
            with pool.Fori(0, B) as b:
                for n in range(2):
                    pool.wait_ge(var_ready, n + 1)
                    nc.gpsimd.tensor_scalar(rstd[:, :], mv[:, :, 1], EPS, None, ALU.add).then_inc(eps_added, 1)
                    pool.wait_ge(eps_added, n + 1)
                    nc.gpsimd.tensor_tensor(rstd[:, :], rstd[:, :], power[:, :], ALU.pow).then_inc(rstd_ready, 1)
                meet(pool, b, N_ENG, arrive, seen, leave, (eps_added, rstd_ready))

        @block.tensor
        def _(pe):
            ident = cst[:, slice(*col["ident"])]
            pe.wait_ge(w_in, 16 * 7)
            with pe.Fori(0, B) as b:
                pe.wait_ge(hot_ready, 1)
                for k in range(NBLK):
                    last = nc.tensor.transpose(ps[0:NTILE, 0, k * P:(k + 1) * P], hot[:, k * NTILE:(k + 1) * NTILE], ident)
                last.then_inc(hot_psum, 1)
                meet(pe, b, N_ENG, arrive, seen, leave, (hot_psum,))

        @block.scalar
        def _(act):
            act.wait_ge(want_sum, 1)
            nc.scalar.activation(want[:, :], want[:, :], ACT.Sign).then_inc(want_ready, 1)
            with act.Fori(0, B) as b:
                act.wait_ge(xf_ready, 1)
                nc.scalar.activation(sg[:, :, :], xf[:, :, :], ACT.Sign).then_inc(sign_ready, 1)
                act.wait_ge(hot_psum, 1)
                nc.scalar.activation(hotT_all[:, bass.ds(b, 1), :], ps[0:NTILE, 0:1, :], ACT.Copy).then_inc(hot_turned, 1)
                meet(act, b, N_ENG, arrive, seen, leave, (sign_ready, hot_turned))

        @block.vector
        def _(dve):
            nc.vector.memset(least[:, :], BIG)
            nc.vector.memset(most[:, :], -BIG)
            dve.wait_ge(w_in, 16 * 7)
            nc.vector.tensor_reduce(want[:, :], slopes[:, :, :], AXX, ALU.add).then_inc(want_sum, 1)
            dve.wait_ge(want_ready, 1)
            with dve.Fori(0, B) as b:
                link = Chain(dve, step)

                def moments(x, n):
                    for k in range(NBLK):
                        last = nc.vector.bn_stats(stats[:, k, :], x[:, k, :])
                    link(last)
                    for k in range(NBLK):
                        last = nc.vector.bn_aggr(mv[:, k, :], stats[:, k, :])
                    last.then_inc(var_ready, 1)
                    dve.wait_ge(var_ready, n + 1)
                    dve.wait_ge(rstd_ready, n + 1)

                def normalised(dst, x):
                    for k in range(NBLK):
                        last = nc.vector.tensor_scalar(dst[:, k, :], x[:, k, :], mv[:, k, 0:1], rstd[:, k:k + 1], ALU.subtract, ALU.mult)
                    link(last)

                dve.wait_ge(x_in, 16)
                moments(xs, 0)
                normalised(xn, xs)
                moments(xn, 1)
                normalised(xf, xn)
                nc.vector.tensor_copy(xn_all[:, bass.ds(b, 1), :], xn[:, :, :].rearrange("p k c -> p (k c)").unsqueeze(1))
                link(nc.vector.tensor_tensor(xf[:, :, :], xf[:, :, :], gamma[:, :].unsqueeze(1).broadcast_to([P, NBLK, HID]), ALU.mult))
                nc.vector.tensor_tensor(xf[:, :, :], xf[:, :, :], beta[:, :].unsqueeze(1).broadcast_to([P, NBLK, HID]), ALU.add).then_inc(xf_ready, 1)
                dve.wait_ge(sign_ready, 1)
                link(nc.vector.tensor_tensor(w1[:, :, :], sg[:, :, :], want[:, :].unsqueeze(1).broadcast_to([P, NBLK, HID]), ALU.mult))
                link(nc.vector.tensor_reduce(ts[:, :], w1[:, :, :].rearrange("p k (t j) -> p (k t) j", j=SLICE), AXX, ALU.add))
                link(nc.vector.tensor_reduce(cs[:, :], ts[:, :].rearrange("p (c t) -> p c t", t=PER_CLUSTER), AXX, ALU.add))
                link(nc.vector.scalar_tensor_tensor(cs[:, :], cs[:, :], float(NCLUSTER), cst[:, slice(*col["cluster"])], ALU.mult, ALU.subtract))
                link(nc.vector.tensor_reduce(top[:, :], per_block(cs[:, :]), AXX, ALU.max))
                link(nc.vector.tensor_tensor(per_block(ch[:, :]), per_block(cs[:, :]), top[:, :].unsqueeze(2).broadcast_to([P, NBLK, NCLUSTER]), ALU.is_equal))
                link(nc.vector.scalar_tensor_tensor(ts[:, :], ts[:, :], float(PER_CLUSTER), cst[:, slice(*col["in_cluster"])], ALU.mult, ALU.subtract))
                tiles = ts[:, :].rearrange("p (c t) -> p c t", t=PER_CLUSTER)
                link(nc.vector.scalar_tensor_tensor(tiles, ch[:, :].unsqueeze(2).broadcast_to([P, NBLK * NCLUSTER, PER_CLUSTER]), 1000.0, tiles, ALU.mult, ALU.add))
                link(nc.vector.tensor_reduce(top[:, :], per_block(ts[:, :]), AXX, ALU.max))
                nc.vector.tensor_tensor(per_block(hot[:, :]), per_block(ts[:, :]), top[:, :].unsqueeze(2).broadcast_to([P, NBLK, NTILE]), ALU.is_equal).then_inc(hot_ready, 1)
                dve.wait_ge(hot_ready, 1)
                nc.vector.tensor_copy(hot_all[:, bass.ds(b, 1), :], hot[:, :].unsqueeze(1))
                link(nc.vector.tensor_tensor(w2[:, :, :].rearrange("p k (t j) -> p (k t) j", j=SLICE), xf[:, :, :].rearrange("p k (t j) -> p (k t) j", j=SLICE),
                                             hot[:, :].unsqueeze(2).broadcast_to([P, NT, SLICE]), ALU.mult))
                link(nc.vector.tensor_reduce(sl[:, :].rearrange("p (k j) -> p k j", k=NBLK), w2[:, :, :].rearrange("p k (t j) -> p k j t", j=SLICE), AXX, ALU.add))
                nc.vector.tensor_copy(sl_all[:, bass.ds(b, 1), :], sl[:, :].unsqueeze(1))
                nc.vector.tensor_reduce(ends[:, 0, :], per_block(sl[:, :]), AXX, ALU.min)
                link(nc.vector.tensor_reduce(ends[:, 1, :], per_block(sl[:, :]), AXX, ALU.max))
                nc.vector.tensor_scalar(pen[:, :], hot[:, :], -BIG, BIG, ALU.mult, ALU.add)
                nc.vector.tensor_tensor(per_block(lo[:, :]), per_block(hot[:, :]), ends[:, 0, :].unsqueeze(2).broadcast_to([P, NBLK, NTILE]), ALU.mult)
                link(nc.vector.tensor_tensor(per_block(hi[:, :]), per_block(hot[:, :]), ends[:, 1, :].unsqueeze(2).broadcast_to([P, NBLK, NTILE]), ALU.mult))
                nc.vector.tensor_tensor(lo[:, :], lo[:, :], pen[:, :], ALU.add)
                link(nc.vector.tensor_tensor(hi[:, :], hi[:, :], pen[:, :], ALU.subtract))
                nc.vector.tensor_tensor(least[:, :], least[:, :], lo[:, :], ALU.min)
                link(nc.vector.tensor_tensor(most[:, :], most[:, :], hi[:, :], ALU.max))
                meet(dve, b, N_ENG, arrive, seen, leave, (step, var_ready, xf_ready, hot_ready, x_in))

        first.close()

        ends_ready, ends_psum, table_ready = t.sem("f2_ends_ready"), t.sem("f2_ends_psum"), t.sem("f2_table_ready")
        in_x, in_s, hot_copied, tab_psum, clipped, exped, mixed, stored = (
            t.sem("f2_" + n) for n in ("in_x", "in_s", "hot_copied", "tab_psum", "clipped", "exped", "mixed", "stored"))
        step2, arrive2, seen2, leave2 = t.sem("f2_step"), t.sem("f2_arrive"), t.sem("f2_seen"), t.sem("f2_leave")
        block = ctx.enter_context(nc.Block())
        BASES, SLOPES, SCALE, LEAST, MOST = 0, SLICE * GRID, TAB - 3, TAB - 2, TAB - 1

        @block.sync
        def _(sp):
            with sp.Fori(0, B) as b:
                sp.dma_start(s1[:, :, :], tokens(s1_dram, b)).then_inc(in_s, 16)
                sp.dma_start(xs[:, :, :], tokens(x1_dram, b)).then_inc(in_x, 16)
                sp.wait_ge(mixed, 1)
                sp.dma_start(tokens(out, b), xf[:, :, :]).then_inc(stored, 16)
                sp.wait_ge(stored, 16)
                meet(sp, b, N_ENG, arrive2, seen2, leave2, (mixed, stored))

        @block.gpsimd
        def _(pool):
            with pool.Fori(0, B) as b:
                nc.gpsimd.tensor_copy(hotT[:, :].unsqueeze(1), hotT_all[:, bass.ds(b, 1), :]).then_inc(hot_copied, 1)
                meet(pool, b, N_ENG, arrive2, seen2, leave2, (hot_copied,))

        @block.tensor
        def _(pe):
            pe.wait_ge(ends_ready, 2)
            for n in range(2):
                last = nc.tensor.transpose(ps[0:NTILE, 1, n * P:(n + 1) * P], ends64[:, n, :], cst[:, slice(*col["ident"])])
            last.then_inc(ends_psum, 1)
            pe.wait_ge(table_ready, 2)
            with pe.Fori(0, B) as b:
                pe.wait_ge(hot_copied, 1)
                for k in range(NBLK):
                    last = nc.tensor.matmul(ps[:, 2 + k // 2, (k % 2) * HID:(k % 2) * HID + TAB], hotT[:, k * P:(k + 1) * P], table[:, :],
                                            start=True, stop=True)
                last.then_inc(tab_psum, 1)
                meet(pe, b, N_ENG, arrive2, seen2, leave2, (tab_psum,))

        @block.scalar
        def _(act):
            with act.Fori(0, B) as b:
                act.wait_ge(clipped, 1)
                nc.scalar.activation(w1[:, :, :], w1[:, :, :], ACT.Exp).then_inc(exped, 1)
                meet(act, b, N_ENG, arrive2, seen2, leave2, (exped,))

        @block.vector
        def _(dve):
            for n, (src, op) in enumerate(((least, ALU.min), (most, ALU.max))):
                nc.vector.tensor_reduce(ends64[:, n, :], src[:, :].rearrange("p (k t) -> p t k", k=NBLK), AXX, op).then_inc(ends_ready, 1)
            dve.wait_ge(ends_psum, 1)
            for n, op in enumerate((ALU.min, ALU.max)):
                nc.vector.tensor_reduce(table[:, LEAST + n:LEAST + n + 1], ps[0:NTILE, 1, n * P:(n + 1) * P], AXX, op).then_inc(table_ready, 1)
            got = ps[:, 2:4, :].rearrange("p a (k c) -> p (a k) c", k=2)

            def four(ap):
                return ap.rearrange("p (k j) -> p k j", j=SLICE)

            def each(ap):
                return ap.unsqueeze(2).broadcast_to([P, NBLK, SLICE])

            with dve.Fori(0, B) as b:
                link = Chain(dve, step2)
                dve.wait_ge(tab_psum, 1)
                link(nc.vector.tensor_copy(tab[:, :, :], got[:, :, SCALE:TAB]))
                scale, least_t, most_t = (tab[:, :, n] for n in range(3))
                nc.vector.tensor_tensor(four(sl[:, :]), sl_all[:, bass.ds(b, 1), :].rearrange("p a (k j) -> p (a k) j", j=SLICE), each(least_t), ALU.subtract)
                link(nc.vector.tensor_tensor(rng[:, :], most_t, least_t, ALU.subtract))
                link(nc.vector.tensor_scalar(rng[:, :], rng[:, :], 1e-8, None, ALU.add))
                link(nc.vector.reciprocal(rng[:, :], rng[:, :]))
                link(nc.vector.tensor_tensor(four(sl[:, :]), four(sl[:, :]), each(rng[:, :]), ALU.mult))
                link(nc.vector.tensor_scalar(sl[:, :], sl[:, :], 0.0, U_MAX, ALU.max, ALU.min))
                link(nc.vector.tensor_scalar(sl[:, :], sl[:, :], float(GRID), None, ALU.mult))
                link(nc.vector.tensor_tensor(d[:, :, :], sl[:, :].unsqueeze(2).broadcast_to([P, NBLK * SLICE, GRID]),
                                             cst[:, col["grid"][0]:col["grid"][0] + GRID].unsqueeze(1).broadcast_to([P, NBLK * SLICE, GRID]), ALU.subtract))
                nc.vector.tensor_tensor(cells(val), got[:, :, SLOPES:SLOPES + SLICE * GRID], cells(d), ALU.mult)
                link(nc.vector.tensor_scalar(ge[:, :, :], d[:, :, :], 0.0, None, ALU.is_ge))
                nc.vector.scalar_tensor_tensor(in_[:, :, :], d[:, :, :], 1.0, ge[:, :, :], ALU.is_lt, ALU.mult)
                link(nc.vector.tensor_tensor(cells(val), got[:, :, BASES:BASES + SLICE * GRID], cells(val), ALU.add))
                link(nc.vector.tensor_tensor(val[:, :, :], val[:, :, :], in_[:, :, :], ALU.mult))
                link(nc.vector.tensor_reduce(dl[:, :], val[:, :, :], AXX, ALU.add))
                link(nc.vector.tensor_tensor(four(dl[:, :]), four(dl[:, :]), each(scale), ALU.mult))
                link(nc.vector.tensor_tensor(w2[:, :, :].rearrange("p k (t j) -> p k t j", j=SLICE),
                                             hot_all[:, bass.ds(b, 1), :].rearrange("p a (k t) -> p (a k) t", k=NBLK).unsqueeze(3).broadcast_to([P, NBLK, NTILE, SLICE]),
                                             four(dl[:, :]).unsqueeze(2).broadcast_to([P, NBLK, NTILE, SLICE]), ALU.mult))
                link(nc.vector.tensor_tensor(flat(w2), flat(w2), xn_all[:, bass.ds(b, 1), :].rearrange("p a n -> p (a n)"), ALU.add))
                nc.vector.tensor_scalar(w1[:, :, :], w2[:, :, :], -1.0, 80.0, ALU.mult, ALU.min).then_inc(clipped, 1)
                dve.wait_ge(exped, 1)
                link(nc.vector.tensor_scalar(w1[:, :, :], w1[:, :, :], 1.0, None, ALU.add))
                link(nc.vector.reciprocal(w1[:, :, :], w1[:, :, :]))
                link(nc.vector.tensor_tensor(w1[:, :, :], w1[:, :, :], w2[:, :, :], ALU.mult))
                dve.wait_ge(in_s, 16)
                link(nc.vector.tensor_tensor(w1[:, :, :], w1[:, :, :], s1[:, :, :], ALU.mult))
                dve.wait_ge(in_x, 16)
                nc.vector.tensor_tensor(xf[:, :, :], w1[:, :, :], xs[:, :, :], ALU.add).then_inc(mixed, 1)
                meet(dve, b, N_ENG, arrive2, seen2, leave2, (step2, clipped, in_s, in_x))


def recurrent_d2_kernel(nc, A, cst_cols, cols1, cols2, out):
    with ExitStack() as ctx:
        t = Scope(nc, ctx)
        ps = ctx.enter_context(nc.psum_tensor("ps", [P, 8, S], F32))
        parts_dram = [nc.dram_tensor(f"parts_{n}", [NPART, HD, B * H, S], BF16, kind="Internal").ap() for n in range(4)]
        v_dram = [nc.dram_tensor(f"values_{n}", [B * NG, P, NBLK * GH * (HD + 1)], F32, kind="Internal").ap() for n in range(2)]
        x1_dram = nc.dram_tensor("x1_dram", [B, S, HID], F32, kind="Internal").ap()
        s1_dram = nc.dram_tensor("s1_dram", [B, S, HID], F32, kind="Internal").ap()
        w = {}
        layer0 = ctx.enter_context(ExitStack())
        mids = Scope(nc, layer0)
        cst = mids.sb("cst0", [P, A["consts0"].shape[1]])
        with ExitStack() as early:
            e = Scope(nc, early)
            for name, shape, dt in (
                ("o_a", [P, KC, HID], F32), ("o_f", [P, KC, HID], F32),
                ("ident_b", [P, P], BF16), ("mask_qk", [P, P], BF16), ("mask_kq", [P, P], BF16),
            ):
                w[name] = mids.sb(name, shape, dt)
            for name, shape in (
                ("d", [P, KC, 2 * LAT]), ("q_a", [LAT, HID]), ("q_b", [LAT, HID]), ("k_a", [2 * LAT, HID]),
                ("v_a", [2 * LAT, HID]), ("kr_a", [P, KC, HID]), ("kr_b", [P, KC, HID]),
                ("q_f", [P, KC, HID]), ("k_f", [P, KC, HID]), ("v_f", [P, KC, HID]),
            ):
                w[name] = e.sb("w_" + name, shape)
            load_layer0(nc, e, w, cst, cst_cols, A)
            project_layer0(nc, ps, w, cst, cst_cols, A, parts_dram, v_dram)
        with ExitStack() as mid:
            o_all = Scope(nc, mid).sb("o_all", [P, B * NG, 2, NBLK * GH * HD])
            attend_layer0(nc, ps, w, cst, cst_cols, parts_dram, v_dram, o_all)
            gate_layer0(nc, ps, w, cst, cst_cols, A, o_all, x1_dram)
        layer0.close()
        recur_layer1(nc, ps, cols1, A, x1_dram, s1_dram)
        mix_layer1(nc, ps, cols2, A, x1_dram, s1_dram, out)


_INS = {
    "L0_attn_hidden_states": "x", "L0_attn_w_kv_d": "w_kv_d", "L0_attn_w_q_d": "w_q_d", "L0_attn_w_k_u": "w_k_u",
    "L0_attn_w_q_u": "w_q_u", "L0_attn_w_v_u": "w_v_u", "L0_attn_w_rope_k": "w_rope_k",
    "L0_attn_w_rope_q": "w_rope_q", "L0_attn_w_o": "w_o", "L0_ffn_Wa": "Wa", "L0_ffn_Wp": "Wp",
    "L0_ffn_w_std": "w_std", "L0_ffn_w_rec": "w_rec", "L1_attn_Wq": "Wq", "L1_attn_Wk": "Wk", "L1_attn_Wv": "Wv",
    "L1_attn_Wo": "Wo", "L1_attn_betas": "betas", "L1_ffn_ln_gamma": "gamma", "L1_ffn_ln_beta": "beta",
    "L1_ffn_spline_bases": "bases", "L1_ffn_spline_slopes": "slopes", "L1_ffn_output_scale": "oscale",
}


def kernel(**inputs):
    import concourse.bacc as bacc
    from concourse.bass_utils import run_bass_kernel_spmd

    nc = bacc.Bacc("TRN2", target_bir_lowering=False, num_devices=1)
    consts0, cols0 = shape_constants(0)
    consts1, cols1 = shape_constants(1)
    consts2, cols2 = shape_constants(2)
    arrays, A = {}, {}
    for long, short in _INS.items():
        a = np.ascontiguousarray(inputs[long])
        arrays[f"in_{short}"] = a
        A[short] = nc.dram_tensor(f"in_{short}", a.shape, mybir.dt.from_np(a.dtype), kind="ExternalInput").ap()
    for name, a in (("consts0", consts0), ("consts1", consts1), ("consts2", consts2)):
        arrays["in_" + name] = a
        A[name] = nc.dram_tensor("in_" + name, a.shape, F32, kind="ExternalInput").ap()
    out = nc.dram_tensor("out", (B, S, HID), F32, kind="ExternalOutput").ap()
    recurrent_d2_kernel(nc, A, cols0, cols1, cols2, out)
    r = run_bass_kernel_spmd(nc, [arrays], core_ids=[0])
    return r.results[0]["out"]
```

```python
import math
from contextlib import ExitStack

import numpy as np

import concourse.bass as bass
from concourse import mybir

F32 = mybir.dt.float32
BF16 = mybir.dt.bfloat16
ALU = mybir.AluOpType
ACT = mybir.ActivationFunctionType
AXX = mybir.AxisListType.X

P = 128
B, S, HID = 8, 512, 256
NBLK = S // P
KC = HID // P
H, HD = 16, 16
HH = HD // 2
LAT = HID // 8
HALF = 8 * HD
NHALF = H // 8
GH = 4
NG = H // GH
NPART = 3
Q_SLOT = (0, 1, 2, 0, 1, 0)
K_SLOT = (0, 0, 0, 1, 1, 2)
STACK = len(Q_SLOT) * HD
MROWS = GH * NPART
EPS = 1e-5
THRESHOLD = 0.1
BIG = 1.0e30
ATTN, FFN = 0, 1

DK = 128
SEG = 64
NSEG = S // SEG
NTILE, SLICE, GRID, PER_CLUSTER = 64, 4, 16, 8
NCLUSTER = NTILE // PER_CLUSTER


def shape_constants(phase):
    cols = {}
    parts = []

    def put(name, a):
        at = sum(x.shape[1] for x in parts)
        parts.append(a.astype(np.float32))
        cols[name] = (at, at + a.shape[1])

    r = np.arange(P)
    put("ident", np.eye(P))
    if phase == 1:
        seg = r // SEG
        ok = (seg[:, None] == seg[None, :]) & (r[None, :] <= r[:, None])
        put("mask_seg", np.where(ok, 0.0, -BIG))
        return np.concatenate(parts, axis=1), cols
    if phase == 2:
        put("grid", np.tile(np.arange(GRID), (P, SLICE)))
        put("cluster", np.tile(np.arange(NCLUSTER), (P, NBLK)))
        put("in_cluster", np.tile(np.arange(PER_CLUSTER), (P, NBLK * NCLUSTER)))
        return np.concatenate(parts, axis=1), cols
    half = HH // 2
    inv_freq = (1.0 / 10000.0 ** (np.arange(0, HH, 2, dtype=np.float32) / HH)).astype(np.float32)
    angle = (np.arange(S, dtype=np.float32)[:, None] * inv_freq[None, :]).astype(np.float32)
    sin, cos = np.sin(angle).T, np.cos(angle).T
    c, s = np.zeros((HD, S)), np.zeros((HD, S))
    c[:HH] = 1.0
    c[HH:HH + half] = cos
    c[HH + half:] = cos
    s[HH:HH + half] = -sin
    s[HH + half:] = sin
    put("rope_c", np.tile(c, (8, 1)))
    put("rope_s", np.tile(s, (8, 1)))
    put("mask_qk", np.where(r[None, :] > r[:, None], -BIG, 0.0))
    put("mask_kq", np.where(r[None, :] < r[:, None], -BIG, 0.0))
    one = np.zeros((P, GH))
    for h in range(GH):
        one[STACK + h * NPART:STACK + (h + 1) * NPART, h] = 1.0
    put("own_max", one)
    return np.concatenate(parts, axis=1), cols


def meet(eng, turn, n, arrive, seen, leave, mine=()):
    eng.drain().then_inc(arrive, 1)
    eng.wait_ge(arrive, (turn + 1) * n)
    eng.sem_inc(seen, 1)
    for s in mine:
        eng.sem_clear(s)
    eng.sem_inc(leave, 1)
    eng.wait_ge(leave, (turn + 1) * n)
    eng.sem_inc(seen, 1)


def wait_apart(eng, sem, value, seen):
    eng.wait_ge(sem, value)
    eng.sem_inc(seen, 1)


class Scope:

    def __init__(self, nc, ctx):
        self.nc, self.ctx = nc, ctx

    def sb(self, name, shape, dt=F32):
        return self.ctx.enter_context(self.nc.sbuf_tensor(name, shape, dt))

    def sem(self, name):
        return self.ctx.enter_context(self.nc.semaphore(name))


class Chain:

    def __init__(self, eng, sem):
        self.eng, self.sem, self.n = eng, sem, 0

    def __call__(self, ins):
        self.n += 1
        ins.then_inc(self.sem, 1)
        self.eng.wait_ge(self.sem, self.n)


def spread(ap, shape):
    return ap.broadcast_to(shape)


def load_layer0(nc, sc, w, cst, col, A):
    with ExitStack() as ctx:
        t = Scope(nc, ctx)
        wqu = t.sb("wqu", [LAT, P])
        wrq = t.sb("wrq", [LAT, P])
        wku = t.sb("wku", [2 * LAT, P])
        wrk = t.sb("wrk", [P, KC, P])
        wa = t.sb("wa", [P, KC, 768])
        hs = t.sb("head_scales", [P, 8, H])
        hs2 = t.sb("kept_low", [P, H, HH])
        loaded = t.sem("l0_loaded")
        cleared = t.sem("l0_cleared")
        clamped = t.sem("l0_clamped")
        rooted = t.sem("l0_rooted")
        step = t.sem("l0_step")
        N_DMA = 13
        block = ctx.enter_context(nc.Block())

        @block.sync
        def _(sp):
            for dst, src in (
                (cst[:, :], A["consts0"]),
                (w["d"][:, :, 0:LAT], A["w_q_d"].rearrange("(k p) n -> p k n", p=P)),
                (w["d"][:, :, LAT:2 * LAT], A["w_kv_d"].rearrange("(k p) n -> p k n", p=P)),
                (wqu[:, :], A["w_q_u"]),
                (wrq[:, :], A["w_rope_q"]),
                (wku[LAT:2 * LAT, :], A["w_k_u"]),
                (w["v_a"][LAT:2 * LAT, :], A["w_v_u"]),
                (wrk[:, :, :], A["w_rope_k"].rearrange("(k p) n -> p k n", p=P)),
                (wa[:, :, :], A["Wa"].rearrange("(k p) n -> p k n", p=P)),
                (w["o_a"][:, :, :], A["w_o"].rearrange("(k p) n -> p k n", p=P)),
                (w["o_f"][:, :, :], A["Wp"].rearrange("(k p) n -> p k n", p=P)),
                (hs[:, 0, :], A["w_std"].unsqueeze(0).broadcast_to([P, H])),
                (hs[:, 1, :], A["w_rec"].unsqueeze(0).broadcast_to([P, H])),
            ):
                sp.dma_start(dst, src).then_inc(loaded, 16)

        @block.gpsimd
        def _(pool):
            nc.gpsimd.memset(hs[:, 7, :], 0.5).then_inc(cleared, 1)
            pool.wait_ge(cleared, 1)
            pool.wait_ge(clamped, 2)
            nc.gpsimd.tensor_tensor(hs[:, 2, :], hs[:, 2, :], hs[:, 7, :], ALU.pow).then_inc(rooted, 1)
            nc.gpsimd.tensor_tensor(hs[:, 3, :], hs[:, 3, :], hs[:, 7, :], ALU.pow).then_inc(rooted, 1)

        @block.vector
        def _(dve):
            link = Chain(dve, step)
            for name in ("q_a", "q_b", "k_a", "kr_a", "kr_b"):
                nc.vector.memset(w[name][:], 0.0)
            dve.wait_ge(loaded, 16 * N_DMA)
            nc.vector.tensor_scalar(hs[:, 2, :], hs[:, 0, :], 1e-8, None, ALU.max).then_inc(clamped, 1)
            nc.vector.tensor_scalar(hs[:, 3, :], hs[:, 1, :], 1e-8, None, ALU.max).then_inc(clamped, 1)
            link(nc.vector.tensor_copy(w["ident_b"][:, :], cst[:, slice(*col["ident"])]))
            nc.vector.tensor_copy(w["mask_qk"][:, :], cst[:, slice(*col["mask_qk"])])
            nc.vector.tensor_copy(w["mask_kq"][:, :], cst[:, slice(*col["mask_kq"])])

            def heads(ap):
                return ap.rearrange("p (h c) -> p h c", h=H)

            half = HH // 2
            for plain, rope, dst_a, dst_b, lo, hi in (
                (wqu, wrq, w["q_a"], w["q_b"], 0, LAT),
                (wku, None, w["k_a"], None, LAT, 2 * LAT),
            ):
                nc.vector.tensor_copy(heads(dst_a[lo:hi, :])[:, :, 0:HH], heads(plain[lo:hi, :]))
                if rope is not None:
                    nc.vector.tensor_copy(heads(dst_a[lo:hi, :])[:, :, HH:HD], heads(rope[lo:hi, :]))
                    nc.vector.tensor_copy(heads(dst_b[lo:hi, :])[:, :, HH:HH + half], heads(rope[lo:hi, :])[:, :, half:HH])
                    nc.vector.tensor_copy(heads(dst_b[lo:hi, :])[:, :, HH + half:HD], heads(rope[lo:hi, :])[:, :, 0:half])
            for k in range(KC):
                src = heads(wrk[:, k, :])
                nc.vector.tensor_copy(heads(w["kr_a"][:, k, :])[:, :, HH:HD], src)
                nc.vector.tensor_copy(heads(w["kr_b"][:, k, :])[:, :, HH:HH + half], src[:, :, half:HH])
                nc.vector.tensor_copy(heads(w["kr_b"][:, k, :])[:, :, HH + half:HD], src[:, :, 0:half])
                nc.vector.tensor_copy(w["v_f"][:, k, :], wa[:, k, 2 * P:2 * P + HID])
            dve.wait_ge(rooted, 2)
            link(nc.vector.tensor_scalar(hs[:, 4, :], hs[:, 1, :], THRESHOLD, None, ALU.is_gt))
            link(nc.vector.tensor_scalar(hs[:, 5, :], hs[:, 4, :], -1.0, 1.0, ALU.mult, ALU.add))
            link(nc.vector.tensor_tensor(hs[:, 4, :], hs[:, 4, :], hs[:, 3, :], ALU.mult))
            link(nc.vector.tensor_tensor(hs[:, 5, :], hs[:, 5, :], hs[:, 3, :], ALU.mult))
            std, swap, keep = (spread(hs[:, n, :].unsqueeze(2), [P, H, HH]) for n in (2, 4, 5))
            for k in range(KC):
                q_std, k_std, q_low, k_low = (heads(wa[:, k, at:at + P]) for at in (0, P, 2 * P + HID, 3 * P + HID))
                q_out, k_out = heads(w["q_f"][:, k, :]), heads(w["k_f"][:, k, :])
                link(nc.vector.tensor_tensor(q_out[:, :, 0:HH], q_std, std, ALU.mult))
                link(nc.vector.tensor_tensor(k_out[:, :, 0:HH], k_std, std, ALU.mult))
                for out, swapped, kept in ((q_out, k_low, q_low), (k_out, q_low, k_low)):
                    link(nc.vector.tensor_tensor(out[:, :, HH:HD], swapped, swap, ALU.mult))
                    link(nc.vector.tensor_tensor(hs2[:, :, :], kept, keep, ALU.mult))
                    link(nc.vector.tensor_tensor(out[:, :, HH:HD], out[:, :, HH:HD], hs2[:, :, :], ALU.add))


def project_layer0(nc, ps, w, cst, col, A, parts_dram, v_dram):
    with ExitStack() as ctx:
        t = Scope(nc, ctx)
        x = t.sb("p_x", [P, NBLK, HID])
        xn = t.sb("p_xn", [P, NBLK, HID])
        stats = t.sb("p_stats", [P, NBLK, 6])
        mv = t.sb("p_mv", [P, NBLK, 2])
        rstd = t.sb("p_rstd", [P, NBLK])
        power = t.sb("p_power", [P, NBLK])
        xT = t.sb("p_xT", [P, KC, S])
        dT = t.sb("p_dT", [2 * LAT, S])
        rc = t.sb("p_rc", [P, NHALF, S])
        rs = t.sb("p_rs", [P, NHALF, S])
        full = [t.sb(f"p_full{n}", [P, NHALF, S]) for n in range(4)]
        rest = [t.sb(f"p_rest{n}", [P, NHALF, S]) for n in range(4)]
        part = [t.sb(f"p_part{n}", [P, NPART, NHALF, S], BF16) for n in range(4)]
        va = [t.sb(f"p_v{n}", [P, NG, NBLK, GH, HD + 1]) for n in range(2)]

        x_in = t.sem("x_in")
        var_ready, rstd_ready = t.sem("var_ready"), t.sem("rstd_ready")
        xn_ready, xt_psum, xt_ready = t.sem("xn_ready"), t.sem("xt_psum"), t.sem("xt_ready")
        d_psum, d_ready = t.sem("d_psum"), t.sem("d_ready")
        ffn_psum, ffn_full = t.sem("ffn_psum"), t.sem("ffn_full")
        rope_psum, rope_terms, rope_full = t.sem("rope_psum"), t.sem("rope_terms"), t.sem("rope_full")
        v_psum, v_ready = t.sem("v_psum"), t.sem("v_ready")
        hi_ready, rest_ready, mid_ready, lo_ready = (t.sem(f"part_{n}") for n in ("hi", "rest", "mid", "lo"))
        stored = t.sem("parts_stored")
        dve_step, pool_step, preset = t.sem("p_dve_step"), t.sem("p_pool_step"), t.sem("p_preset")
        arrive, seen, leave = t.sem("p_arrive"), t.sem("p_seen"), t.sem("p_leave")
        N_ENG = 5
        N_STORE = 4 * NPART * NHALF + 2
        ORDER = (2, 3, 0, 1)
        block = ctx.enter_context(nc.Block())

        @block.sync
        def _(sp):
            with sp.Fori(0, B) as b:
                sp.dma_start(x[:, :, :], tokens(A["x"], b)).then_inc(x_in, 16)
                for n, tensor in enumerate(ORDER):
                    for m in range(NPART):
                        sp.wait_ge((hi_ready, mid_ready, lo_ready)[m], n + 1)
                        for f in range(NHALF):
                            rows = parts_dram[tensor][m, :, bass.ds(b * H + f * 8, 8), :]
                            sp.dma_start(rows.rearrange("d h n -> h d n"), part[tensor][:, m, f, :]).then_inc(stored, 16)
                for kind in (ATTN, FFN):
                    sp.wait_ge(v_ready, 2 * (kind + 1))
                    sp.dma_start(v_dram[kind][bass.ds(b * NG, NG), :, :].rearrange("g p n -> p g n"),
                                 va[kind][:, :, :, :, :].rearrange("p g k h c -> p g (k h c)")).then_inc(stored, 16)
                sp.wait_ge(stored, 16 * N_STORE)
                meet(sp, b, N_ENG, arrive, seen, leave, (x_in, stored))

        @block.gpsimd
        def _(pool):
            nc.gpsimd.memset(power[:, :], -0.5).then_inc(preset, 1)
            nc.gpsimd.memset(va[0][:], 1.0)
            nc.gpsimd.memset(va[1][:], 1.0).then_inc(preset, 1)
            pool.wait_ge(preset, 2)
            with pool.Fori(0, B) as b:
                pool.wait_ge(var_ready, 1)
                nc.gpsimd.tensor_scalar(rstd[:, :], mv[:, :, 1], EPS, None, ALU.add).then_inc(pool_step, 1)
                pool.wait_ge(pool_step, 1)
                nc.gpsimd.tensor_tensor(rstd[:, :], rstd[:, :], power[:, :], ALU.pow).then_inc(rstd_ready, 1)
                for n, tensor in enumerate(ORDER):
                    if tensor < 2:
                        pool.wait_ge(rope_terms, tensor + 1)
                        nc.gpsimd.tensor_tensor(full[tensor][:, :, :], rc[:, :, :], rs[:, :, :], ALU.add).then_inc(rope_full, 1)
                    pool.wait_ge(hi_ready, n + 1)
                    nc.gpsimd.tensor_tensor(rest[tensor][:, :, :], full[tensor][:, :, :], part[tensor][:, 0, :, :], ALU.subtract).then_inc(rest_ready, 1)
                    pool.wait_ge(mid_ready, n + 1)
                    nc.gpsimd.tensor_tensor(part[tensor][:, 2, :, :], rest[tensor][:, :, :], part[tensor][:, 1, :, :], ALU.subtract).then_inc(lo_ready, 1)
                meet(pool, b, N_ENG, arrive, seen, leave, (rstd_ready, pool_step, rope_full, rest_ready, lo_ready))

        @block.scalar
        def _(act):
            act.wait_ge(preset, 2)
            with act.Fori(0, B) as b:
                act.wait_ge(xt_psum, 1)
                nc.scalar.activation(xT[:, :, :], ps[:, 0:2, :], ACT.Copy).then_inc(xt_ready, 1)
                act.wait_ge(d_psum, 1)
                nc.scalar.activation(dT[:, :], ps[0:2 * LAT, 2, :], ACT.Copy).then_inc(d_ready, 1)
                for n, tensor in enumerate(ORDER):
                    if tensor >= 2:
                        act.wait_ge(ffn_psum, n + 1)
                        at = 4 + 2 * n
                        nc.scalar.activation(full[tensor][:, :, :], ps[:, at:at + 2, :], ACT.Copy).then_inc(ffn_full, 1)
                        act.wait_ge(ffn_full, n + 1)
                    else:
                        act.wait_ge(rope_full, tensor + 1)
                    nc.scalar.activation(part[tensor][:, 0, :, :], full[tensor][:, :, :], ACT.Copy).then_inc(hi_ready, 1)
                    act.wait_ge(rest_ready, n + 1)
                    nc.scalar.activation(part[tensor][:, 1, :, :], rest[tensor][:, :, :], ACT.Copy).then_inc(mid_ready, 1)
                for kind in (ATTN, FFN):
                    for j in range(2):
                        act.wait_ge(v_psum, 2 * kind + j + 1)
                        for i in range(2):
                            k = 2 * j + i
                            last = nc.scalar.activation(
                                va[kind][:, :, k, :, 0:HD],
                                ps[:, 2 * kind + j, i * HID:(i + 1) * HID].rearrange("p (g h c) -> p g h c", g=NG, h=GH), ACT.Copy)
                        last.then_inc(v_ready, 1)
                meet(act, b, N_ENG, arrive, seen, leave, (xt_ready, d_ready, ffn_full, hi_ready, mid_ready, v_ready))

        @block.vector
        def _(dve):
            with dve.Fori(0, B) as b:
                link = Chain(dve, dve_step)
                dve.wait_ge(x_in, 16)
                for k in range(NBLK):
                    last = nc.vector.bn_stats(stats[:, k, :], x[:, k, :])
                link(last)
                for k in range(NBLK):
                    last = nc.vector.bn_aggr(mv[:, k, :], stats[:, k, :])
                last.then_inc(var_ready, 1)
                dve.wait_ge(var_ready, 1)
                dve.wait_ge(rstd_ready, 1)
                for k in range(NBLK):
                    last = nc.vector.tensor_scalar(xn[:, k, :], x[:, k, :], mv[:, k, 0:1], rstd[:, k:k + 1], ALU.subtract, ALU.mult)
                last.then_inc(xn_ready, 1)
                for n in range(2):
                    at = 4 * n
                    dve.wait_ge(rope_psum, n + 1)
                    if n:
                        dve.wait_ge(rope_full, 1)
                    for f in range(NHALF):
                        nc.vector.tensor_tensor(rc[:, f, :], ps[:, at + f, :], cst[:, slice(*col["rope_c"])], ALU.mult)
                        last = nc.vector.tensor_tensor(rs[:, f, :], ps[:, at + 2 + f, :], cst[:, slice(*col["rope_s"])], ALU.mult)
                    last.then_inc(rope_terms, 1)
                meet(dve, b, N_ENG, arrive, seen, leave, (dve_step, var_ready, xn_ready, rope_terms))

        @block.tensor
        def _(pe):
            ident = cst[:, slice(*col["ident"])]

            def product(out, pairs):
                for n, (lhsT, rhs) in enumerate(pairs):
                    last = nc.tensor.matmul(out, lhsT, rhs, start=(n == 0), stop=(n == len(pairs) - 1))
                return last

            with pe.Fori(0, B) as b:
                pe.wait_ge(xn_ready, 1)
                for c in range(KC):
                    for k in range(NBLK):
                        last = nc.tensor.transpose(ps[:, c, k * P:(k + 1) * P], xn[:, k, c * P:(c + 1) * P], ident)
                last.then_inc(xt_psum, 1)
                pe.wait_ge(xt_ready, 1)
                product(ps[0:2 * LAT, 2, :], [(w["d"][:, c, :], xT[:, c, :]) for c in range(KC)]).then_inc(d_psum, 1)
                for n, name in enumerate(("q_f", "k_f")):
                    for f in range(NHALF):
                        last = product(ps[:, 4 + 2 * n + f, :],
                                       [(w[name][:, c, f * P:(f + 1) * P], xT[:, c, :]) for c in range(KC)])
                    last.then_inc(ffn_psum, 1)
                pe.wait_ge(d_ready, 1)
                for f in range(NHALF):
                    cols = slice(f * P, (f + 1) * P)
                    product(ps[:, f, :], [(w["q_a"][:, cols], dT[0:LAT, :])])
                    last = product(ps[:, 2 + f, :], [(w["q_b"][:, cols], dT[0:LAT, :])])
                last.then_inc(rope_psum, 1)
                pe.wait_ge(ffn_full, 2)
                for f in range(NHALF):
                    cols = slice(f * P, (f + 1) * P)
                    rope = [(w["kr_a"][:, c, cols], xT[:, c, :]) for c in range(KC)]
                    product(ps[:, 4 + f, :], [(w["k_a"][LAT:2 * LAT, cols], dT[LAT:2 * LAT, :])] + rope)
                    last = product(ps[:, 6 + f, :], [(w["kr_b"][:, c, cols], xT[:, c, :]) for c in range(KC)])
                last.then_inc(rope_psum, 1)
                pe.wait_ge(rope_terms, 1)
                for kind in (ATTN, FFN):
                    for k in range(NBLK):
                        blk = slice(k * P, (k + 1) * P)
                        if kind == ATTN:
                            pairs = [(dT[LAT:2 * LAT, blk], w["v_a"][LAT:2 * LAT, :])]
                        else:
                            pairs = [(xT[:, c, blk], w["v_f"][:, c, :]) for c in range(KC)]
                        last = product(ps[:, 2 * kind + k // 2, (k % 2) * HID:(k % 2 + 1) * HID], pairs)
                        if k % 2:
                            last.then_inc(v_psum, 1)
                meet(pe, b, N_ENG, arrive, seen, leave, (xt_psum, d_psum, ffn_psum, rope_psum, v_psum))


def attend_layer0(nc, ps, w, cst, col, parts_dram, v_dram, o_dram):
    NSLOT = 8
    TURNS = B * NG * 2 // NSLOT
    N_S = NBLK * GH
    N_E = NBLK * GH // 2
    START = [sum(S - j * P for j in range(k)) for k in range(NBLK + 1)]
    MID = N_E // 2
    TURN_MAX = 4
    S_ORDER = (1, 2, 0, 3)
    E_ORDER = (0, 3, 1, 2)
    QUAD = P // GH
    with ExitStack() as ctx:
        t = Scope(nc, ctx)
        qs = [t.sb(f"a_q{n}", [P, GH, S], BF16) for n in range(NSLOT)]
        ks = [t.sb(f"a_k{n}", [P, GH, S], BF16) for n in range(NSLOT)]
        vs = [t.sb(f"a_v{n}", [P, NBLK, GH, HD + 1]) for n in range(NSLOT)]
        pt = [t.sb(f"a_p{n}", [P, GH, START[NBLK]]) for n in range(2)]
        ot = [t.sb(f"a_o{n}", [P, S]) for n in range(2)]
        negm = t.sb("a_negm", [P, N_S])
        mrest = t.sb("a_mrest", [P, N_S])
        mp = t.sb("a_mp", [P, N_S, NPART], BF16)
        turned = [t.sb(f"a_turned{n}", [P, S], BF16) for n in range(2)]
        loaded = [t.sem(f"a_loaded{n}") for n in range(NSLOT)]
        preset = t.sem("a_preset")
        s_ready, s_taken = t.sem("score_ready"), t.sem("score_taken")
        m_split, mt_ready, m_copied, m_placed = (t.sem("max_" + n) for n in ("split", "turned", "copied", "placed"))
        st_ready, exp_done = t.sem("turned_score_ready"), t.sem("prob_ready")
        pv_ready, o_taken = t.sem("out_ready"), t.sem("out_taken")
        o_stored = [t.sem(f"out_stored{n}") for n in range(2)]
        m_step = t.sem("max_step")
        block = ctx.enter_context(nc.Block())

        def upto(turn, r, per, c):
            return turn * (NSLOT * per) + (r * per + c)

        def placed(turn, r):
            return turn * (NSLOT // 2) + r // 2

        def mt(lo, hi):
            return ps[STACK:STACK + MROWS, 7, lo // 2:hi // 2].bitcast(BF16)

        def units(eng, unit):
            unit(0, 0, 0)
            unit(0, 1, 1)
            with eng.Fori(0, TURNS - 1) as turn:
                for r in range(2, NSLOT + 2):
                    unit(turn, r, None)
            for r in range(2, NSLOT):
                unit(TURNS - 1, r, None)

        def follows(turn, r, n):
            return not (isinstance(turn, int) and turn == TURNS - 1) or r + n < NSLOT

        @block.sync
        def _(sp):
            def load(turn, r):
                at, slot = placed(turn, r), r % NSLOT
                q, k = parts_dram[2 * (r % 2)], parts_dram[2 * (r % 2) + 1]
                heads = bass.ds(at * GH, GH)
                row = 0
                for m in (NPART, NPART - 1, NPART - 2):
                    sp.dma_start(qs[slot][row:row + m * HD, :, :],
                                 q[0:m, :, heads, :].rearrange("a d h n -> (a d) h n")).then_inc(loaded[slot], 16)
                    one = NPART - m
                    sp.dma_start(ks[slot][row:row + m * HD, :, :].rearrange("p h n -> p (h n)"),
                                 k[one:one + 1, :, heads, :].rearrange("a d h n -> a d (h n)").broadcast_to([m, HD, GH * S])).then_inc(loaded[slot], 16)
                    row += m * HD
                sp.dma_start(vs[slot][:, :, :, :].rearrange("p k h c -> p (k h c)"),
                             v_dram[r % 2][bass.ds(at, 1), :, :].rearrange("a p n -> (a p) n")).then_inc(loaded[slot], 16)

            def store(turn, r):
                sp.wait_ge(o_taken, upto(turn, r, 1, 1))
                for h in range(GH):
                    sp.dma_start(o_dram[r % 2][bass.ds(placed(turn, r) * GH + h, 1), :, :].rearrange("a c n -> (a c) n"),
                                 ot[r % 2][h * QUAD:h * QUAD + HD + 1, :]).then_inc(o_stored[r % 2], 16)

            def place_max(turn, r):
                sp.wait_ge(m_copied, upto(turn, r, 1, 1))
                rows = slice(STACK, STACK + MROWS)
                sp.dma_start(qs[r % NSLOT][rows, :, :],
                             turned[r % 2][rows, :].unsqueeze(1).broadcast_to([MROWS, GH, S])).then_inc(m_placed, 16)

            for r in range(NSLOT):
                load(0, r)
            place_max(0, 0)
            place_max(0, 1)
            with sp.Fori(0, TURNS - 1) as turn:
                for r in range(NSLOT):
                    place_max(turn, r + 2)
                    store(turn, r)
                    load(turn, r + NSLOT)
            for r in range(NSLOT):
                if r + 2 < NSLOT:
                    place_max(TURNS - 1, r + 2)
                store(TURNS - 1, r)
            for n in range(2):
                sp.wait_ge(o_stored[n], TURNS * NSLOT // 2 * GH * 16)

        @block.tensor
        def _(pe):
            pe.wait_ge(preset, 2)

            def score(turn, r, c, start=False):
                slot, k, h = r % NSLOT, S_ORDER[c // GH], c % GH
                if c == 0:
                    pe.wait_ge(loaded[slot], (turn + r // NSLOT) * (16 * 7) + 16 * 7)
                if not (start and c < 2):
                    pe.wait_ge(s_taken, upto(turn, r, N_S, c - 1))
                bank = 4 + c % 2
                nc.tensor.matmul(ps[:, bank, 0:(k + 1) * P], qs[slot][0:STACK, h, k * P:(k + 1) * P],
                                 ks[slot][0:STACK, h, 0:(k + 1) * P], start=True, stop=False)
                nc.tensor.matmul(ps[:, bank, k * P:(k + 1) * P], w["ident_b"][:, :], w["mask_qk"][:, :],
                                 start=False, stop=True).then_inc(s_ready, 1)

            def turn_max(turn, r):
                pe.wait_ge(m_split, upto(turn, r, 1, 1))
                for k in range(NBLK):
                    last = nc.tensor.transpose(mt(k * P, (k + 1) * P), mp[:, k * GH:(k + 1) * GH, :].rearrange("p h m -> p (h m)"),
                                               w["ident_b"][:, :])
                last.then_inc(mt_ready, 1)

            def turned_score(turn, r, c, first):
                slot, k, pair = r % NSLOT, E_ORDER[c // 2], c % 2
                if c == 0:
                    pe.wait_ge(m_placed, upto(turn, r, 16, 16))
                if not (first and c < 2):
                    pe.wait_ge(exp_done, upto(turn, r, N_E, c - 1))
                for j in range(2):
                    h, bank = 2 * pair + j, 2 * (c % 2) + j
                    nc.tensor.matmul(ps[:, bank, 0:S - k * P], ks[slot][0:STACK + MROWS, h, k * P:(k + 1) * P],
                                     qs[slot][0:STACK + MROWS, h, k * P:S], start=True, stop=False)
                    last = nc.tensor.matmul(ps[:, bank, 0:P], w["ident_b"][:, :], w["mask_kq"][:, :], start=False, stop=True)
                last.then_inc(st_ready, 1)

            def values(turn, r, part, start=False):
                slot, k = r % NSLOT, part // 2
                if part == 0:
                    pe.wait_ge(exp_done, upto(turn, r, N_E, N_E))
                    if not start:
                        pe.wait_ge(o_taken, upto(turn, r, 1, 0))
                for h in (2 * (part % 2), 2 * (part % 2) + 1):
                    last = nc.tensor.matmul(ps[h * QUAD:h * QUAD + HD + 1, 6, k * P:S], vs[slot][:, k, h, :],
                                            pt[r % 2][:, h, START[k]:START[k + 1]], start=(k == 0), stop=(k == NBLK - 1),
                                            skip_group_check=True)
                if part == 2 * NBLK - 1:
                    last.then_inc(pv_ready, 1)

            def unit(turn, r, first):
                for c in range(N_E):
                    turned_score(turn, r, c, first == 0)
                    for i in range(2):
                        if c < MID and follows(turn, r, 1):
                            score(turn, r + 1, N_S // 2 + 2 * c + i)
                        elif c >= MID and follows(turn, r, 2):
                            score(turn, r + 2, 2 * (c - MID) + i)
                    if first != 0:
                        values(turn, r - 1, c, start=(first == 1))
                    if c == TURN_MAX and follows(turn, r, 1):
                        turn_max(turn, r + 1)

            for c in range(N_S):
                score(0, 0, c, start=True)
            turn_max(0, 0)
            for c in range(N_S // 2):
                score(0, 1, c)
            units(pe, unit)
            for part in range(2 * NBLK):
                values(TURNS - 1, NSLOT - 1, part)

        @block.scalar
        def _(act):
            def copy_max(turn, r):
                act.wait_ge(mt_ready, upto(turn, r, 1, 1))
                nc.scalar.activation(turned[r % 2][STACK:STACK + MROWS, :], mt(0, S), ACT.Copy).then_inc(m_copied, 1)

            def take_out(turn, r, start=False):
                if not start:
                    act.wait_ge(o_stored[r % 2], upto(turn, r - r % 2, GH * 16 // 2, 0))
                act.wait_ge(pv_ready, upto(turn, r, 1, 1))
                nc.scalar.activation(ot[r % 2][:, :], ps[:, 6, :], ACT.Copy).then_inc(o_taken, 1)

            def unit(turn, r, first):
                for c in range(N_E):
                    k, pair = E_ORDER[c // 2], c % 2
                    act.wait_ge(st_ready, upto(turn, r, N_E, c + 1))
                    bank = 2 * (c % 2)
                    nc.scalar.activation(pt[r % 2][:, 2 * pair:2 * pair + 2, START[k]:START[k + 1]],
                                         ps[:, bank:bank + 2, 0:S - k * P], ACT.Exp, scale=float(HD) ** -0.5).then_inc(exp_done, 1)
                    if c == TURN_MAX + 1 and follows(turn, r, 1):
                        copy_max(turn, r + 1)
                if first != 0:
                    take_out(turn, r - 1, start=(first == 1))

            copy_max(0, 0)
            unit(0, 0, 0)
            unit(0, 1, 1)
            unit(0, 2, 2)
            with act.Fori(0, TURNS - 1) as turn:
                for r in range(3, NSLOT + 3):
                    unit(turn, r, None)
            for r in range(3, NSLOT):
                unit(TURNS - 1, r, None)
            take_out(TURNS - 1, NSLOT - 1)

        @block.vector
        def _(dve):
            nc.vector.memset(ps[:, 6, :], 0.0).then_inc(preset, 1)
            for n in range(NSLOT):
                last = nc.vector.tensor_copy(
                    ks[n][STACK:STACK + MROWS, :, :],
                    cst[STACK:STACK + MROWS, slice(*col["own_max"])].unsqueeze(2).broadcast_to([MROWS, GH, S]))
            last.then_inc(preset, 1)

            def maxima(turn, r, first=None):
                for c in range(N_S):
                    k = S_ORDER[c // GH]
                    dve.wait_ge(s_ready, upto(turn, r, N_S, c + 1))
                    nc.vector.tensor_reduce(negm[:, k * GH + c % GH:k * GH + c % GH + 1], ps[:, 4 + c % 2, 0:(k + 1) * P], AXX, ALU.max, negate=True).then_inc(s_taken, 1)
                dve.wait_ge(s_taken, upto(turn, r, N_S, N_S))
                nc.vector.tensor_copy(mp[:, :, 0], negm[:, :]).then_inc(m_step, 1)
                dve.wait_ge(m_step, upto(turn, r, 3, 1))
                nc.vector.tensor_tensor(mrest[:, :], negm[:, :], mp[:, :, 0], ALU.subtract).then_inc(m_step, 1)
                dve.wait_ge(m_step, upto(turn, r, 3, 2))
                nc.vector.tensor_copy(mp[:, :, 1], mrest[:, :]).then_inc(m_step, 1)
                dve.wait_ge(m_step, upto(turn, r, 3, 3))
                nc.vector.tensor_tensor(mp[:, :, 2], mrest[:, :], mp[:, :, 1], ALU.subtract).then_inc(m_split, 1)

            units(dve, maxima)


def tokens(ap, b):
    return ap[bass.ds(b, 1), :, :].rearrange("a (k p) c -> p (a k) c", p=P)


def gate_layer0(nc, ps, w, cst, col, A, o_dram, inv_dram, x1_dram):
    PAR = 2
    N_LOAD = 4 * KC
    with ExitStack() as ctx:
        t = Scope(nc, ctx)
        x, x1 = ([t.sb(f"g_{n}{p}", [P, NBLK, HID]) for p in range(PAR)] for n in ("x", "x1"))
        oT, sums = ([[t.sb(f"g_{n}{p}{kind}", [P, KC, S]) for kind in range(2)] for p in range(PAR)] for n in ("oT", "sum"))
        all_sums = t.sb("g_all_sums", [P, 2, S])
        e, r = (t.sb("g_" + n, [P, 2 * S]) for n in ("e", "r"))
        g = [t.sb(f"g_g{p}", [P, 2 * S]) for p in range(PAR)]
        sums_in, inverted, inverse_out = (t.sem("g_" + n) for n in ("sums_in", "inverted", "inverse_out"))
        loaded, x_in, x1_out = ([t.sem(f"g_{n}{p}") for p in range(PAR)] for n in ("loaded", "x_in", "x1_out"))
        scaled, projected, gated, x1_ready = (t.sem("g_" + n) for n in ("scaled", "projected", "gated", "x1_ready"))
        clipped, exped, one_added, step, seen = (t.sem("g_" + n) for n in ("clipped", "exped", "one_added", "step", "seen"))
        N_STEP = 2
        block = ctx.enter_context(nc.Block())

        def upto(turn, p, per, c):
            return turn * (PAR * per) + (p * per + c)

        def early(turn, p=0):
            return isinstance(turn, int) and turn == 0 and p < PAR

        def ahead(eng, first, step):
            if first:
                first(0, 0)
            for p in range(PAR):
                step(0, p, False)
            with eng.Fori(1, B // PAR - 1) as turn:
                for p in range(PAR):
                    step(turn, p, False)
            for p in range(PAR):
                step(B // PAR - 1, p, p == PAR - 1)

        @block.sync
        def _(sp):
            def load_x(turn, p):
                sp.dma_start(x[p % PAR][:, :, :], tokens(A["x"], turn * PAR + p)).then_inc(x_in[p % PAR], 16)

            def load(turn, p):
                b, q = turn * PAR + p, p % PAR
                for kind in (ATTN, FFN):
                    for c in range(KC):
                        heads = o_dram[kind][bass.ds(b * H + c * (P // HD), P // HD), :, :]
                        sp.dma_start(oT[q][kind][:, c, :], heads[:, 0:HD, :]).then_inc(loaded[q], 16)
                        sp.dma_start(sums[q][kind][:, c, :],
                                     inv_dram[kind][bass.ds(b * H + c * (P // HD), P // HD), :]
                                     .unsqueeze(1).broadcast_to([P // HD, HD, S])).then_inc(loaded[q], 16)

            def store(turn, p):
                sp.wait_ge(x1_ready, upto(turn, p, 1, 1))
                sp.dma_start(tokens(x1_dram, turn * PAR + p), x1[p][:, :, :]).then_inc(x1_out[p], 16)

            for kind in (ATTN, FFN):
                sp.dma_start(all_sums[:, kind, :], o_dram[kind][:, HD:HD + 1, :].rearrange("h a n -> h (a n)")).then_inc(sums_in, 16)
            for kind in (ATTN, FFN):
                sp.wait_ge(inverted, kind + 1)
                sp.dma_start(inv_dram[kind], all_sums[:, kind, :]).then_inc(inverse_out, 16)
            sp.wait_ge(inverse_out, 32)
            for p in range(PAR):
                load(0, p)
                load_x(0, p)
            with sp.Fori(0, B // PAR - 1) as turn:
                for p in range(PAR):
                    sp.wait_ge(projected, upto(turn, p, 2, 2))
                    load(turn, p + PAR)
                    store(turn, p)
                    load_x(turn, p + PAR)
            for p in range(PAR):
                store(B // PAR - 1, p)
                sp.wait_ge(x1_out[p], B // PAR * 16)

        @block.gpsimd
        def _(pool):
            def scale(turn, p):
                wait_apart(pool, loaded[p % PAR], (turn + p // PAR) * (16 * N_LOAD) + 16 * N_LOAD, seen)
                for kind in (ATTN, FFN):
                    nc.gpsimd.tensor_tensor(oT[p % PAR][kind][:, :, :], oT[p % PAR][kind][:, :, :],
                                            sums[p % PAR][kind][:, :, :], ALU.mult).then_inc(scaled, 1)

            def batch(turn, p, last):
                if not last:
                    scale(turn, p + 1)
                if not early(turn):
                    wait_apart(pool, x1_out[p], turn * 16, seen)
                wait_apart(pool, x_in[p], turn * 16 + 16, seen)
                wait_apart(pool, gated, upto(turn, p, 1, 1), seen)
                nc.gpsimd.tensor_tensor(x1[p][:, :, :].rearrange("p k c -> p (k c)"), x[p][:, :, :].rearrange("p k c -> p (k c)"),
                                        g[p][:, :], ALU.add).then_inc(x1_ready, 1)

            ahead(pool, scale, batch)

        @block.tensor
        def _(pe):
            def batch(turn, p, last):
                for kind in (ATTN, FFN):
                    pe.wait_ge(scaled, upto(turn, p, 2, kind + 1))
                    if kind == 0 and not early(turn):
                        pe.wait_ge(x1_ready, upto(turn, p, 1, 1 - PAR))
                    wo = w["o_a"] if kind == ATTN else w["o_f"]
                    for k in range(NBLK):
                        for c in range(KC):
                            last_mm = nc.tensor.matmul(ps[:, 4 * p + 2 * kind + k // 2, (k % 2) * HID:(k % 2 + 1) * HID],
                                                       oT[p][kind][:, c, k * P:(k + 1) * P], wo[:, c, :], start=(c == 0), stop=(c == KC - 1))
                    last_mm.then_inc(projected, 1)

            ahead(pe, None, batch)

        @block.scalar
        def _(act):
            def batch(turn, p, last):
                act.wait_ge(clipped, upto(turn, p, 1, 1))
                nc.scalar.activation(e[:, :], e[:, :], ACT.Exp).then_inc(exped, 1)
                act.wait_ge(exped, upto(turn, p, 1, 1))
                nc.scalar.activation(e[:, :], e[:, :], ACT.Copy, bias=1.0).then_inc(one_added, 1)

            ahead(act, None, batch)

        @block.vector
        def _(dve):
            dve.wait_ge(sums_in, 32)
            for kind in (ATTN, FFN):
                nc.vector.reciprocal(all_sums[:, kind, :], all_sums[:, kind, :]).then_inc(inverted, 1)

            def batch(turn, p, last):
                count = [0]

                def link(ins):
                    count[0] += 1
                    ins.then_inc(step, 1)
                    dve.wait_ge(step, upto(turn, p, N_STEP, count[0]))

                s_ps, y_ps = (ps[:, at:at + 2, :].rearrange("p k n -> p (k n)") for at in (4 * p, 4 * p + 2))
                dve.wait_ge(projected, upto(turn, p, 2, 2))
                nc.vector.tensor_scalar(e[:, :], y_ps, -1.0, 80.0, ALU.mult, ALU.min).then_inc(clipped, 1)
                dve.wait_ge(one_added, upto(turn, p, 1, 1))
                link(nc.vector.reciprocal(r[:, :], e[:, :]))
                if not early(turn):
                    dve.wait_ge(x1_ready, upto(turn, p, 1, 1 - PAR))
                link(nc.vector.tensor_tensor(g[p][:, :], y_ps, r[:, :], ALU.mult))
                nc.vector.tensor_tensor(g[p][:, :], s_ps, g[p][:, :], ALU.mult).then_inc(gated, 1)

            ahead(dve, None, batch)


def recur_layer1(nc, ps, col, A, x1_dram, s1_dram):
    NGRP = 4
    NPAIR = NSEG // 2
    WB = DK + 1
    with ExitStack() as ctx:
        t = Scope(nc, ctx)
        cst = t.sb("cst1", [P, A["consts1"].shape[1]])
        wq, wk, wv = (t.sb("m_" + n, [P, KC, NGRP * GH * DK]) for n in ("wq", "wk", "wv"))
        NJ = NGRP * GH
        wo = t.sb("m_wo", [P, NJ, HID])
        share = t.sb("m_share", [P, 2, NGRP * GH])
        se = t.sb("m_se", [P, NGRP * GH])
        ident_b = t.sb("m_ident_b", [P, P], BF16)
        mask_b = t.sb("m_mask_b", [P, P], BF16)
        xs = t.sb("m_xs", [P, NBLK, HID])
        stats = t.sb("m_stats", [P, NBLK, 6])
        mv = t.sb("m_mv", [P, NBLK, 2])
        rstd = t.sb("m_rstd", [P, NBLK])
        power = t.sb("m_power", [P, NBLK])
        xT = t.sb("m_xT", [P, KC, S])
        qT = t.sb("m_qT", [P, S])
        kT = t.sb("m_kT", [P, S])
        eq, ek = t.sb("m_eq", [P, S]), t.sb("m_ek", [P, S])
        sk = t.sb("m_sk", [P, S])
        sg = [[t.sb(f"m_sg{g}{h}", [P, NPAIR, 4, SEG]) for h in range(GH)] for g in range(2)]
        kn = [t.sb(f"m_kn{g}", [P, GH, NPAIR, DK]) for g in range(2)]
        v = [t.sb(f"m_v{g}", [P, NPAIR, GH, DK]) for g in range(2)]
        am = [t.sb(f"m_am{g}", [P, NPAIR, GH, DK]) for g in range(2)]
        at = [t.sb(f"m_at{g}", [P, GH, S]) for g in range(NGRP)]
        pr = t.sb("m_pr", [P, NPAIR, P])
        prT = t.sb("m_prT", [P, S])
        negm, psum_, prec = t.sb("m_negm", [P, NPAIR]), t.sb("m_psum", [P, NPAIR]), t.sb("m_prec", [P, NPAIR])
        mem = t.sb("m_mem", [P, GH, WB])
        rd = t.sb("m_rd", [P, GH])
        tmp = t.sb("m_tmp", [P, GH, DK])
        delta = t.sb("m_delta", [P, GH, WB])
        acc = t.sb("m_acc", [P, HID])

        w_in, preset, share_step = t.sem("w_in"), t.sem("m_preset"), t.sem("share_step")
        share_clip, share_exp, share_ready = t.sem("share_clip"), t.sem("share_exp"), t.sem("share_ready")
        stat_ready, apart, power_set = t.sem("m_stat_ready"), t.sem("m_apart"), t.sem("m_power_set")
        x_in, var_ready, eps_added, rstd_ready, xn_ready, xt_psum, xt_ready = (
            t.sem("m_" + n) for n in ("x_in", "var_ready", "eps_added", "rstd_ready", "xn_ready", "xt_psum", "xt_ready"))
        proj_ready, qk_ready, min_ready, exp_ready, sigq_ready, sigk_ready, sigk_placed = (
            t.sem(n) for n in ("proj_ready", "qk_ready", "min_ready", "exp_ready", "sigma_q_ready", "sigma_k_ready", "sigma_k_placed"))
        v_psum, v_ready, kn_psum, kn_ready = (t.sem(n) for n in ("v_psum1", "v_ready1", "kn_psum", "kn_ready"))
        sc_ready, max_raw, max_ready, p_ready, rs_ready, pn_ready = (
            t.sem(n) for n in ("sc_ready", "max_raw", "max_ready", "p_ready", "rs_ready", "pn_ready"))
        pt_psum, pt_ready, bt_psum, bt_ready = (t.sem(n) for n in ("pt_psum", "pt_ready", "bt_psum", "bt_ready"))
        d_ready, rd_ready, tmp_ready, delta_ready, read_done, u_ready, mem_ready = (
            t.sem(n) for n in ("d_ready", "rd_ready", "tmp_ready", "delta_ready", "read_done", "u_ready", "mem_ready"))
        am_psum, at_ready, out_psum, acc_ready, stored = (
            t.sem(n) for n in ("am_psum", "at_ready", "out_psum1", "acc_ready", "s_stored"))
        N_W = 6
        NUPD = NSEG - 1
        block = ctx.enter_context(nc.Block())

        class Group:

            def __init__(self, b, g):
                self.b, self.g = b + g // NGRP, g % NGRP
                self.par = g % 2
                self._b, self._g = b, g

            def upto(self, per, c):
                return self._b * (NGRP * per) + (self._g * per + c)

            def head(self, h):
                return self.g * GH + h

            @property
            def first(self):
                return isinstance(self._b, int) and self._b == 0 and self._g == 0

        def khalf(s):
            return slice(SEG * (s % 2), SEG * (s % 2) + SEG)

        def qhalf(s):
            return khalf(s + 1)

        def region(lo, hi, part=slice(0, P)):
            return ps[part, 0:2, :].rearrange("p b (h c) -> p (b h) c", h=2)[:, :, lo:hi]

        def windows(turn, last):
            for g in range(NGRP):
                n = Group(turn, g)
                yield n, (None if last and g == NGRP - 1 else Group(turn, g + 1)), (Group(turn, g - 1) if g else None)

        def run(eng, prologue, window):
            prologue()
            window(None, Group(0, 0), None)
            with eng.Fori(0, B - 1) as turn:
                for n, m, o in windows(turn, False):
                    window(n, m, o)
            for n, m, o in windows(B - 1, True):
                window(n, m, o)

        @block.sync
        def _(sp):
            sp.dma_start(cst[:, :], A["consts1"]).then_inc(w_in, 16)
            for dst, src in ((wq, A["Wq"]), (wk, A["Wk"]), (wv, A["Wv"])):
                sp.dma_start(dst[:, :, :], src.rearrange("(k p) n -> p k n", p=P)).then_inc(w_in, 16)
            sp.dma_start(wo[:, :, :], A["Wo"].rearrange("(h p) n -> p h n", p=P)).then_inc(w_in, 16)
            with nc.allow_non_contiguous_dma(reason="2048 words, once"):
                sp.dma_start(share[:, 0, :], A["betas"].rearrange("a h b p -> p (a h b)")).then_inc(w_in, 16)
            sp.dma_start(xs[:, :, :], tokens(x1_dram, 0)).then_inc(x_in, 16)
            sp.sem_inc(stored, 16)
            def store(b, g):
                sp.wait_ge(acc_ready, b * NGRP + (g + 1))
                rows = s1_dram[bass.ds(b, 1), :, :].rearrange("a (s g h r) c -> g h (a s) r c", s=NSEG, g=NGRP, h=GH)
                for h in range(GH):
                    sp.dma_start(rows[g, h], acc[h * NSEG * 4:(h + 1) * NSEG * 4, :]).then_inc(stored, 16)

            with sp.Fori(0, B - 1) as b:
                sp.wait_ge(xt_psum, b + 1)
                sp.dma_start(xs[:, :, :], tokens(x1_dram, b + 1)).then_inc(x_in, 16)
                for g in range(NGRP):
                    store(b, g)
            for g in range(NGRP):
                store(B - 1, g)
            sp.wait_ge(stored, 16 * (1 + B * NGRP * GH))

        @block.gpsimd
        def _(pool):
            nc.gpsimd.memset(power[:, :], -0.5).then_inc(power_set, 1)
            pool.wait_ge(power_set, 1)

            def inv_std(b):
                wait_apart(pool, var_ready, b + 1, apart)
                nc.gpsimd.tensor_scalar(rstd[:, :], mv[:, :, 1], EPS, None, ALU.add).then_inc(eps_added, 1)
                pool.wait_ge(eps_added, b + 1)
                nc.gpsimd.tensor_tensor(rstd[:, :], rstd[:, :], power[:, :], ALU.pow).then_inc(rstd_ready, 1)

            def place_keys(m, h):
                wait_apart(pool, sigk_ready, m.upto(GH, h + 1), apart)
                nc.gpsimd.tensor_copy(sg[m.par][h][:, :, 0:4:3, :], sk[:, :].rearrange("p (a b c) -> p a b c", a=NPAIR, b=2)).then_inc(sigk_placed, 1)

            def normalise(m, h):
                pool.wait_ge(rs_ready, m.upto(GH, h + 1))
                p = pr
                nc.gpsimd.tensor_tensor(p[:, :, :], p[:, :, :], prec[:, :].unsqueeze(2).broadcast_to([P, NPAIR, P]), ALU.mult).then_inc(pn_ready, 1)

            def window(n, m, o):
                if n is not None:
                    normalise(n, GH - 1)
                if m is not None:
                    for h in range(GH):
                        place_keys(m, h)
                        if h < GH - 1:
                            normalise(m, h)
                if n is not None and n.g == 1 and not (isinstance(n.b, int) and n.b == B - 1):
                    inv_std(n.b + 1)

            run(pool, lambda: inv_std(0), window)

        @block.tensor
        def _(pe):
            ident = cst[:, slice(*col["ident"])]

            def product(out, pairs):
                for i, (lhsT, rhs) in enumerate(pairs):
                    last = nc.tensor.matmul(out, lhsT, rhs, start=(i == 0), stop=(i == len(pairs) - 1))
                return last

            def turn_x(b, first=False):
                pe.wait_ge(xn_ready, b + 1)
                if not first:
                    pe.wait_ge(qk_ready, (b * NGRP) * (2 * GH))
                for c in range(KC):
                    for k in range(NBLK):
                        last = nc.tensor.transpose(ps[:, 2 + c, k * P:(k + 1) * P], xs[:, k, c * P:(c + 1) * P], ident)
                last.then_inc(xt_psum, 1)

            def project(m, h):
                if h == 0:
                    pe.wait_ge(xt_ready, m.b + 1)
                if not (m.first and h == 0):
                    pe.wait_ge(qk_ready, m.upto(2 * GH, 2 * h))
                cols = slice(m.head(h) * DK, (m.head(h) + 1) * DK)
                for bank, weights in ((2, wq), (3, wk)):
                    product(ps[:, bank, :], [(weights[:, c, cols], xT[:, c, :]) for c in range(KC)]).then_inc(proj_ready, 1)

            def project_v(m, k, bank):
                product(ps[:, bank, :], [(xT[:, c, k * P:(k + 1) * P], wv[:, c, m.g * GH * DK:(m.g + 1) * GH * DK])
                                         for c in range(KC)]).then_inc(v_psum, 1)

            def turn_keys(m, h):
                pe.wait_ge(sigk_ready, m.upto(GH, h + 1))
                pe.wait_ge(v_ready, m.upto(NBLK, 2 if h == 0 else NBLK))
                if h:
                    pe.wait_ge(kn_ready, m.upto(GH, h))
                for p in range(NPAIR):
                    blk = slice(p * P, (p + 1) * P)
                    last = nc.tensor.transpose(ps[:, 5, blk], sk[:, blk], ident)
                last.then_inc(kn_psum, 1)

            def score(m, h):
                pe.wait_ge(qk_ready, m.upto(2 * GH, 2 * h + 2))
                if not (m.first and h == 0):
                    pe.wait_ge(p_ready, m.upto(GH, h))
                nc.tensor.matmul(ps[:, 6, :].rearrange("p (a c) -> p a c", a=NPAIR), ident_b[:, :],
                                 mask_b[:, :].unsqueeze(1).broadcast_to([P, NPAIR, P]), start=True, stop=False, skip_group_check=True)
                for p in range(NPAIR):
                    blk = slice(p * P, (p + 1) * P)
                    last = nc.tensor.matmul(ps[:, 6, blk], qT[:, blk], kT[:, blk],
                                            start=False, stop=(p == NPAIR - 1), skip_group_check=True)
                last.then_inc(sc_ready, 1)

            def turn_probs(m, h):
                pe.wait_ge(pn_ready, m.upto(GH, h + 1))
                if not (m.first and h == 0):
                    pe.wait_ge(bt_ready, m.upto(GH, h))
                for p in range(NPAIR):
                    last = nc.tensor.transpose(ps[:, 7, p * P:(p + 1) * P], pr[:, p, :], ident)
                last.then_inc(pt_psum, 1)

            def local(m, h):
                pe.wait_ge(pt_ready, m.upto(GH, h + 1))
                pe.wait_ge(v_ready, m.upto(NBLK, NBLK))
                for p in range(NPAIR):
                    blk = slice(p * P, (p + 1) * P)
                    last = nc.tensor.matmul(ps[:, 7, blk], v[m.par][:, p, h, :], prT[:, blk], start=True, stop=True)
                last.then_inc(bt_psum, 1)

            def read_memory(n, s):
                if s == 0:
                    pe.wait_ge(sigq_ready, n.upto(GH, GH))
                    pe.wait_ge(sigk_placed, n.upto(GH, GH))
                pe.wait_ge(mem_ready, n.upto(NSEG, s + 1))
                for h in range(GH):
                    last = nc.tensor.matmul(region(0, WB)[:, h, :], sg[n.par][h][:, s // 2, 2 * (s % 2):2 * (s % 2) + 2, :].rearrange("p a c -> p (a c)"),
                                            mem[:, h, :], start=True, stop=True)
                last.then_inc(d_ready, 1)

            def write_memory(n, s):
                if s == 0:
                    pe.wait_ge(kn_ready, n.upto(GH, GH))
                pe.wait_ge(delta_ready, n.upto(NUPD, s + 1))
                pe.wait_ge(read_done, n.upto(NSEG, s + 1))
                half = khalf(s)
                for h in range(GH):
                    last = nc.tensor.matmul(region(0, WB)[:, h, :], kn[n.par][half, h, s // 2, :], delta[half, h, :], start=True, stop=True)
                last.then_inc(u_ready, 1)

            def turn_read(o, h, bank):
                pe.wait_ge(read_done, o.upto(NSEG, NSEG))
                for p in range(NPAIR):
                    last = nc.tensor.transpose(ps[:, bank, p * P:(p + 1) * P], am[o.par][:, p, h, :], ident)
                last.then_inc(am_psum, 1)

            def emit(o, j):
                if j == 0:
                    pe.wait_ge(at_ready, o.upto(GH, GH))
                heads = at[o.g][:, :, :].rearrange("p h (r j) -> p (h r) j", j=NJ)
                for i in range(j * NJ // 2, (j + 1) * NJ // 2):
                    last = nc.tensor.matmul(ps[:, 4, 0:HID], heads[:, :, i], wo[:, i, :], start=(i == 0), stop=(i == NJ - 1))
                if j:
                    last.then_inc(out_psum, 1)

            def window(n, m, o):
                for s in range(NSEG):
                    if n is not None:
                        read_memory(n, s)
                    if m is not None:
                        if s % 2 == 0:
                            project(m, s // 2)
                        elif s < 4:
                            if o is not None or (s == 1 and n is not None and not n.first):
                                if s == 1:
                                    if o is not None:
                                        pe.wait_ge(at_ready, o.upto(GH, 2))
                                    else:
                                        pe.wait_ge(acc_ready, n.upto(1, 0))
                                else:
                                    pe.wait_ge(at_ready, o.upto(GH, GH))
                            if s == 3:
                                pe.wait_ge(kn_ready, m.upto(GH, 1))
                                pe.wait_ge(v_ready, m.upto(NBLK, 2))
                            project_v(m, s - 1, 4)
                            project_v(m, s, 5)
                    if o is not None and s in (5, 7):
                        if s == 5 and m is not None:
                            pe.wait_ge(v_ready, m.upto(NBLK, NBLK))
                        emit(o, (s - 5) // 2)
                    if n is not None and s < NUPD:
                        write_memory(n, s)
                    if n is not None and s == 0:
                        turn_probs(n, GH - 1)
                    if n is not None and s == 1:
                        local(n, GH - 1)
                    if m is not None and s % 2 == 0 and s:
                        turn_probs(m, s // 2 - 1)
                    if m is not None and s % 2:
                        score(m, s // 2)
                        if s > 1:
                            local(m, s // 2 - 1)
                        turn_keys(m, s // 2)
                    if o is not None and s in (0, 2):
                        if s == 0:
                            if n is not None:
                                pe.wait_ge(kn_ready, n.upto(GH, GH))
                            if o.g:
                                pe.wait_ge(acc_ready, o.upto(1, 0))
                        else:
                            if m is not None:
                                pe.wait_ge(v_ready, m.upto(NBLK, 2))
                                pe.wait_ge(kn_ready, m.upto(GH, 1))
                            else:
                                pe.wait_ge(at_ready, o.upto(GH, 2))
                        turn_read(o, s, 5)
                        turn_read(o, s + 1, 4)
                if n is not None and n.g == 2 and m is not None and not (isinstance(n.b, int) and n.b == B - 1):
                    turn_x(n.b + 1)
                if n is not None and n.g == NGRP - 1:
                    if m is not None:
                        pe.wait_ge(kn_ready, m.upto(GH, GH))
                    pe.wait_ge(acc_ready, n.upto(1, 0))
                    turn_read(n, 0, 5)
                    turn_read(n, 1, 4)
                    pe.wait_ge(at_ready, n.upto(GH, 2))
                    turn_read(n, 2, 5)
                    turn_read(n, 3, 4)
                    emit(n, 0)
                    emit(n, 1)

            def prologue():
                pe.wait_ge(preset, 2)
                pe.wait_ge(w_in, 16 * N_W)
                turn_x(0, first=True)

            run(pe, prologue, window)

        @block.scalar
        def _(act):
            def take_x(b):
                act.wait_ge(xt_psum, b + 1)
                nc.scalar.activation(xT[:, :, :], ps[:, 2:4, :], ACT.Copy).then_inc(xt_ready, 1)

            def take_qk(m, h):
                for i, dst in enumerate((qT, kT)):
                    act.wait_ge(proj_ready, m.upto(2 * GH, 2 * h + i + 1))
                    nc.scalar.activation(dst[:, :], ps[:, 2 + i, :], ACT.Copy).then_inc(qk_ready, 1)
                for i, e in enumerate((eq, ek)):
                    act.wait_ge(min_ready, m.upto(2 * GH, 2 * h + i + 1))
                    nc.scalar.activation(e[:, :], e[:, :], ACT.Exp).then_inc(exp_ready, 1)

            def take_v(m, k, bank):
                act.wait_ge(v_psum, m.upto(NBLK, k + 1))
                nc.scalar.activation(v[m.par][:, k, :, :].rearrange("p h c -> p (h c)"), ps[:, bank, :], ACT.Copy).then_inc(v_ready, 1)

            def take_keys(m, h):
                act.wait_ge(kn_psum, m.upto(GH, h + 1))
                nc.scalar.activation(kn[m.par][:, h, :, :].rearrange("p a c -> p (a c)"), ps[:, 5, :], ACT.Copy).then_inc(kn_ready, 1)

            def probabilities(m, h):
                act.wait_ge(max_ready, m.upto(GH, h + 1))
                for p in range(NPAIR):
                    last = nc.scalar.activation(pr[:, p, :], ps[:, 6, p * P:(p + 1) * P], ACT.Exp,
                                                bias=negm[:, p:p + 1], scale=float(DK) ** -0.5, accum_out=psum_[:, p:p + 1])
                last.then_inc(p_ready, 1)

            def take_turned_probs(m, h):
                act.wait_ge(pt_psum, m.upto(GH, h + 1))
                nc.scalar.activation(prT[:, :], ps[:, 7, :], ACT.Copy).then_inc(pt_ready, 1)

            def take_local(m, h):
                act.wait_ge(bt_psum, m.upto(GH, h + 1))
                nc.scalar.activation(at[m.g][:, h, :], ps[:, 7, :], ACT.Copy, scale=share[:, 1, m.head(h):m.head(h) + 1]).then_inc(bt_ready, 1)

            def take_read(n, s):
                act.wait_ge(rd_ready, n.upto(NSEG, s + 1))
                half = qhalf(s)
                for h in range(GH):
                    last = nc.scalar.activation(am[n.par][half, s // 2, h, :], region(0, DK, half)[:, h, :], ACT.Copy, scale=rd[half, h:h + 1])
                last.then_inc(read_done, 1)

            def take_out(o):
                act.wait_ge(out_psum, o.upto(1, 1))
                act.wait_ge(stored, o.upto(16 * GH, 16))
                nc.scalar.activation(acc[:, :], ps[:, 4, 0:HID], ACT.Copy).then_inc(acc_ready, 1)

            def window(n, m, o):
                for s in range(NSEG):
                    if n is not None:
                        take_read(n, s)
                    if m is not None:
                        if s % 2 == 0:
                            take_qk(m, s // 2)
                        elif s < 4:
                            take_v(m, s - 1, 4)
                            take_v(m, s, 5)
                    if n is not None and s == 0:
                        take_turned_probs(n, GH - 1)
                    if n is not None and s == 1:
                        take_local(n, GH - 1)
                    if m is not None and s % 2 == 0 and s:
                        take_turned_probs(m, s // 2 - 1)
                    if m is not None and s % 2:
                        probabilities(m, s // 2)
                        if s > 1:
                            take_local(m, s // 2 - 1)
                        take_keys(m, s // 2)
                    if o is not None and s == 7:
                        take_out(o)
                if n is not None and n.g == 2 and m is not None and not (isinstance(n.b, int) and n.b == B - 1):
                    take_x(n.b + 1)
                if n is not None and n.g == NGRP - 1:
                    take_out(n)

            def prologue():
                act.wait_ge(share_clip, 1)
                nc.scalar.activation(se[:, :], se[:, :], ACT.Exp).then_inc(share_exp, 1)
                act.wait_ge(share_ready, 1)
                take_x(0)

            run(act, prologue, window)

        @block.vector
        def _(dve):
            def normalise_x(b):
                dve.wait_ge(rstd_ready, b + 1)
                for k in range(NBLK):
                    last = nc.vector.tensor_scalar(xs[:, k, :], xs[:, k, :], mv[:, k, 0:1], rstd[:, k:k + 1], ALU.subtract, ALU.mult)
                last.then_inc(xn_ready, 1)

            def stats_x(b):
                dve.wait_ge(x_in, b * 16 + 16)
                for k in range(NBLK):
                    last = nc.vector.bn_stats(stats[:, k, :], xs[:, k, :])
                last.then_inc(stat_ready, 1)
                wait_apart(dve, stat_ready, b + 1, apart)
                for k in range(NBLK):
                    last = nc.vector.bn_aggr(mv[:, k, :], stats[:, k, :])
                last.then_inc(var_ready, 1)
                dve.wait_ge(var_ready, b + 1)

            def pairs(x):
                return x[:, :].rearrange("p (a c) -> p a c", a=NPAIR)

            def sigma(m, h):
                for i, (x, e) in enumerate(((qT, eq), (kT, ek))):
                    dve.wait_ge(qk_ready, m.upto(2 * GH, 2 * h + i + 1))
                    nc.vector.tensor_scalar(e[:, :], x[:, :], 0.0, None, ALU.min).then_inc(min_ready, 1)
                dve.wait_ge(exp_ready, m.upto(2 * GH, 2 * h + 1))
                nc.vector.scalar_tensor_tensor(sg[m.par][h][:, :, 1:3, :].rearrange("p a b c -> p a (b c)"), pairs(qT), 1.0,
                                               pairs(eq), ALU.add, ALU.max).then_inc(sigq_ready, 1)
                dve.wait_ge(exp_ready, m.upto(2 * GH, 2 * h + 2))
                if not (m.first and h == 0):
                    dve.wait_ge(sigk_placed, m.upto(GH, h))
                nc.vector.scalar_tensor_tensor(sk[:, :], kT[:, :], 1.0, ek[:, :], ALU.add, ALU.max).then_inc(sigk_ready, 1)

            def maximum(m, h):
                dve.wait_ge(sc_ready, m.upto(GH, h + 1))
                nc.vector.tensor_reduce(negm[:, :], ps[:, 6, :].rearrange("p (a c) -> p a c", a=NPAIR), AXX, ALU.max, negate=True).then_inc(max_raw, 1)
                dve.wait_ge(max_raw, m.upto(GH, h + 1))
                nc.vector.tensor_scalar(negm[:, :], negm[:, :], float(DK) ** -0.5, None, ALU.mult).then_inc(max_ready, 1)

            def inv_sum(m, h):
                dve.wait_ge(p_ready, m.upto(GH, h + 1))
                nc.vector.reciprocal(prec[:, :], psum_[:, :]).then_inc(rs_ready, 1)

            def reset_memory(n):
                if not n.first:
                    dve.wait_ge(read_done, n.upto(NSEG, 0))
                nc.vector.memset(mem[:, :, 0:DK], 0.0)
                nc.vector.memset(mem[:, :, DK:WB], 1.0 / DK).then_inc(mem_ready, 1)

            def change(n, s):
                dve.wait_ge(d_ready, n.upto(NSEG, s + 1))
                nc.vector.reciprocal(rd[:, :], region(DK, WB)[:, :, 0]).then_inc(rd_ready, 1)
                if s == NUPD:
                    return
                half = khalf(s)
                dve.wait_ge(rd_ready, n.upto(NSEG, s + 1))
                nc.vector.tensor_tensor(tmp[half, :, :], region(0, DK, half), rd[half, :].unsqueeze(2).broadcast_to([SEG, GH, DK]), ALU.mult).then_inc(tmp_ready, 1)
                if s == 0:
                    dve.wait_ge(v_ready, n.upto(NBLK, NBLK))
                dve.wait_ge(tmp_ready, n.upto(NUPD, s + 1))
                nc.vector.tensor_tensor(delta[half, :, 0:DK], v[n.par][half, s // 2, :, :], tmp[half, :, :], ALU.subtract).then_inc(delta_ready, 1)

            def update(n, s):
                dve.wait_ge(u_ready, n.upto(NUPD, s + 1))
                dve.wait_ge(mem_ready, n.upto(NSEG, s + 1))
                nc.vector.tensor_tensor(mem[:, :, :], region(0, WB), mem[:, :, :], ALU.add).then_inc(mem_ready, 1)

            def add_read(o, h, bank):
                dve.wait_ge(am_psum, o.upto(GH, h + 1))
                dve.wait_ge(bt_ready, o.upto(GH, h + 1))
                read = ps[:, bank, :].rearrange("p (a b c) -> p a b c", a=NPAIR, b=2)
                sum_ = at[o.g][:, h, :].rearrange("p (a b c) -> p a b c", a=NPAIR, b=2)
                for i in range(2):
                    last = nc.vector.scalar_tensor_tensor(sum_[:, :, i, :], read[:, :, 1 - i, :], share[:, 0, o.head(h):o.head(h) + 1],
                                                          sum_[:, :, i, :], ALU.mult, ALU.add)
                last.then_inc(at_ready, 1)

            def window(n, m, o):
                for s in range(NSEG):
                    if n is not None:
                        change(n, s)
                        if s == 0:
                            inv_sum(n, GH - 1)
                    if m is not None and s % 2 == 0 and s:
                        inv_sum(m, s // 2 - 1)
                    if n is not None and s < NUPD:
                        update(n, s)
                    if m is not None:
                        if s % 2 == 0:
                            sigma(m, s // 2)
                        else:
                            maximum(m, s // 2)
                    if o is not None and s in (0, 2):
                        add_read(o, s, 5)
                        add_read(o, s + 1, 4)
                    if n is not None and n.g in (1, 2) and m is not None and s == 4 and not (isinstance(n.b, int) and n.b == B - 1):
                        if n.g == 1:
                            stats_x(n.b + 1)
                        else:
                            normalise_x(n.b + 1)
                if m is not None:
                    reset_memory(m)
                if n is not None and n.g == NGRP - 1:
                    for h in range(GH):
                        add_read(n, h, 5 - h % 2)

            def prologue():
                link = Chain(dve, share_step)
                nc.vector.memset(delta[:, :, DK:WB], 1.0).then_inc(preset, 1)
                dve.wait_ge(w_in, 16 * N_W)
                nc.vector.tensor_copy(ident_b[:, :], cst[:, slice(*col["ident"])])
                nc.vector.tensor_copy(mask_b[:, :], cst[:, slice(*col["mask_seg"])]).then_inc(preset, 1)
                nc.vector.tensor_scalar(se[:, :], share[:, 0, :], -1.0, 80.0, ALU.mult, ALU.min).then_inc(share_clip, 1)
                dve.wait_ge(share_exp, 1)
                link(nc.vector.tensor_scalar(se[:, :], se[:, :], 1.0, None, ALU.add))
                link(nc.vector.reciprocal(share[:, 0, :], se[:, :]))
                nc.vector.tensor_scalar(share[:, 1, :], share[:, 0, :], -1.0, 1.0, ALU.mult, ALU.add).then_inc(share_ready, 1)
                stats_x(0)
                normalise_x(0)

            run(dve, prologue, window)

def mix_layer1(nc, ps, col, A, x1_dram, s1_dram, out):
    NT = NBLK * NTILE
    TAB = 2 * SLICE * GRID + 3
    U_MAX = float(np.float32(1.0 - 1e-6))
    with ExitStack() as ctx:
        t = Scope(nc, ctx)
        cst = t.sb("cst2", [P, A["consts2"].shape[1]])
        xs, xn, xf, sg, w1, w2 = (t.sb("f_" + n, [P, NBLK, HID]) for n in ("xs", "xn", "xf", "sg", "w1", "w2"))
        s1 = t.sb("f_s1", [P, NBLK, HID])
        xn_all = t.sb("f_xn_all", [P, B, NBLK * HID])
        hot_all = t.sb("f_hot_all", [P, B, NT])
        hotT_all = t.sb("f_hotT_all", [NTILE, B, S])
        sl_all = t.sb("f_sl_all", [P, B, NBLK * SLICE])
        slopes = t.sb("f_slopes", [P, NTILE * SLICE, GRID])
        want = t.sb("f_want", [P, NTILE * SLICE])
        gamma, beta = t.sb("f_gamma", [P, HID]), t.sb("f_beta", [P, HID])
        table = t.sb("f_table", [NTILE, TAB])
        stats, mv = t.sb("f_stats", [P, NBLK, 6]), t.sb("f_mv", [P, NBLK, 2])
        rstd, power = t.sb("f_rstd", [P, NBLK]), t.sb("f_power", [P, NBLK])
        ts, hot, pen, lo, hi = (t.sb("f_" + n, [P, NT]) for n in ("ts", "hot", "pen", "lo", "hi"))
        cs, ch = t.sb("f_cs", [P, NBLK * NCLUSTER]), t.sb("f_ch", [P, NBLK * NCLUSTER])
        top = t.sb("f_top", [P, NBLK])
        ends = t.sb("f_ends", [P, 2, NBLK])
        least, most = t.sb("f_least", [P, NT]), t.sb("f_most", [P, NT])
        ends64 = t.sb("f_ends64", [P, 2, NTILE])
        hotT = t.sb("f_hotT", [NTILE, S])
        sl, dl = t.sb("f_sl", [P, NBLK * SLICE]), t.sb("f_dl", [P, NBLK * SLICE])
        tab = t.sb("f_tab", [P, NBLK, 3])
        rng = t.sb("f_rng", [P, NBLK])
        d, ge, in_, val = (t.sb("f_" + n, [P, NBLK * SLICE, GRID]) for n in ("d", "ge", "in", "val"))

        w_in, preset, want_sum, want_ready = t.sem("f_w_in"), t.sem("f_preset"), t.sem("f_want_sum"), t.sem("f_want_ready")
        x_in, var_ready, eps_added, rstd_ready = (t.sem("f_" + n) for n in ("x_in", "var_ready", "eps_added", "rstd_ready"))
        xf_ready, sign_ready, hot_ready, hot_psum, hot_turned = (t.sem("f_" + n) for n in ("xf_ready", "sign_ready", "hot_ready", "hot_psum", "hot_turned"))
        step, pstep = t.sem("f_step"), t.sem("f_pstep")
        arrive, seen, leave = t.sem("f_arrive"), t.sem("f_seen"), t.sem("f_leave")
        N_ENG = 5
        first = ExitStack()
        block = first.enter_context(nc.Block())

        def per_block(ap):
            return ap.rearrange("p (k n) -> p k n", k=NBLK)

        def cells(x):
            return x[:, :, :].rearrange("p (k j) g -> p k (j g)", k=NBLK)

        def flat(x):
            return x[:, :, :].rearrange("p k c -> p (k c)")

        @block.sync
        def _(sp):
            for dst, src in (
                (cst[:, :], A["consts2"]),
                (slopes[:, :, :].rearrange("p a g -> p (a g)"), A["slopes"].rearrange("(o t) j g -> o (t j g)", o=1).broadcast_to([P, NTILE * SLICE * GRID])),
                (gamma[:, :], A["gamma"].unsqueeze(0).broadcast_to([P, HID])),
                (beta[:, :], A["beta"].unsqueeze(0).broadcast_to([P, HID])),
                (table[:, 0:SLICE * GRID], A["bases"].rearrange("t j g -> t (j g)")),
                (table[:, SLICE * GRID:2 * SLICE * GRID], A["slopes"].rearrange("t j g -> t (j g)")),
                (table[:, 2 * SLICE * GRID:2 * SLICE * GRID + 1], A["oscale"].unsqueeze(1)),
            ):
                sp.dma_start(dst, src).then_inc(w_in, 16)
            with sp.Fori(0, B) as b:
                sp.dma_start(xs[:, :, :], tokens(x1_dram, b)).then_inc(x_in, 16)
                sp.wait_ge(x_in, 16)
                meet(sp, b, N_ENG, arrive, seen, leave, ())

        @block.gpsimd
        def _(pool):
            nc.gpsimd.memset(power[:, :], -0.5).then_inc(preset, 1)
            pool.wait_ge(preset, 1)
            with pool.Fori(0, B) as b:
                for n in range(2):
                    pool.wait_ge(var_ready, n + 1)
                    nc.gpsimd.tensor_scalar(rstd[:, :], mv[:, :, 1], EPS, None, ALU.add).then_inc(eps_added, 1)
                    pool.wait_ge(eps_added, n + 1)
                    nc.gpsimd.tensor_tensor(rstd[:, :], rstd[:, :], power[:, :], ALU.pow).then_inc(rstd_ready, 1)
                meet(pool, b, N_ENG, arrive, seen, leave, (eps_added, rstd_ready))

        @block.tensor
        def _(pe):
            ident = cst[:, slice(*col["ident"])]
            pe.wait_ge(w_in, 16 * 7)
            with pe.Fori(0, B) as b:
                pe.wait_ge(hot_ready, 1)
                for k in range(NBLK):
                    last = nc.tensor.transpose(ps[0:NTILE, 0, k * P:(k + 1) * P], hot[:, k * NTILE:(k + 1) * NTILE], ident)
                last.then_inc(hot_psum, 1)
                meet(pe, b, N_ENG, arrive, seen, leave, (hot_psum,))

        @block.scalar
        def _(act):
            act.wait_ge(want_sum, 1)
            nc.scalar.activation(want[:, :], want[:, :], ACT.Sign).then_inc(want_ready, 1)
            with act.Fori(0, B) as b:
                act.wait_ge(xf_ready, 1)
                nc.scalar.activation(sg[:, :, :], xf[:, :, :], ACT.Sign).then_inc(sign_ready, 1)
                act.wait_ge(hot_psum, 1)
                nc.scalar.activation(hotT_all[:, bass.ds(b, 1), :], ps[0:NTILE, 0:1, :], ACT.Copy).then_inc(hot_turned, 1)
                meet(act, b, N_ENG, arrive, seen, leave, (sign_ready, hot_turned))

        @block.vector
        def _(dve):
            nc.vector.memset(least[:, :], BIG)
            nc.vector.memset(most[:, :], -BIG)
            dve.wait_ge(w_in, 16 * 7)
            nc.vector.tensor_reduce(want[:, :], slopes[:, :, :], AXX, ALU.add).then_inc(want_sum, 1)
            dve.wait_ge(want_ready, 1)
            with dve.Fori(0, B) as b:
                link = Chain(dve, step)

                def moments(x, n):
                    for k in range(NBLK):
                        last = nc.vector.bn_stats(stats[:, k, :], x[:, k, :])
                    link(last)
                    for k in range(NBLK):
                        last = nc.vector.bn_aggr(mv[:, k, :], stats[:, k, :])
                    last.then_inc(var_ready, 1)
                    dve.wait_ge(var_ready, n + 1)
                    dve.wait_ge(rstd_ready, n + 1)

                def normalised(dst, x):
                    for k in range(NBLK):
                        last = nc.vector.tensor_scalar(dst[:, k, :], x[:, k, :], mv[:, k, 0:1], rstd[:, k:k + 1], ALU.subtract, ALU.mult)
                    link(last)

                dve.wait_ge(x_in, 16)
                moments(xs, 0)
                normalised(xn, xs)
                moments(xn, 1)
                normalised(xf, xn)
                nc.vector.tensor_copy(xn_all[:, bass.ds(b, 1), :], xn[:, :, :].rearrange("p k c -> p (k c)").unsqueeze(1))
                link(nc.vector.tensor_tensor(xf[:, :, :], xf[:, :, :], gamma[:, :].unsqueeze(1).broadcast_to([P, NBLK, HID]), ALU.mult))
                nc.vector.tensor_tensor(xf[:, :, :], xf[:, :, :], beta[:, :].unsqueeze(1).broadcast_to([P, NBLK, HID]), ALU.add).then_inc(xf_ready, 1)
                dve.wait_ge(sign_ready, 1)
                link(nc.vector.tensor_tensor(w1[:, :, :], sg[:, :, :], want[:, :].unsqueeze(1).broadcast_to([P, NBLK, HID]), ALU.mult))
                link(nc.vector.tensor_reduce(ts[:, :], w1[:, :, :].rearrange("p k (t j) -> p (k t) j", j=SLICE), AXX, ALU.add))
                link(nc.vector.tensor_reduce(cs[:, :], ts[:, :].rearrange("p (c t) -> p c t", t=PER_CLUSTER), AXX, ALU.add))
                link(nc.vector.scalar_tensor_tensor(cs[:, :], cs[:, :], float(NCLUSTER), cst[:, slice(*col["cluster"])], ALU.mult, ALU.subtract))
                link(nc.vector.tensor_reduce(top[:, :], per_block(cs[:, :]), AXX, ALU.max))
                link(nc.vector.tensor_tensor(per_block(ch[:, :]), per_block(cs[:, :]), top[:, :].unsqueeze(2).broadcast_to([P, NBLK, NCLUSTER]), ALU.is_equal))
                link(nc.vector.scalar_tensor_tensor(ts[:, :], ts[:, :], float(PER_CLUSTER), cst[:, slice(*col["in_cluster"])], ALU.mult, ALU.subtract))
                tiles = ts[:, :].rearrange("p (c t) -> p c t", t=PER_CLUSTER)
                link(nc.vector.scalar_tensor_tensor(tiles, ch[:, :].unsqueeze(2).broadcast_to([P, NBLK * NCLUSTER, PER_CLUSTER]), 1000.0, tiles, ALU.mult, ALU.add))
                link(nc.vector.tensor_reduce(top[:, :], per_block(ts[:, :]), AXX, ALU.max))
                nc.vector.tensor_tensor(per_block(hot[:, :]), per_block(ts[:, :]), top[:, :].unsqueeze(2).broadcast_to([P, NBLK, NTILE]), ALU.is_equal).then_inc(hot_ready, 1)
                dve.wait_ge(hot_ready, 1)
                nc.vector.tensor_copy(hot_all[:, bass.ds(b, 1), :], hot[:, :].unsqueeze(1))
                link(nc.vector.tensor_tensor(w2[:, :, :].rearrange("p k (t j) -> p (k t) j", j=SLICE), xf[:, :, :].rearrange("p k (t j) -> p (k t) j", j=SLICE),
                                             hot[:, :].unsqueeze(2).broadcast_to([P, NT, SLICE]), ALU.mult))
                link(nc.vector.tensor_reduce(sl[:, :].rearrange("p (k j) -> p k j", k=NBLK), w2[:, :, :].rearrange("p k (t j) -> p k j t", j=SLICE), AXX, ALU.add))
                nc.vector.tensor_copy(sl_all[:, bass.ds(b, 1), :], sl[:, :].unsqueeze(1))
                nc.vector.tensor_reduce(ends[:, 0, :], per_block(sl[:, :]), AXX, ALU.min)
                link(nc.vector.tensor_reduce(ends[:, 1, :], per_block(sl[:, :]), AXX, ALU.max))
                nc.vector.tensor_scalar(pen[:, :], hot[:, :], -BIG, BIG, ALU.mult, ALU.add)
                nc.vector.tensor_tensor(per_block(lo[:, :]), per_block(hot[:, :]), ends[:, 0, :].unsqueeze(2).broadcast_to([P, NBLK, NTILE]), ALU.mult)
                link(nc.vector.tensor_tensor(per_block(hi[:, :]), per_block(hot[:, :]), ends[:, 1, :].unsqueeze(2).broadcast_to([P, NBLK, NTILE]), ALU.mult))
                nc.vector.tensor_tensor(lo[:, :], lo[:, :], pen[:, :], ALU.add)
                link(nc.vector.tensor_tensor(hi[:, :], hi[:, :], pen[:, :], ALU.subtract))
                nc.vector.tensor_tensor(least[:, :], least[:, :], lo[:, :], ALU.min)
                link(nc.vector.tensor_tensor(most[:, :], most[:, :], hi[:, :], ALU.max))
                meet(dve, b, N_ENG, arrive, seen, leave, (step, var_ready, xf_ready, hot_ready, x_in))

        first.close()

        ends_ready, ends_psum, table_ready = t.sem("f2_ends_ready"), t.sem("f2_ends_psum"), t.sem("f2_table_ready")
        in_x, in_s, hot_copied, tab_psum, clipped, exped, mixed, stored = (
            t.sem("f2_" + n) for n in ("in_x", "in_s", "hot_copied", "tab_psum", "clipped", "exped", "mixed", "stored"))
        step2, arrive2, seen2, leave2 = t.sem("f2_step"), t.sem("f2_arrive"), t.sem("f2_seen"), t.sem("f2_leave")
        block = ctx.enter_context(nc.Block())
        BASES, SLOPES, SCALE, LEAST, MOST = 0, SLICE * GRID, TAB - 3, TAB - 2, TAB - 1

        @block.sync
        def _(sp):
            with sp.Fori(0, B) as b:
                sp.dma_start(s1[:, :, :], tokens(s1_dram, b)).then_inc(in_s, 16)
                sp.dma_start(xs[:, :, :], tokens(x1_dram, b)).then_inc(in_x, 16)
                sp.wait_ge(mixed, 1)
                sp.dma_start(tokens(out, b), xf[:, :, :]).then_inc(stored, 16)
                sp.wait_ge(stored, 16)
                meet(sp, b, N_ENG, arrive2, seen2, leave2, (mixed, stored))

        @block.gpsimd
        def _(pool):
            with pool.Fori(0, B) as b:
                nc.gpsimd.tensor_copy(hotT[:, :].unsqueeze(1), hotT_all[:, bass.ds(b, 1), :]).then_inc(hot_copied, 1)
                meet(pool, b, N_ENG, arrive2, seen2, leave2, (hot_copied,))

        @block.tensor
        def _(pe):
            pe.wait_ge(ends_ready, 2)
            for n in range(2):
                last = nc.tensor.transpose(ps[0:NTILE, 1, n * P:(n + 1) * P], ends64[:, n, :], cst[:, slice(*col["ident"])])
            last.then_inc(ends_psum, 1)
            pe.wait_ge(table_ready, 2)
            with pe.Fori(0, B) as b:
                pe.wait_ge(hot_copied, 1)
                for k in range(NBLK):
                    last = nc.tensor.matmul(ps[:, 2 + k // 2, (k % 2) * HID:(k % 2) * HID + TAB], hotT[:, k * P:(k + 1) * P], table[:, :],
                                            start=True, stop=True)
                last.then_inc(tab_psum, 1)
                meet(pe, b, N_ENG, arrive2, seen2, leave2, (tab_psum,))

        @block.scalar
        def _(act):
            with act.Fori(0, B) as b:
                act.wait_ge(clipped, 1)
                nc.scalar.activation(w1[:, :, :], w1[:, :, :], ACT.Exp).then_inc(exped, 1)
                meet(act, b, N_ENG, arrive2, seen2, leave2, (exped,))

        @block.vector
        def _(dve):
            for n, (src, op) in enumerate(((least, ALU.min), (most, ALU.max))):
                nc.vector.tensor_reduce(ends64[:, n, :], src[:, :].rearrange("p (k t) -> p t k", k=NBLK), AXX, op).then_inc(ends_ready, 1)
            dve.wait_ge(ends_psum, 1)
            for n, op in enumerate((ALU.min, ALU.max)):
                nc.vector.tensor_reduce(table[:, LEAST + n:LEAST + n + 1], ps[0:NTILE, 1, n * P:(n + 1) * P], AXX, op).then_inc(table_ready, 1)
            got = ps[:, 2:4, :].rearrange("p a (k c) -> p (a k) c", k=2)

            def four(ap):
                return ap.rearrange("p (k j) -> p k j", j=SLICE)

            def each(ap):
                return ap.unsqueeze(2).broadcast_to([P, NBLK, SLICE])

            with dve.Fori(0, B) as b:
                link = Chain(dve, step2)
                dve.wait_ge(tab_psum, 1)
                link(nc.vector.tensor_copy(tab[:, :, :], got[:, :, SCALE:TAB]))
                scale, least_t, most_t = (tab[:, :, n] for n in range(3))
                nc.vector.tensor_tensor(four(sl[:, :]), sl_all[:, bass.ds(b, 1), :].rearrange("p a (k j) -> p (a k) j", j=SLICE), each(least_t), ALU.subtract)
                link(nc.vector.tensor_tensor(rng[:, :], most_t, least_t, ALU.subtract))
                link(nc.vector.tensor_scalar(rng[:, :], rng[:, :], 1e-8, None, ALU.add))
                link(nc.vector.reciprocal(rng[:, :], rng[:, :]))
                link(nc.vector.tensor_tensor(four(sl[:, :]), four(sl[:, :]), each(rng[:, :]), ALU.mult))
                link(nc.vector.tensor_scalar(sl[:, :], sl[:, :], 0.0, U_MAX, ALU.max, ALU.min))
                link(nc.vector.tensor_scalar(sl[:, :], sl[:, :], float(GRID), None, ALU.mult))
                link(nc.vector.tensor_tensor(d[:, :, :], sl[:, :].unsqueeze(2).broadcast_to([P, NBLK * SLICE, GRID]),
                                             cst[:, col["grid"][0]:col["grid"][0] + GRID].unsqueeze(1).broadcast_to([P, NBLK * SLICE, GRID]), ALU.subtract))
                nc.vector.tensor_tensor(cells(val), got[:, :, SLOPES:SLOPES + SLICE * GRID], cells(d), ALU.mult)
                link(nc.vector.tensor_scalar(ge[:, :, :], d[:, :, :], 0.0, None, ALU.is_ge))
                nc.vector.scalar_tensor_tensor(in_[:, :, :], d[:, :, :], 1.0, ge[:, :, :], ALU.is_lt, ALU.mult)
                link(nc.vector.tensor_tensor(cells(val), got[:, :, BASES:BASES + SLICE * GRID], cells(val), ALU.add))
                link(nc.vector.tensor_tensor(val[:, :, :], val[:, :, :], in_[:, :, :], ALU.mult))
                link(nc.vector.tensor_reduce(dl[:, :], val[:, :, :], AXX, ALU.add))
                link(nc.vector.tensor_tensor(four(dl[:, :]), four(dl[:, :]), each(scale), ALU.mult))
                link(nc.vector.tensor_tensor(w2[:, :, :].rearrange("p k (t j) -> p k t j", j=SLICE),
                                             hot_all[:, bass.ds(b, 1), :].rearrange("p a (k t) -> p (a k) t", k=NBLK).unsqueeze(3).broadcast_to([P, NBLK, NTILE, SLICE]),
                                             four(dl[:, :]).unsqueeze(2).broadcast_to([P, NBLK, NTILE, SLICE]), ALU.mult))
                link(nc.vector.tensor_tensor(flat(w2), flat(w2), xn_all[:, bass.ds(b, 1), :].rearrange("p a n -> p (a n)"), ALU.add))
                nc.vector.tensor_scalar(w1[:, :, :], w2[:, :, :], -1.0, 80.0, ALU.mult, ALU.min).then_inc(clipped, 1)
                dve.wait_ge(exped, 1)
                link(nc.vector.tensor_scalar(w1[:, :, :], w1[:, :, :], 1.0, None, ALU.add))
                link(nc.vector.reciprocal(w1[:, :, :], w1[:, :, :]))
                link(nc.vector.tensor_tensor(w1[:, :, :], w1[:, :, :], w2[:, :, :], ALU.mult))
                dve.wait_ge(in_s, 16)
                link(nc.vector.tensor_tensor(w1[:, :, :], w1[:, :, :], s1[:, :, :], ALU.mult))
                dve.wait_ge(in_x, 16)
                nc.vector.tensor_tensor(xf[:, :, :], w1[:, :, :], xs[:, :, :], ALU.add).then_inc(mixed, 1)
                meet(dve, b, N_ENG, arrive2, seen2, leave2, (step2, clipped, in_s, in_x))


def recurrent_d2_kernel(nc, A, cst_cols, cols1, cols2, out):
    with ExitStack() as ctx:
        t = Scope(nc, ctx)
        ps = ctx.enter_context(nc.psum_tensor("ps", [P, 8, S], F32))
        parts_dram = [nc.dram_tensor(f"parts_{n}", [NPART, HD, B * H, S], BF16, kind="Internal").ap() for n in range(4)]
        v_dram = [nc.dram_tensor(f"values_{n}", [B * NG, P, NBLK * GH * (HD + 1)], F32, kind="Internal").ap() for n in range(2)]
        o_dram = [nc.dram_tensor(f"outs_{n}", [B * H, HD + 1, S], F32, kind="Internal").ap() for n in range(2)]
        inv_dram = [nc.dram_tensor(f"inverse_sums_{n}", [B * H, S], F32, kind="Internal").ap() for n in range(2)]
        x1_dram = nc.dram_tensor("x1_dram", [B, S, HID], F32, kind="Internal").ap()
        s1_dram = nc.dram_tensor("s1_dram", [B, S, HID], F32, kind="Internal").ap()
        w = {}
        layer0 = ctx.enter_context(ExitStack())
        mids = Scope(nc, layer0)
        cst = mids.sb("cst0", [P, A["consts0"].shape[1]])
        with ExitStack() as early:
            e = Scope(nc, early)
            for name, shape, dt in (
                ("o_a", [P, KC, HID], F32), ("o_f", [P, KC, HID], F32),
                ("ident_b", [P, P], BF16), ("mask_qk", [P, P], BF16), ("mask_kq", [P, P], BF16),
            ):
                w[name] = mids.sb(name, shape, dt)
            for name, shape in (
                ("d", [P, KC, 2 * LAT]), ("q_a", [LAT, HID]), ("q_b", [LAT, HID]), ("k_a", [2 * LAT, HID]),
                ("v_a", [2 * LAT, HID]), ("kr_a", [P, KC, HID]), ("kr_b", [P, KC, HID]),
                ("q_f", [P, KC, HID]), ("k_f", [P, KC, HID]), ("v_f", [P, KC, HID]),
            ):
                w[name] = e.sb("w_" + name, shape)
            load_layer0(nc, e, w, cst, cst_cols, A)
            project_layer0(nc, ps, w, cst, cst_cols, A, parts_dram, v_dram)
        attend_layer0(nc, ps, w, cst, cst_cols, parts_dram, v_dram, o_dram)
        gate_layer0(nc, ps, w, cst, cst_cols, A, o_dram, inv_dram, x1_dram)
        layer0.close()
        recur_layer1(nc, ps, cols1, A, x1_dram, s1_dram)
        mix_layer1(nc, ps, cols2, A, x1_dram, s1_dram, out)


_INS = {
    "L0_attn_hidden_states": "x", "L0_attn_w_kv_d": "w_kv_d", "L0_attn_w_q_d": "w_q_d", "L0_attn_w_k_u": "w_k_u",
    "L0_attn_w_q_u": "w_q_u", "L0_attn_w_v_u": "w_v_u", "L0_attn_w_rope_k": "w_rope_k",
    "L0_attn_w_rope_q": "w_rope_q", "L0_attn_w_o": "w_o", "L0_ffn_Wa": "Wa", "L0_ffn_Wp": "Wp",
    "L0_ffn_w_std": "w_std", "L0_ffn_w_rec": "w_rec", "L1_attn_Wq": "Wq", "L1_attn_Wk": "Wk", "L1_attn_Wv": "Wv",
    "L1_attn_Wo": "Wo", "L1_attn_betas": "betas", "L1_ffn_ln_gamma": "gamma", "L1_ffn_ln_beta": "beta",
    "L1_ffn_spline_bases": "bases", "L1_ffn_spline_slopes": "slopes", "L1_ffn_output_scale": "oscale",
}


def kernel(**inputs):
    import concourse.bacc as bacc
    from concourse.bass_utils import run_bass_kernel_spmd

    nc = bacc.Bacc("TRN2", target_bir_lowering=False, num_devices=1)
    consts0, cols0 = shape_constants(0)
    consts1, cols1 = shape_constants(1)
    consts2, cols2 = shape_constants(2)
    arrays, A = {}, {}
    for long, short in _INS.items():
        a = np.ascontiguousarray(inputs[long])
        arrays[f"in_{short}"] = a
        A[short] = nc.dram_tensor(f"in_{short}", a.shape, mybir.dt.from_np(a.dtype), kind="ExternalInput").ap()
    for name, a in (("consts0", consts0), ("consts1", consts1), ("consts2", consts2)):
        arrays["in_" + name] = a
        A[name] = nc.dram_tensor("in_" + name, a.shape, F32, kind="ExternalInput").ap()
    out = nc.dram_tensor("out", (B, S, HID), F32, kind="ExternalOutput").ap()
    recurrent_d2_kernel(nc, A, cols0, cols1, cols2, out)
    r = run_bass_kernel_spmd(nc, [arrays], core_ids=[0])
    return r.results[0]["out"]
```

```python
import math
from contextlib import ExitStack

import numpy as np

import concourse.bass as bass
from concourse import mybir

F32 = mybir.dt.float32
BF16 = mybir.dt.bfloat16
ALU = mybir.AluOpType
ACT = mybir.ActivationFunctionType
AXX = mybir.AxisListType.X

P = 128
B, S, HID = 8, 512, 256
NBLK = S // P
KC = HID // P
H, HD = 16, 16
HH = HD // 2
LAT = HID // 8
NHALF = H // 8
GH = 4
NG = H // GH
NPART = 3
Q_SLOT = (0, 1, 2, 0, 1, 0)
K_SLOT = (0, 0, 0, 1, 1, 2)
STACK = len(Q_SLOT) * HD
MROWS = GH * NPART
EPS = 1e-5
THRESHOLD = 0.1
BIG = 1.0e30
ATTN, FFN = 0, 1

DK = 128
SEG = 64
NSEG = S // SEG
NTILE, SLICE, GRID, PER_CLUSTER = 64, 4, 16, 8
NCLUSTER = NTILE // PER_CLUSTER


def shape_constants(phase):
    cols = {}
    parts = []

    def put(name, a):
        at = sum(x.shape[1] for x in parts)
        parts.append(a.astype(np.float32))
        cols[name] = (at, at + a.shape[1])

    r = np.arange(P)
    put("ident", np.eye(P))
    if phase == 1:
        seg = r // SEG
        ok = (seg[:, None] == seg[None, :]) & (r[None, :] <= r[:, None])
        put("mask_seg", np.where(ok, 0.0, -BIG))
        return np.concatenate(parts, axis=1), cols
    if phase == 2:
        put("grid", np.tile(np.arange(GRID), (P, SLICE)))
        put("cluster", np.tile(np.arange(NCLUSTER), (P, NBLK)))
        put("in_cluster", np.tile(np.arange(PER_CLUSTER), (P, NBLK * NCLUSTER)))
        return np.concatenate(parts, axis=1), cols
    half = HH // 2
    inv_freq = (1.0 / 10000.0 ** (np.arange(0, HH, 2, dtype=np.float32) / HH)).astype(np.float32)
    angle = (np.arange(S, dtype=np.float32)[:, None] * inv_freq[None, :]).astype(np.float32)
    sin, cos = np.sin(angle).T, np.cos(angle).T
    c, s = np.zeros((HD, S)), np.zeros((HD, S))
    c[:HH] = 1.0
    c[HH:HH + half] = cos
    c[HH + half:] = cos
    s[HH:HH + half] = -sin
    s[HH + half:] = sin
    put("rope_c", np.tile(c, (8, 1)))
    put("rope_s", np.tile(s, (8, 1)))
    put("mask_qk", np.where(r[None, :] > r[:, None], -BIG, 0.0))
    put("mask_kq", np.where(r[None, :] < r[:, None], -BIG, 0.0))
    one = np.zeros((P, GH))
    for h in range(GH):
        one[STACK + h * NPART:STACK + (h + 1) * NPART, h] = 1.0
    put("own_max", one)
    return np.concatenate(parts, axis=1), cols


def wait_apart(eng, sem, value, seen):
    eng.wait_ge(sem, value)
    eng.sem_inc(seen, 1)


class Scope:

    def __init__(self, nc, ctx):
        self.nc, self.ctx = nc, ctx

    def sb(self, name, shape, dt=F32):
        return self.ctx.enter_context(self.nc.sbuf_tensor(name, shape, dt))

    def sem(self, name):
        return self.ctx.enter_context(self.nc.semaphore(name))


class Chain:

    def __init__(self, eng, sem):
        self.eng, self.sem, self.n = eng, sem, 0

    def __call__(self, ins):
        self.n += 1
        ins.then_inc(self.sem, 1)
        self.eng.wait_ge(self.sem, self.n)


PAR = 2


def upto(turn, p, per, c):
    return turn * (PAR * per) + (p * per + c)


def early(turn, p=0):
    return isinstance(turn, int) and turn == 0 and p < PAR


def by_pairs(eng, first, step):
    if first:
        first(0, 0)
    for p in range(PAR):
        step(0, p, False)
    with eng.Fori(1, B // PAR - 1) as turn:
        for p in range(PAR):
            step(turn, p, False)
    for p in range(PAR):
        step(B // PAR - 1, p, p == PAR - 1)


N_SIG = 4


def sigmoid(act, nc, e, y, one, step, log_ready, turn, p):
    nc.scalar.activation(e, y, ACT.Abs).then_inc(step, 1)
    act.wait_ge(step, upto(turn, p, N_SIG, 1))
    nc.scalar.activation(e, e, ACT.Exp, scale=-1.0).then_inc(step, 1)
    act.wait_ge(step, upto(turn, p, N_SIG, 2))
    nc.scalar.activation(e, e, ACT.Ln, bias=one[:, 0:1]).then_inc(step, 1)
    act.wait_ge(log_ready, upto(turn, p, 1, 1))
    nc.scalar.activation(e, e, ACT.Exp).then_inc(step, 1)


def log_sigmoid(dve, nc, e, y, step, log_ready, turn, p):
    dve.wait_ge(step, upto(turn, p, N_SIG, 3))
    nc.vector.scalar_tensor_tensor(e, y, 0.0, e, ALU.min, ALU.subtract).then_inc(log_ready, 1)
    dve.wait_ge(step, upto(turn, p, N_SIG, N_SIG))


def spread(ap, shape):
    return ap.broadcast_to(shape)


def load_layer0(nc, sc, w, cst, col, A):
    with ExitStack() as ctx:
        t = Scope(nc, ctx)
        wqu = t.sb("wqu", [LAT, P])
        wrq = t.sb("wrq", [LAT, P])
        wku = t.sb("wku", [2 * LAT, P])
        wrk = t.sb("wrk", [P, KC, P])
        wa = t.sb("wa", [P, KC, 768])
        hs = t.sb("head_scales", [P, 8, H])
        hs2 = t.sb("kept_low", [P, H, HH])
        loaded = t.sem("l0_loaded")
        clamped = t.sem("l0_clamped")
        rooted = t.sem("l0_rooted")
        step = t.sem("l0_step")
        N_DMA = 13
        block = ctx.enter_context(nc.Block())

        @block.sync
        def _(sp):
            for dst, src in (
                (cst[:, :], A["consts0"]),
                (w["d"][:, :, 0:LAT], A["w_q_d"].rearrange("(k p) n -> p k n", p=P)),
                (w["d"][:, :, LAT:2 * LAT], A["w_kv_d"].rearrange("(k p) n -> p k n", p=P)),
                (wqu[:, :], A["w_q_u"]),
                (wrq[:, :], A["w_rope_q"]),
                (wku[LAT:2 * LAT, :], A["w_k_u"]),
                (w["v_a"][LAT:2 * LAT, :], A["w_v_u"]),
                (wrk[:, :, :], A["w_rope_k"].rearrange("(k p) n -> p k n", p=P)),
                (wa[:, :, :], A["Wa"].rearrange("(k p) n -> p k n", p=P)),
                (w["o_a"][:, :, :], A["w_o"].rearrange("(k p) n -> p k n", p=P)),
                (w["o_f"][:, :, :], A["Wp"].rearrange("(k p) n -> p k n", p=P)),
                (hs[:, 0, :], A["w_std"].unsqueeze(0).broadcast_to([P, H])),
                (hs[:, 1, :], A["w_rec"].unsqueeze(0).broadcast_to([P, H])),
            ):
                sp.dma_start(dst, src).then_inc(loaded, 16)

        @block.gpsimd
        def _(pool):
            nc.gpsimd.memset(hs[:, 7, :], 0.5).then_inc(rooted, 1)
            pool.wait_ge(rooted, 1)
            pool.wait_ge(clamped, 2)
            nc.gpsimd.tensor_tensor(hs[:, 2, :], hs[:, 2, :], hs[:, 7, :], ALU.pow).then_inc(rooted, 1)
            nc.gpsimd.tensor_tensor(hs[:, 3, :], hs[:, 3, :], hs[:, 7, :], ALU.pow).then_inc(rooted, 1)

        @block.vector
        def _(dve):
            link = Chain(dve, step)
            for name in ("q_a", "q_b", "k_a", "kr_a", "kr_b"):
                nc.vector.memset(w[name][:], 0.0)
            dve.wait_ge(loaded, 16 * N_DMA)
            nc.vector.tensor_scalar(hs[:, 2, :], hs[:, 0, :], 1e-8, None, ALU.max).then_inc(clamped, 1)
            nc.vector.tensor_scalar(hs[:, 3, :], hs[:, 1, :], 1e-8, None, ALU.max).then_inc(clamped, 1)
            link(nc.vector.tensor_copy(w["ident_b"][:, :], cst[:, slice(*col["ident"])]))
            nc.vector.tensor_copy(w["mask_qk"][:, :], cst[:, slice(*col["mask_qk"])])
            nc.vector.tensor_copy(w["mask_kq"][:, :], cst[:, slice(*col["mask_kq"])])

            def heads(ap):
                return ap.rearrange("p (h c) -> p h c", h=H)

            half = HH // 2
            for plain, rope, dst_a, dst_b, lo, hi in (
                (wqu, wrq, w["q_a"], w["q_b"], 0, LAT),
                (wku, None, w["k_a"], None, LAT, 2 * LAT),
            ):
                nc.vector.tensor_copy(heads(dst_a[lo:hi, :])[:, :, 0:HH], heads(plain[lo:hi, :]))
                if rope is not None:
                    nc.vector.tensor_copy(heads(dst_a[lo:hi, :])[:, :, HH:HD], heads(rope[lo:hi, :]))
                    nc.vector.tensor_copy(heads(dst_b[lo:hi, :])[:, :, HH:HH + half], heads(rope[lo:hi, :])[:, :, half:HH])
                    nc.vector.tensor_copy(heads(dst_b[lo:hi, :])[:, :, HH + half:HD], heads(rope[lo:hi, :])[:, :, 0:half])
            for k in range(KC):
                src = heads(wrk[:, k, :])
                nc.vector.tensor_copy(heads(w["kr_a"][:, k, :])[:, :, HH:HD], src)
                nc.vector.tensor_copy(heads(w["kr_b"][:, k, :])[:, :, HH:HH + half], src[:, :, half:HH])
                nc.vector.tensor_copy(heads(w["kr_b"][:, k, :])[:, :, HH + half:HD], src[:, :, 0:half])
                nc.vector.tensor_copy(w["v_f"][:, k, :], wa[:, k, 2 * P:2 * P + HID])
            dve.wait_ge(rooted, 3)
            link(nc.vector.tensor_scalar(hs[:, 4, :], hs[:, 1, :], THRESHOLD, None, ALU.is_gt))
            link(nc.vector.tensor_scalar(hs[:, 5, :], hs[:, 4, :], -1.0, 1.0, ALU.mult, ALU.add))
            link(nc.vector.tensor_tensor(hs[:, 4, :], hs[:, 4, :], hs[:, 3, :], ALU.mult))
            link(nc.vector.tensor_tensor(hs[:, 5, :], hs[:, 5, :], hs[:, 3, :], ALU.mult))
            std, swap, keep = (spread(hs[:, n, :].unsqueeze(2), [P, H, HH]) for n in (2, 4, 5))
            for k in range(KC):
                q_std, k_std, q_low, k_low = (heads(wa[:, k, at:at + P]) for at in (0, P, 2 * P + HID, 3 * P + HID))
                q_out, k_out = heads(w["q_f"][:, k, :]), heads(w["k_f"][:, k, :])
                link(nc.vector.tensor_tensor(q_out[:, :, 0:HH], q_std, std, ALU.mult))
                link(nc.vector.tensor_tensor(k_out[:, :, 0:HH], k_std, std, ALU.mult))
                for out, swapped, kept in ((q_out, k_low, q_low), (k_out, q_low, k_low)):
                    link(nc.vector.tensor_tensor(out[:, :, HH:HD], swapped, swap, ALU.mult))
                    link(nc.vector.tensor_tensor(hs2[:, :, :], kept, keep, ALU.mult))
                    link(nc.vector.tensor_tensor(out[:, :, HH:HD], out[:, :, HH:HD], hs2[:, :, :], ALU.add))


def project_layer0(nc, ps, seen, w, cst, col, A, parts_dram, v_dram):
    with ExitStack() as ctx:
        t = Scope(nc, ctx)
        x = t.sb("p_x", [P, NBLK, HID])
        xn = t.sb("p_xn", [P, NBLK, HID])
        stats = t.sb("p_stats", [P, NBLK, 6])
        mv = t.sb("p_mv", [P, NBLK, 2])
        rstd = t.sb("p_rstd", [P, NBLK])
        power = t.sb("p_power", [P, NBLK])
        xT = [t.sb(f"p_xT{n}", [P, KC, S]) for n in range(PAR)]
        dT = [t.sb(f"p_dT{n}", [2 * LAT, S]) for n in range(PAR)]
        rc = t.sb("p_rc", [P, NHALF, S])
        rs = t.sb("p_rs", [P, NHALF, S])
        full = [t.sb(f"p_full{n}", [P, NHALF, S]) for n in range(4)]
        rest = [t.sb(f"p_rest{n}", [P, NHALF, S]) for n in range(4)]
        part = [t.sb(f"p_part{n}", [P, NPART, NHALF, S], BF16) for n in range(4)]
        va = [t.sb(f"p_v{n}", [P, NG, NBLK, GH, HD + 1]) for n in range(2)]

        x_in = t.sem("x_in")
        stat_ready, var_ready, eps_added, rstd_ready = (t.sem(n) for n in ("stat_ready", "var_ready", "eps_added", "rstd_ready"))
        xn_ready, xt_psum, xt_ready = t.sem("xn_ready"), t.sem("xt_psum"), t.sem("xt_ready")
        d_psum, d_ready = t.sem("d_psum"), t.sem("d_ready")
        ffn_psum, ffn_full = t.sem("ffn_psum"), t.sem("ffn_full")
        rope_psum, rope_terms, rope_full = t.sem("rope_psum"), t.sem("rope_terms"), t.sem("rope_full")
        v_psum, v_ready = t.sem("v_psum"), t.sem("v_ready")
        hi_ready, rest_ready, mid_ready, lo_ready = (t.sem(f"part_{n}") for n in ("hi", "rest", "mid", "lo"))
        stored = [t.sem(f"parts_stored{n}") for n in range(4)]
        v_stored = [t.sem(f"values_stored{n}") for n in range(2)]
        preset = t.sem("p_preset")
        ORDER = (2, 3, 0, 1)
        block = ctx.enter_context(nc.Block())

        @block.sync
        def _(sp):
            def load(turn, p):
                sp.dma_start(x[:, :, :], tokens(A["x"], turn * PAR + p)).then_inc(x_in, 16)

            def start(turn, p):
                load(turn, p)
                sp.wait_ge(xn_ready, 1)
                load(turn, p + 1)

            def batch(turn, p, last):
                b = turn * PAR + p
                if not (last or (isinstance(turn, int) and b == B - 2)):
                    sp.wait_ge(xn_ready, upto(turn, p, 1, 2))
                    load(turn, p + 2)
                for n, tensor in enumerate(ORDER):
                    for m in range(NPART):
                        sp.wait_ge((hi_ready, mid_ready, lo_ready)[m], upto(turn, p, 4, n + 1))
                        for f in range(NHALF):
                            rows = parts_dram[tensor][m, :, bass.ds(b * H + f * 8, 8), :]
                            sp.dma_start(rows.rearrange("d h n -> h d n"), part[tensor][:, m, f, :]).then_inc(stored[tensor], 16)
                for kind in (ATTN, FFN):
                    sp.wait_ge(v_ready, upto(turn, p, 4, 2 * (kind + 1)))
                    sp.dma_start(v_dram[kind][bass.ds(b * NG, NG), :, :].rearrange("g p n -> p g n"),
                                 va[kind][:, :, :, :, :].rearrange("p g k h c -> p g (k h c)")).then_inc(v_stored[kind], 16)

            by_pairs(sp, start, batch)
            for s in stored:
                sp.wait_ge(s, 16 * NPART * NHALF * B)
            for s in v_stored:
                sp.wait_ge(s, 16 * B)

        @block.gpsimd
        def _(pool):
            nc.gpsimd.memset(power[:, :], -0.5).then_inc(preset, 1)
            nc.gpsimd.memset(va[0][:], 1.0)
            nc.gpsimd.memset(va[1][:], 1.0).then_inc(preset, 1)
            pool.wait_ge(preset, 2)

            def inv_std(turn, p):
                wait_apart(pool, var_ready, upto(turn, p, 1, 1), seen)
                nc.gpsimd.tensor_scalar(rstd[:, :], mv[:, :, 1], EPS, None, ALU.add).then_inc(eps_added, 1)
                wait_apart(pool, eps_added, upto(turn, p, 1, 1), seen)
                nc.gpsimd.tensor_tensor(rstd[:, :], rstd[:, :], power[:, :], ALU.pow).then_inc(rstd_ready, 1)

            def batch(turn, p, last):
                if not last:
                    inv_std(turn, p + 1)
                for n, tensor in enumerate(ORDER):
                    if tensor < 2:
                        wait_apart(pool, rope_terms, upto(turn, p, 2, tensor + 1), seen)
                        nc.gpsimd.tensor_tensor(full[tensor][:, :, :], rc[:, :, :], rs[:, :, :], ALU.add).then_inc(rope_full, 1)
                    wait_apart(pool, hi_ready, upto(turn, p, 4, n + 1), seen)
                    nc.gpsimd.tensor_tensor(rest[tensor][:, :, :], full[tensor][:, :, :], part[tensor][:, 0, :, :], ALU.subtract).then_inc(rest_ready, 1)
                    wait_apart(pool, mid_ready, upto(turn, p, 4, n + 1), seen)
                    nc.gpsimd.tensor_tensor(part[tensor][:, 2, :, :], rest[tensor][:, :, :], part[tensor][:, 1, :, :], ALU.subtract).then_inc(lo_ready, 1)

            by_pairs(pool, inv_std, batch)

        @block.scalar
        def _(act):
            act.wait_ge(preset, 2)

            def take_x(turn, p):
                act.wait_ge(xt_psum, upto(turn, p, 1, 1))
                nc.scalar.activation(xT[p % PAR][:, :, :], ps[:, 4:6, :], ACT.Copy).then_inc(xt_ready, 1)

            def take_d(turn, p):
                act.wait_ge(d_psum, upto(turn, p, 1, 1))
                nc.scalar.activation(dT[p % PAR][:, :], ps[0:2 * LAT, 6, :], ACT.Copy).then_inc(d_ready, 1)

            def split(turn, p, n):
                tensor = ORDER[n]
                if tensor >= 2:
                    act.wait_ge(ffn_full, upto(turn, p, 2, n + 1))
                else:
                    act.wait_ge(rope_full, upto(turn, p, 2, tensor + 1))
                if not (early(turn) and p == 0):
                    act.wait_ge(stored[tensor], upto(turn, p, 16 * NPART * NHALF, 0))
                nc.scalar.activation(part[tensor][:, 0, :, :], full[tensor][:, :, :], ACT.Copy).then_inc(hi_ready, 1)
                act.wait_ge(rest_ready, upto(turn, p, 4, n + 1))
                nc.scalar.activation(part[tensor][:, 1, :, :], rest[tensor][:, :, :], ACT.Copy).then_inc(mid_ready, 1)

            def take_v(turn, p, kind):
                if not (early(turn) and p == 0):
                    act.wait_ge(v_stored[kind], upto(turn, p, 16, 0))
                for j in range(2):
                    act.wait_ge(v_psum, upto(turn, p, 4, 2 * kind + j + 1))
                    for i in range(2):
                        k = 2 * j + i
                        done = nc.scalar.activation(
                            va[kind][:, :, k, :, 0:HD],
                            ps[:, 2 * kind + j, i * HID:(i + 1) * HID].rearrange("p (g h c) -> p g h c", g=NG, h=GH), ACT.Copy)
                    done.then_inc(v_ready, 1)

            def start(turn, p):
                take_x(turn, p)
                take_d(turn, p)

            def batch(turn, p, last):
                for n in range(2):
                    act.wait_ge(ffn_psum, upto(turn, p, 2, n + 1))
                    nc.scalar.activation(full[2 + n][:, :, :], ps[:, 4 + 2 * n:6 + 2 * n, :], ACT.Copy).then_inc(ffn_full, 1)
                for n in range(3):
                    split(turn, p, n)
                take_v(turn, p, ATTN)
                if not last:
                    take_x(turn, p + 1)
                take_v(turn, p, FFN)
                if not last:
                    take_d(turn, p + 1)
                split(turn, p, 3)

            by_pairs(act, start, batch)

        @block.vector
        def _(dve):
            def normalise(turn, p):
                dve.wait_ge(x_in, upto(turn, p, 16, 16))
                for k in range(NBLK):
                    last = nc.vector.bn_stats(stats[:, k, :], x[:, k, :])
                last.then_inc(stat_ready, 1)
                wait_apart(dve, stat_ready, upto(turn, p, 1, 1), seen)
                for k in range(NBLK):
                    last = nc.vector.bn_aggr(mv[:, k, :], stats[:, k, :])
                last.then_inc(var_ready, 1)
                dve.wait_ge(var_ready, upto(turn, p, 1, 1))
                dve.wait_ge(rstd_ready, upto(turn, p, 1, 1))
                for k in range(NBLK):
                    last = nc.vector.tensor_scalar(xn[:, k, :], x[:, k, :], mv[:, k, 0:1], rstd[:, k:k + 1], ALU.subtract, ALU.mult)
                last.then_inc(xn_ready, 1)

            def batch(turn, p, last):
                if not last:
                    dve.wait_ge(xt_psum, upto(turn, p, 1, 1))
                    normalise(turn, p + 1)
                for n in range(2):
                    at = 4 * n
                    dve.wait_ge(rope_psum, upto(turn, p, 2, n + 1))
                    if n or not (early(turn) and p == 0):
                        dve.wait_ge(rope_full, upto(turn, p, 2, n))
                    for f in range(NHALF):
                        nc.vector.tensor_tensor(rc[:, f, :], ps[:, at + f, :], cst[:, slice(*col["rope_c"])], ALU.mult)
                        done = nc.vector.tensor_tensor(rs[:, f, :], ps[:, at + 2 + f, :], cst[:, slice(*col["rope_s"])], ALU.mult)
                    done.then_inc(rope_terms, 1)

            by_pairs(dve, normalise, batch)

        @block.tensor
        def _(pe):
            ident = cst[:, slice(*col["ident"])]

            def product(out, pairs):
                for n, (lhsT, rhs) in enumerate(pairs):
                    last = nc.tensor.matmul(out, lhsT, rhs, start=(n == 0), stop=(n == len(pairs) - 1))
                return last

            def turn_x(turn, p):
                pe.wait_ge(xn_ready, upto(turn, p, 1, 1))
                for c in range(KC):
                    for k in range(NBLK):
                        last = nc.tensor.transpose(ps[:, 4 + c, k * P:(k + 1) * P], xn[:, k, c * P:(c + 1) * P], ident)
                last.then_inc(xt_psum, 1)

            def latent(turn, p):
                pe.wait_ge(xt_ready, upto(turn, p, 1, 1))
                product(ps[0:2 * LAT, 6, :], [(w["d"][:, c, :], xT[p % PAR][:, c, :]) for c in range(KC)]).then_inc(d_psum, 1)

            def values(turn, p, kind):
                for k in range(NBLK):
                    blk = slice(k * P, (k + 1) * P)
                    if kind == ATTN:
                        pairs = [(dT[p][LAT:2 * LAT, blk], w["v_a"][LAT:2 * LAT, :])]
                    else:
                        pairs = [(xT[p][:, c, blk], w["v_f"][:, c, :]) for c in range(KC)]
                    last = product(ps[:, 2 * kind + k // 2, (k % 2) * HID:(k % 2 + 1) * HID], pairs)
                    if k % 2:
                        last.then_inc(v_psum, 1)

            def start(turn, p):
                turn_x(turn, p)
                latent(turn, p)

            def batch(turn, p, last):
                for n, name in enumerate(("q_f", "k_f")):
                    if n:
                        pe.wait_ge(d_ready, upto(turn, p, 1, 1))
                    for f in range(NHALF):
                        done = product(ps[:, 4 + 2 * n + f, :],
                                       [(w[name][:, c, f * P:(f + 1) * P], xT[p][:, c, :]) for c in range(KC)])
                    done.then_inc(ffn_psum, 1)
                if not (early(turn) and p == 0):
                    pe.wait_ge(v_ready, upto(turn, p, 4, 0))
                for f in range(NHALF):
                    cols = slice(f * P, (f + 1) * P)
                    product(ps[:, f, :], [(w["q_a"][:, cols], dT[p][0:LAT, :])])
                    done = product(ps[:, 2 + f, :], [(w["q_b"][:, cols], dT[p][0:LAT, :])])
                done.then_inc(rope_psum, 1)
                pe.wait_ge(ffn_full, upto(turn, p, 2, 2))
                for f in range(NHALF):
                    cols = slice(f * P, (f + 1) * P)
                    rope = [(w["kr_a"][:, c, cols], xT[p][:, c, :]) for c in range(KC)]
                    product(ps[:, 4 + f, :], [(w["k_a"][LAT:2 * LAT, cols], dT[p][LAT:2 * LAT, :])] + rope)
                    done = product(ps[:, 6 + f, :], [(w["kr_b"][:, c, cols], xT[p][:, c, :]) for c in range(KC)])
                done.then_inc(rope_psum, 1)
                pe.wait_ge(rope_terms, upto(turn, p, 2, 1))
                values(turn, p, ATTN)
                if not last:
                    pe.wait_ge(rope_terms, upto(turn, p, 2, 2))
                    turn_x(turn, p + 1)
                values(turn, p, FFN)
                if not last:
                    latent(turn, p + 1)

            by_pairs(pe, start, batch)


def attend_layer0(nc, ps, w, cst, col, parts_dram, v_dram, o_dram):
    NSLOT = 8
    TURNS = B * NG * 2 // NSLOT
    N_S = NBLK * GH
    N_E = NBLK * GH // 2
    START = [sum(S - j * P for j in range(k)) for k in range(NBLK + 1)]
    MID = N_E // 2
    TURN_MAX = 4
    S_PAIRS = ((1, 2), (0, 3))
    E_PAIRS = ((0, 3), (1, 2))
    QUAD = P // GH
    with ExitStack() as ctx:
        t = Scope(nc, ctx)
        qs = [t.sb(f"a_q{n}", [P, GH, S], BF16) for n in range(NSLOT)]
        ks = [t.sb(f"a_k{n}", [P, GH, S], BF16) for n in range(NSLOT)]
        vs = [t.sb(f"a_v{n}", [P, NBLK, GH, HD + 1]) for n in range(NSLOT)]
        pt = [t.sb(f"a_p{n}", [P, GH, START[NBLK]]) for n in range(2)]
        ot = [t.sb(f"a_o{n}", [P, S]) for n in range(2)]
        negm = t.sb("a_negm", [P, N_S])
        mrest = t.sb("a_mrest", [P, N_S])
        mp = t.sb("a_mp", [P, N_S, NPART], BF16)
        turned = [t.sb(f"a_turned{n}", [P, S], BF16) for n in range(2)]
        loaded = [t.sem(f"a_loaded{n}") for n in range(NSLOT)]
        s_ready, s_taken = t.sem("score_ready"), t.sem("score_taken")
        m_split, mt_ready, m_copied, m_placed = (t.sem("max_" + n) for n in ("split", "turned", "copied", "placed"))
        st_ready, exp_done = t.sem("turned_score_ready"), t.sem("prob_ready")
        pv_ready, o_taken = t.sem("out_ready"), t.sem("out_taken")
        o_stored = [t.sem(f"out_stored{n}") for n in range(2)]
        m_step, preset = t.sem("max_step"), t.sem("a_preset")
        block = ctx.enter_context(nc.Block())

        def upto(turn, r, per, c):
            return turn * (NSLOT * per) + (r * per + c)

        def placed(turn, r):
            return turn * (NSLOT // 2) + r // 2

        def score_chunk(c):
            return S_PAIRS[c // (N_S // 2)][c % 2], c // 2 % GH

        def prob_chunk(c):
            return E_PAIRS[c // (N_E // 2)][c % 2], c // 2 % 2

        def mt(lo, hi):
            return ps[STACK:STACK + MROWS, 7, lo // 2:hi // 2].bitcast(BF16)

        def units(eng, unit):
            unit(0, 0, 0)
            unit(0, 1, 1)
            with eng.Fori(0, TURNS - 1) as turn:
                for r in range(2, NSLOT + 2):
                    unit(turn, r, None)
            for r in range(2, NSLOT):
                unit(TURNS - 1, r, None)

        def follows(turn, r, n):
            return not (isinstance(turn, int) and turn == TURNS - 1) or r + n < NSLOT

        @block.sync
        def _(sp):
            def load(turn, r):
                at, slot = placed(turn, r), r % NSLOT
                q, k = parts_dram[2 * (r % 2)], parts_dram[2 * (r % 2) + 1]
                heads = bass.ds(at * GH, GH)
                row = 0
                for m in (NPART, NPART - 1, NPART - 2):
                    sp.dma_start(qs[slot][row:row + m * HD, :, :],
                                 q[0:m, :, heads, :].rearrange("a d h n -> (a d) h n")).then_inc(loaded[slot], 16)
                    one = NPART - m
                    sp.dma_start(ks[slot][row:row + m * HD, :, :].rearrange("p h n -> p (h n)"),
                                 k[one:one + 1, :, heads, :].rearrange("a d h n -> a d (h n)").broadcast_to([m, HD, GH * S])).then_inc(loaded[slot], 16)
                    row += m * HD
                sp.dma_start(vs[slot][:, :, :, :].rearrange("p k h c -> p (k h c)"),
                             v_dram[r % 2][bass.ds(at, 1), :, :].rearrange("a p n -> (a p) n")).then_inc(loaded[slot], 16)

            def store(turn, r):
                sp.wait_ge(o_taken, upto(turn, r, 1, 1))
                for h in range(GH):
                    sp.dma_start(o_dram[r % 2][bass.ds(placed(turn, r) * GH + h, 1), :, :].rearrange("a c n -> (a c) n"),
                                 ot[r % 2][h * QUAD:h * QUAD + HD + 1, :]).then_inc(o_stored[r % 2], 16)

            def place_max(turn, r):
                sp.wait_ge(m_copied, upto(turn, r, 1, 1))
                rows = slice(STACK, STACK + MROWS)
                sp.dma_start(qs[r % NSLOT][rows, :, :],
                             turned[r % 2][rows, :].unsqueeze(1).broadcast_to([MROWS, GH, S])).then_inc(m_placed, 16)

            for r in range(NSLOT):
                load(0, r)
            place_max(0, 0)
            place_max(0, 1)
            with sp.Fori(0, TURNS - 1) as turn:
                for r in range(NSLOT):
                    place_max(turn, r + 2)
                    store(turn, r)
                    load(turn, r + NSLOT)
            for r in range(NSLOT):
                if r + 2 < NSLOT:
                    place_max(TURNS - 1, r + 2)
                store(TURNS - 1, r)
            for n in range(2):
                sp.wait_ge(o_stored[n], TURNS * NSLOT // 2 * GH * 16)

        @block.tensor
        def _(pe):
            pe.wait_ge(preset, 2)

            def score(turn, r, c, start=False):
                slot, (k, h) = r % NSLOT, score_chunk(c)
                if c == 0:
                    pe.wait_ge(loaded[slot], (turn + r // NSLOT) * (16 * 7) + 16 * 7)
                if not (start and c < 2):
                    pe.wait_ge(s_taken, upto(turn, r, N_S, c - 1))
                bank = 4 + c % 2
                nc.tensor.matmul(ps[:, bank, 0:(k + 1) * P], qs[slot][0:STACK, h, k * P:(k + 1) * P],
                                 ks[slot][0:STACK, h, 0:(k + 1) * P], start=True, stop=False)
                nc.tensor.matmul(ps[:, bank, k * P:(k + 1) * P], w["ident_b"][:, :], w["mask_qk"][:, :],
                                 start=False, stop=True).then_inc(s_ready, 1)

            def turn_max(turn, r):
                pe.wait_ge(m_split, upto(turn, r, 1, 1))
                for k in range(NBLK):
                    last = nc.tensor.transpose(mt(k * P, (k + 1) * P), mp[:, k * GH:(k + 1) * GH, :].rearrange("p h m -> p (h m)"),
                                               w["ident_b"][:, :])
                last.then_inc(mt_ready, 1)

            def turned_score(turn, r, c, first):
                slot, (k, pair) = r % NSLOT, prob_chunk(c)
                if c == 0:
                    pe.wait_ge(m_placed, upto(turn, r, 16, 16))
                if not (first and c < 2):
                    pe.wait_ge(exp_done, upto(turn, r, N_E, c - 1))
                for j in range(2):
                    h, bank = 2 * pair + j, 2 * (c % 2) + j
                    nc.tensor.matmul(ps[:, bank, 0:S - k * P], ks[slot][0:STACK + MROWS, h, k * P:(k + 1) * P],
                                     qs[slot][0:STACK + MROWS, h, k * P:S], start=True, stop=False)
                    last = nc.tensor.matmul(ps[:, bank, 0:P], w["ident_b"][:, :], w["mask_kq"][:, :], start=False, stop=True)
                last.then_inc(st_ready, 1)

            def values(turn, r, part, start=False):
                slot, k = r % NSLOT, part // 2
                if part == 0:
                    pe.wait_ge(exp_done, upto(turn, r, N_E, N_E))
                    if not start:
                        pe.wait_ge(o_taken, upto(turn, r, 1, 0))
                for h in (2 * (part % 2), 2 * (part % 2) + 1):
                    last = nc.tensor.matmul(ps[h * QUAD:h * QUAD + HD + 1, 6, k * P:S], vs[slot][:, k, h, :],
                                            pt[r % 2][:, h, START[k]:START[k + 1]], start=(k == 0), stop=(k == NBLK - 1),
                                            skip_group_check=True)
                if part == 2 * NBLK - 1:
                    last.then_inc(pv_ready, 1)

            def unit(turn, r, first):
                for c in range(N_E):
                    turned_score(turn, r, c, first == 0)
                    for i in range(2):
                        if c < MID and follows(turn, r, 1):
                            score(turn, r + 1, N_S // 2 + 2 * c + i)
                        elif c >= MID and follows(turn, r, 2):
                            score(turn, r + 2, 2 * (c - MID) + i)
                    if first != 0:
                        values(turn, r - 1, c, start=(first == 1))
                    if c == TURN_MAX and follows(turn, r, 1):
                        turn_max(turn, r + 1)

            for c in range(N_S):
                score(0, 0, c, start=True)
            turn_max(0, 0)
            for c in range(N_S // 2):
                score(0, 1, c)
            units(pe, unit)
            for part in range(2 * NBLK):
                values(TURNS - 1, NSLOT - 1, part)

        @block.scalar
        def _(act):
            def copy_max(turn, r):
                act.wait_ge(mt_ready, upto(turn, r, 1, 1))
                nc.scalar.activation(turned[r % 2][STACK:STACK + MROWS, :], mt(0, S), ACT.Copy).then_inc(m_copied, 1)

            def take_out(turn, r, start=False):
                if not start:
                    act.wait_ge(o_stored[r % 2], upto(turn, r - r % 2, GH * 16 // 2, 0))
                act.wait_ge(pv_ready, upto(turn, r, 1, 1))
                nc.scalar.activation(ot[r % 2][:, :], ps[:, 6, :], ACT.Copy).then_inc(o_taken, 1)

            def unit(turn, r, first):
                for c in range(N_E):
                    k, pair = prob_chunk(c)
                    act.wait_ge(st_ready, upto(turn, r, N_E, c + 1))
                    bank = 2 * (c % 2)
                    nc.scalar.activation(pt[r % 2][:, 2 * pair:2 * pair + 2, START[k]:START[k + 1]],
                                         ps[:, bank:bank + 2, 0:S - k * P], ACT.Exp, scale=float(HD) ** -0.5).then_inc(exp_done, 1)
                    if c == TURN_MAX and follows(turn, r, 1):
                        copy_max(turn, r + 1)
                if first != 0:
                    take_out(turn, r - 1, start=(first == 1))

            copy_max(0, 0)
            unit(0, 0, 0)
            unit(0, 1, 1)
            unit(0, 2, 2)
            with act.Fori(0, TURNS - 1) as turn:
                for r in range(3, NSLOT + 3):
                    unit(turn, r, None)
            for r in range(3, NSLOT):
                unit(TURNS - 1, r, None)
            take_out(TURNS - 1, NSLOT - 1)

        @block.vector
        def _(dve):
            nc.vector.memset(ps[:, 6, :], 0.0).then_inc(preset, 1)
            for n in range(NSLOT):
                last = nc.vector.tensor_copy(
                    ks[n][STACK:STACK + MROWS, :, :],
                    cst[STACK:STACK + MROWS, slice(*col["own_max"])].unsqueeze(2).broadcast_to([MROWS, GH, S]))
            last.then_inc(preset, 1)

            def maxima(turn, r, first=None):
                for c in range(N_S):
                    k, h = score_chunk(c)
                    dve.wait_ge(s_ready, upto(turn, r, N_S, c + 1))
                    nc.vector.tensor_reduce(negm[:, k * GH + h:k * GH + h + 1], ps[:, 4 + c % 2, 0:(k + 1) * P], AXX, ALU.max, negate=True).then_inc(s_taken, 1)
                dve.wait_ge(s_taken, upto(turn, r, N_S, N_S))
                nc.vector.tensor_copy(mp[:, :, 0], negm[:, :]).then_inc(m_step, 1)
                dve.wait_ge(m_step, upto(turn, r, 3, 1))
                nc.vector.tensor_tensor(mrest[:, :], negm[:, :], mp[:, :, 0], ALU.subtract).then_inc(m_step, 1)
                dve.wait_ge(m_step, upto(turn, r, 3, 2))
                nc.vector.tensor_copy(mp[:, :, 1], mrest[:, :]).then_inc(m_step, 1)
                dve.wait_ge(m_step, upto(turn, r, 3, 3))
                nc.vector.tensor_tensor(mp[:, :, 2], mrest[:, :], mp[:, :, 1], ALU.subtract).then_inc(m_split, 1)

            units(dve, maxima)


def tokens(ap, b):
    return ap[bass.ds(b, 1), :, :].rearrange("a (k p) c -> p (a k) c", p=P)


def gate_layer0(nc, ps, seen, w, cst, col, A, o_dram, inv_dram, x1_dram):
    N_LOAD = 4 * KC
    with ExitStack() as ctx:
        t = Scope(nc, ctx)
        x, x1 = ([t.sb(f"g_{n}{p}", [P, NBLK, HID]) for p in range(PAR)] for n in ("x", "x1"))
        oT, sums = ([[t.sb(f"g_{n}{p}{kind}", [P, KC, S]) for kind in range(2)] for p in range(PAR)] for n in ("oT", "sum"))
        all_sums = t.sb("g_all_sums", [P, 2, S])
        e = [t.sb(f"g_e{p}", [P, 2 * S]) for p in range(PAR)]
        one = t.sb("g_one", [P, 1])
        g = [t.sb(f"g_g{p}", [P, 2 * S]) for p in range(PAR)]
        sums_in, inverted, inverse_out = (t.sem("g_" + n) for n in ("sums_in", "inverted", "inverse_out"))
        loaded, x_in, x1_out = ([t.sem(f"g_{n}{p}") for p in range(PAR)] for n in ("loaded", "x_in", "x1_out"))
        scaled, projected, gated, x1_ready = (t.sem("g_" + n) for n in ("scaled", "projected", "gated", "x1_ready"))
        sig_step, log_ready, by_gate, preset = (t.sem("g_" + n) for n in ("sig_step", "log_ready", "by_gate", "preset"))
        block = ctx.enter_context(nc.Block())

        @block.sync
        def _(sp):
            def load_x(turn, p):
                sp.dma_start(x[p % PAR][:, :, :], tokens(A["x"], turn * PAR + p)).then_inc(x_in[p % PAR], 16)

            def load(turn, p):
                b, q = turn * PAR + p, p % PAR
                for kind in (ATTN, FFN):
                    for c in range(KC):
                        heads = o_dram[kind][bass.ds(b * H + c * (P // HD), P // HD), :, :]
                        sp.dma_start(oT[q][kind][:, c, :], heads[:, 0:HD, :]).then_inc(loaded[q], 16)
                        sp.dma_start(sums[q][kind][:, c, :],
                                     inv_dram[kind][bass.ds(b * H + c * (P // HD), P // HD), :]
                                     .unsqueeze(1).broadcast_to([P // HD, HD, S])).then_inc(loaded[q], 16)

            def store(turn, p):
                sp.wait_ge(x1_ready, upto(turn, p, 1, 1))
                sp.dma_start(tokens(x1_dram, turn * PAR + p), x1[p][:, :, :]).then_inc(x1_out[p], 16)

            for kind in (ATTN, FFN):
                sp.dma_start(all_sums[:, kind, :], o_dram[kind][:, HD:HD + 1, :].rearrange("h a n -> h (a n)")).then_inc(sums_in, 16)
            for kind in (ATTN, FFN):
                sp.wait_ge(inverted, kind + 1)
                sp.dma_start(inv_dram[kind], all_sums[:, kind, :]).then_inc(inverse_out, 16)
            sp.wait_ge(inverse_out, 32)
            for p in range(PAR):
                load(0, p)
                load_x(0, p)
            with sp.Fori(0, B // PAR - 1) as turn:
                for p in range(PAR):
                    sp.wait_ge(projected, upto(turn, p, 2, 2))
                    load(turn, p + PAR)
                    store(turn, p)
                    load_x(turn, p + PAR)
            for p in range(PAR):
                store(B // PAR - 1, p)
                sp.wait_ge(x1_out[p], B // PAR * 16)

        @block.gpsimd
        def _(pool):
            def scale(turn, p):
                wait_apart(pool, loaded[p % PAR], (turn + p // PAR) * (16 * N_LOAD) + 16 * N_LOAD, seen)
                for kind in (ATTN, FFN):
                    nc.gpsimd.tensor_tensor(oT[p % PAR][kind][:, :, :], oT[p % PAR][kind][:, :, :],
                                            sums[p % PAR][kind][:, :, :], ALU.mult).then_inc(scaled, 1)

            def batch(turn, p, last):
                if not last:
                    scale(turn, p + 1)
                if not early(turn):
                    wait_apart(pool, x1_out[p], turn * 16, seen)
                wait_apart(pool, x_in[p], turn * 16 + 16, seen)
                wait_apart(pool, gated, upto(turn, p, 1, 1), seen)
                nc.gpsimd.tensor_tensor(x1[p][:, :, :].rearrange("p k c -> p (k c)"), x[p][:, :, :].rearrange("p k c -> p (k c)"),
                                        g[p][:, :], ALU.add).then_inc(x1_ready, 1)

            by_pairs(pool, scale, batch)

        @block.tensor
        def _(pe):
            def batch(turn, p, last):
                for kind in (ATTN, FFN):
                    pe.wait_ge(scaled, upto(turn, p, 2, kind + 1))
                    if kind == 0 and not early(turn):
                        pe.wait_ge(x1_ready, upto(turn, p, 1, 1 - PAR))
                    wo = w["o_a"] if kind == ATTN else w["o_f"]
                    for k in range(NBLK):
                        for c in range(KC):
                            last_mm = nc.tensor.matmul(ps[:, 4 * p + 2 * kind + k // 2, (k % 2) * HID:(k % 2 + 1) * HID],
                                                       oT[p][kind][:, c, k * P:(k + 1) * P], wo[:, c, :], start=(c == 0), stop=(c == KC - 1))
                    last_mm.then_inc(projected, 1)

            by_pairs(pe, None, batch)

        @block.scalar
        def _(act):
            act.wait_ge(preset, 1)

            def batch(turn, p, last):
                act.wait_ge(projected, upto(turn, p, 2, 2))
                if not early(turn):
                    act.wait_ge(by_gate, upto(turn, p, 1, 1 - PAR))
                sigmoid(act, nc, e[p][:, :], ps[:, 4 * p + 2:4 * p + 4, :].rearrange("p k n -> p (k n)"), one, sig_step, log_ready, turn, p)

            by_pairs(act, None, batch)

        @block.vector
        def _(dve):
            nc.vector.memset(one[:, :], 1.0).then_inc(preset, 1)
            dve.wait_ge(sums_in, 32)
            for kind in (ATTN, FFN):
                nc.vector.reciprocal(all_sums[:, kind, :], all_sums[:, kind, :]).then_inc(inverted, 1)

            def batch(turn, p, last):
                s_ps, y_ps = (ps[:, at:at + 2, :].rearrange("p k n -> p (k n)") for at in (4 * p, 4 * p + 2))
                dve.wait_ge(projected, upto(turn, p, 2, 2))
                log_sigmoid(dve, nc, e[p][:, :], y_ps, sig_step, log_ready, turn, p)
                if not early(turn):
                    dve.wait_ge(x1_ready, upto(turn, p, 1, 1 - PAR))
                nc.vector.tensor_tensor(g[p][:, :], y_ps, e[p][:, :], ALU.mult).then_inc(by_gate, 1)
                dve.wait_ge(by_gate, upto(turn, p, 1, 1))
                nc.vector.tensor_tensor(g[p][:, :], s_ps, g[p][:, :], ALU.mult).then_inc(gated, 1)

            by_pairs(dve, None, batch)


def recur_layer1(nc, ps, seen, col, A, x1_dram, s1_dram):
    NGRP = 4
    NPAIR = NSEG // 2
    WB = DK + 1
    with ExitStack() as ctx:
        t = Scope(nc, ctx)
        cst = t.sb("cst1", [P, A["consts1"].shape[1]])
        wq, wk, wv = (t.sb("m_" + n, [P, KC, NGRP * GH * DK]) for n in ("wq", "wk", "wv"))
        NJ = NGRP * GH
        wo = t.sb("m_wo", [P, NJ, HID])
        share = t.sb("m_share", [P, 2, NGRP * GH])
        se = t.sb("m_se", [P, NGRP * GH])
        ident_b = t.sb("m_ident_b", [P, P], BF16)
        mask_b = t.sb("m_mask_b", [P, P], BF16)
        xs = t.sb("m_xs", [P, NBLK, HID])
        stats = t.sb("m_stats", [P, NBLK, 6])
        mv = t.sb("m_mv", [P, NBLK, 2])
        rstd = t.sb("m_rstd", [P, NBLK])
        power = t.sb("m_power", [P, NBLK])
        xT = t.sb("m_xT", [P, KC, S])
        qT = t.sb("m_qT", [P, S])
        kT = t.sb("m_kT", [P, S])
        eq, ek = t.sb("m_eq", [P, S]), t.sb("m_ek", [P, S])
        sk = t.sb("m_sk", [P, S])
        sg = [[t.sb(f"m_sg{g}{h}", [P, NPAIR, 4, SEG]) for h in range(GH)] for g in range(2)]
        kn = [t.sb(f"m_kn{g}", [P, GH, NPAIR, DK]) for g in range(2)]
        v = [t.sb(f"m_v{g}", [P, NPAIR, GH, DK]) for g in range(2)]
        am = [t.sb(f"m_am{g}", [P, NPAIR, GH, DK]) for g in range(2)]
        at = [t.sb(f"m_at{g}", [P, GH, S]) for g in range(NGRP)]
        pr = t.sb("m_pr", [P, NPAIR, P])
        prT = t.sb("m_prT", [P, S])
        negm, psum_, prec = t.sb("m_negm", [P, NPAIR]), t.sb("m_psum", [P, NPAIR]), t.sb("m_prec", [P, NPAIR])
        mem = t.sb("m_mem", [P, GH, WB])
        rd = t.sb("m_rd", [P, GH])
        tmp = t.sb("m_tmp", [P, GH, DK])
        delta = t.sb("m_delta", [P, GH, WB])
        acc = t.sb("m_acc", [P, HID])

        w_in, preset, share_step = t.sem("w_in"), t.sem("m_preset"), t.sem("share_step")
        share_clip, share_exp, share_ready = t.sem("share_clip"), t.sem("share_exp"), t.sem("share_ready")
        stat_ready, power_set = t.sem("m_stat_ready"), t.sem("m_power_set")
        x_in, var_ready, eps_added, rstd_ready, xn_ready, xt_psum, xt_ready = (
            t.sem("m_" + n) for n in ("x_in", "var_ready", "eps_added", "rstd_ready", "xn_ready", "xt_psum", "xt_ready"))
        proj_ready, qk_ready, min_ready, exp_ready, sigq_ready, sigk_ready, sigk_placed = (
            t.sem(n) for n in ("proj_ready", "qk_ready", "min_ready", "exp_ready", "sigma_q_ready", "sigma_k_ready", "sigma_k_placed"))
        v_psum, v_ready, kn_psum, kn_ready = (t.sem(n) for n in ("v_psum1", "v_ready1", "kn_psum", "kn_ready"))
        sc_ready, max_raw, max_ready, p_ready, rs_ready, pn_ready = (
            t.sem(n) for n in ("sc_ready", "max_raw", "max_ready", "p_ready", "rs_ready", "pn_ready"))
        pt_psum, pt_ready, bt_psum, bt_ready = (t.sem(n) for n in ("pt_psum", "pt_ready", "bt_psum", "bt_ready"))
        d_ready, rd_ready, tmp_ready, delta_ready, read_done, u_ready, mem_ready = (
            t.sem(n) for n in ("d_ready", "rd_ready", "tmp_ready", "delta_ready", "read_done", "u_ready", "mem_ready"))
        am_psum, at_ready, out_psum, acc_ready, stored = (
            t.sem(n) for n in ("am_psum", "at_ready", "out_psum1", "acc_ready", "s_stored"))
        def group_in(g):
            return 16 * (2 + 3 * (g + 1))

        ALL_IN = group_in(NGRP - 1) + 16
        END_BANKS = (5, 4, 0, 1)
        NUPD = NSEG - 1
        block = ctx.enter_context(nc.Block())

        class Group:

            def __init__(self, b, g):
                self.b, self.g = b + g // NGRP, g % NGRP
                self.par = g % 2
                self._b, self._g = b, g

            def upto(self, per, c):
                return self._b * (NGRP * per) + (self._g * per + c)

            def head(self, h):
                return self.g * GH + h

            @property
            def first(self):
                return isinstance(self._b, int) and self._b == 0 and self._g == 0

        def khalf(s):
            return slice(SEG * (s % 2), SEG * (s % 2) + SEG)

        def qhalf(s):
            return khalf(s + 1)

        def region(lo, hi, part=slice(0, P)):
            return ps[part, 0:2, :].rearrange("p b (h c) -> p (b h) c", h=2)[:, :, lo:hi]

        def windows(turn, last):
            for g in range(NGRP):
                n = Group(turn, g)
                yield n, (None if last and g == NGRP - 1 else Group(turn, g + 1)), (None if n.first else Group(turn, g - 1))

        def run(eng, prologue, window):
            prologue()
            window(None, Group(0, 0), None)
            for n, m, o in windows(0, False):
                window(n, m, o)
            with eng.Fori(1, B - 1) as turn:
                for n, m, o in windows(turn, False):
                    window(n, m, o)
            for n, m, o in windows(B - 1, True):
                window(n, m, o)

        @block.sync
        def _(sp):
            sp.dma_start(xs[:, :, :], tokens(x1_dram, 0)).then_inc(x_in, 16)
            sp.dma_start(cst[:, :], A["consts1"]).then_inc(w_in, 16)
            with nc.allow_non_contiguous_dma(reason="2048 words, once"):
                sp.dma_start(share[:, 0, :], A["betas"].rearrange("a h b p -> p (a h b)")).then_inc(w_in, 16)
            for g in range(NGRP):
                cols = slice(g * GH * DK, (g + 1) * GH * DK)
                for dst, src in ((wq, A["Wq"]), (wk, A["Wk"]), (wv, A["Wv"])):
                    sp.dma_start(dst[:, :, cols], src[:, cols].rearrange("(k p) n -> p k n", p=P)).then_inc(w_in, 16)
                sp.wait_ge(w_in, group_in(g))
            sp.dma_start(wo[:, :, :], A["Wo"].rearrange("(h p) n -> p h n", p=P)).then_inc(w_in, 16)
            sp.sem_inc(stored, 16)
            def store(b, g):
                sp.wait_ge(acc_ready, b * NGRP + (g + 1))
                rows = s1_dram[bass.ds(b, 1), :, :].rearrange("a (s g h r) c -> g h (a s) r c", s=NSEG, g=NGRP, h=GH)
                for h in range(GH):
                    sp.dma_start(rows[g, h], acc[h * NSEG * 4:(h + 1) * NSEG * 4, :]).then_inc(stored, 16)

            with sp.Fori(0, B - 1) as b:
                sp.wait_ge(xt_psum, b + 1)
                sp.dma_start(xs[:, :, :], tokens(x1_dram, b + 1)).then_inc(x_in, 16)
                for g in range(NGRP):
                    store(b, g)
            for g in range(NGRP):
                store(B - 1, g)
            sp.wait_ge(stored, 16 * (1 + B * NGRP * GH))

        @block.gpsimd
        def _(pool):
            nc.gpsimd.memset(power[:, :], -0.5).then_inc(power_set, 1)
            pool.wait_ge(power_set, 1)

            def inv_std(b):
                wait_apart(pool, var_ready, b + 1, seen)
                nc.gpsimd.tensor_scalar(rstd[:, :], mv[:, :, 1], EPS, None, ALU.add).then_inc(eps_added, 1)
                pool.wait_ge(eps_added, b + 1)
                nc.gpsimd.tensor_tensor(rstd[:, :], rstd[:, :], power[:, :], ALU.pow).then_inc(rstd_ready, 1)

            def place_keys(m, h):
                wait_apart(pool, sigk_ready, m.upto(GH, h + 1), seen)
                nc.gpsimd.tensor_copy(sg[m.par][h][:, :, 0:4:3, :], sk[:, :].rearrange("p (a b c) -> p a b c", a=NPAIR, b=2)).then_inc(sigk_placed, 1)

            def normalise(m, h):
                pool.wait_ge(rs_ready, m.upto(GH, h + 1))
                p = pr
                nc.gpsimd.tensor_tensor(p[:, :, :], p[:, :, :], prec[:, :].unsqueeze(2).broadcast_to([P, NPAIR, P]), ALU.mult).then_inc(pn_ready, 1)

            def window(n, m, o):
                if n is not None:
                    normalise(n, GH - 1)
                if m is not None:
                    for h in range(GH):
                        place_keys(m, h)
                        if h < GH - 1:
                            normalise(m, h)
                if n is not None and n.g == 1 and not (isinstance(n.b, int) and n.b == B - 1):
                    inv_std(n.b + 1)

            run(pool, lambda: inv_std(0), window)

        @block.tensor
        def _(pe):
            ident = cst[:, slice(*col["ident"])]

            def product(out, pairs):
                for i, (lhsT, rhs) in enumerate(pairs):
                    last = nc.tensor.matmul(out, lhsT, rhs, start=(i == 0), stop=(i == len(pairs) - 1))
                return last

            def turn_x(b, first=False):
                pe.wait_ge(xn_ready, b + 1)
                if not first:
                    pe.wait_ge(qk_ready, (b * NGRP) * (2 * GH))
                for c in range(KC):
                    for k in range(NBLK):
                        last = nc.tensor.transpose(ps[:, 2 + c, k * P:(k + 1) * P], xs[:, k, c * P:(c + 1) * P], ident)
                last.then_inc(xt_psum, 1)

            def project(m, h, bank, c):
                if h == 0 and bank == 2 and c == 0:
                    pe.wait_ge(w_in, group_in(m.g))
                    pe.wait_ge(xt_ready, m.b + 1)
                if c == 0 and not (m.first and h == 0):
                    pe.wait_ge(qk_ready, m.upto(2 * GH, 2 * h + bank - 3))
                weights = wq if bank == 2 else wk
                last = nc.tensor.matmul(ps[:, bank, :], weights[:, c, m.head(h) * DK:(m.head(h) + 1) * DK], xT[:, c, :],
                                        start=(c == 0), stop=(c == KC - 1))
                if c == KC - 1:
                    last.then_inc(proj_ready, 1)

            def project_v(m, k, bank):
                product(ps[:, bank, :], [(xT[:, c, k * P:(k + 1) * P], wv[:, c, m.g * GH * DK:(m.g + 1) * GH * DK])
                                         for c in range(KC)]).then_inc(v_psum, 1)

            PROJECT_FIRST = ((2, 0), (2, 1), (3, 0))

            def turn_keys(m, h):
                pe.wait_ge(sigk_ready, m.upto(GH, h + 1))
                pe.wait_ge(v_ready, m.upto(NBLK, 2 if h == 0 else NBLK))
                if h:
                    pe.wait_ge(kn_ready, m.upto(GH, h))
                for p in range(NPAIR):
                    blk = slice(p * P, (p + 1) * P)
                    last = nc.tensor.transpose(ps[:, 5, blk], sk[:, blk], ident)
                last.then_inc(kn_psum, 1)

            def score(m, h):
                pe.wait_ge(qk_ready, m.upto(2 * GH, 2 * h + 2))
                if not (m.first and h == 0):
                    pe.wait_ge(p_ready, m.upto(GH, h))
                nc.tensor.matmul(ps[:, 6, :].rearrange("p (a c) -> p a c", a=NPAIR), ident_b[:, :],
                                 mask_b[:, :].unsqueeze(1).broadcast_to([P, NPAIR, P]), start=True, stop=False, skip_group_check=True)
                for s in range(NSEG):
                    seg = slice(s * SEG, (s + 1) * SEG)
                    last = nc.tensor.matmul(ps[khalf(s), 6, seg], qT[:, seg], kT[:, seg],
                                            start=False, stop=(s >= NSEG - 2), skip_group_check=True)
                last.then_inc(sc_ready, 1)

            def turn_probs(m, h):
                pe.wait_ge(pn_ready, m.upto(GH, h + 1))
                if not (m.first and h == 0):
                    pe.wait_ge(bt_ready, m.upto(GH, h))
                for p in range(NPAIR):
                    last = nc.tensor.transpose(ps[:, 7, p * P:(p + 1) * P], pr[:, p, :], ident)
                last.then_inc(pt_psum, 1)

            def local(m, h):
                pe.wait_ge(pt_ready, m.upto(GH, h + 1))
                pe.wait_ge(v_ready, m.upto(NBLK, NBLK))
                for p in range(NPAIR):
                    blk = slice(p * P, (p + 1) * P)
                    last = nc.tensor.matmul(ps[:, 7, blk], v[m.par][:, p, h, :], prT[:, blk], start=True, stop=True)
                last.then_inc(bt_psum, 1)

            def read_memory(n, s):
                if s == 0:
                    pe.wait_ge(sigq_ready, n.upto(GH, GH))
                    pe.wait_ge(sigk_placed, n.upto(GH, GH))
                pe.wait_ge(mem_ready, n.upto(NSEG, s + 1))
                for h in range(GH):
                    last = nc.tensor.matmul(region(0, WB)[:, h, :], sg[n.par][h][:, s // 2, 2 * (s % 2):2 * (s % 2) + 2, :].rearrange("p a c -> p (a c)"),
                                            mem[:, h, :], start=True, stop=True)
                last.then_inc(d_ready, 1)

            def write_memory(n, s):
                if s == 0:
                    pe.wait_ge(kn_ready, n.upto(GH, GH))
                pe.wait_ge(delta_ready, n.upto(NUPD, s + 1))
                pe.wait_ge(read_done, n.upto(NSEG, s + 1))
                half = khalf(s)
                for h in range(GH):
                    last = nc.tensor.matmul(region(0, WB)[:, h, :], kn[n.par][half, h, s // 2, :], delta[half, h, :], start=True, stop=True)
                last.then_inc(u_ready, 1)

            def turn_read(o, h, bank):
                pe.wait_ge(read_done, o.upto(NSEG, NSEG))
                for p in range(NPAIR):
                    last = nc.tensor.transpose(ps[:, bank, p * P:(p + 1) * P], am[o.par][:, p, h, :], ident)
                last.then_inc(am_psum, 1)

            def emit(o, j):
                if j == 0:
                    pe.wait_ge(w_in, ALL_IN)
                    pe.wait_ge(at_ready, o.upto(GH, GH))
                heads = at[o.g][:, :, :].rearrange("p h (r j) -> p (h r) j", j=NJ)
                for i in range(j * NJ // 2, (j + 1) * NJ // 2):
                    last = nc.tensor.matmul(ps[:, 4, 0:HID], heads[:, :, i], wo[:, i, :], start=(i == 0), stop=(i == NJ - 1))
                if j:
                    last.then_inc(out_psum, 1)

            def window(n, m, o):
                for s in range(NSEG):
                    if n is not None:
                        read_memory(n, s)
                    if o is not None and s in (0, 2):
                        if s == 0:
                            if n is not None:
                                pe.wait_ge(kn_ready, n.upto(GH, GH))
                            if not o.first:
                                pe.wait_ge(acc_ready, o.upto(1, 0))
                        else:
                            if m is not None:
                                pe.wait_ge(v_ready, m.upto(NBLK, 2))
                                pe.wait_ge(kn_ready, m.upto(GH, 1))
                            else:
                                pe.wait_ge(at_ready, o.upto(GH, 2))
                        turn_read(o, s, 5)
                        turn_read(o, s + 1, 4)
                    if m is not None:
                        if s % 2 == 0:
                            for bank, c in PROJECT_FIRST:
                                project(m, s // 2, bank, c)
                        elif s < 4:
                            if o is not None or (s == 1 and n is not None and not n.first):
                                if s == 1:
                                    if o is not None:
                                        pe.wait_ge(at_ready, o.upto(GH, 2))
                                    else:
                                        pe.wait_ge(acc_ready, n.upto(1, 0))
                                else:
                                    pe.wait_ge(at_ready, o.upto(GH, GH))
                            if s == 3:
                                pe.wait_ge(kn_ready, m.upto(GH, 1))
                                pe.wait_ge(v_ready, m.upto(NBLK, 2))
                            project_v(m, s - 1, 4)
                            project_v(m, s, 5)
                    if o is not None and s in (5, 7):
                        if s == 5 and m is not None:
                            pe.wait_ge(v_ready, m.upto(NBLK, NBLK))
                        emit(o, (s - 5) // 2)
                    if n is not None and s < NUPD:
                        write_memory(n, s)
                    if m is not None and s % 2 == 0:
                        project(m, s // 2, 3, KC - 1)
                    if n is not None and s == 0:
                        turn_probs(n, GH - 1)
                    if n is not None and s == 1:
                        local(n, GH - 1)
                    if m is not None and s % 2 == 0 and s:
                        turn_probs(m, s // 2 - 1)
                    if m is not None and s % 2:
                        score(m, s // 2)
                        if s > 1:
                            local(m, s // 2 - 1)
                        turn_keys(m, s // 2)
                if n is not None and n.g == 2 and m is not None and not (isinstance(n.b, int) and n.b == B - 1):
                    turn_x(n.b + 1)
                if n is not None and m is None:
                    pe.wait_ge(acc_ready, n.upto(1, 0))
                    for h, bank in enumerate(END_BANKS):
                        turn_read(n, h, bank)
                    emit(n, 0)
                    emit(n, 1)

            def prologue():
                pe.wait_ge(preset, 2)
                pe.wait_ge(w_in, group_in(0))
                turn_x(0, first=True)

            run(pe, prologue, window)

        @block.scalar
        def _(act):
            def take_x(b):
                act.wait_ge(xt_psum, b + 1)
                nc.scalar.activation(xT[:, :, :], ps[:, 2:4, :], ACT.Copy).then_inc(xt_ready, 1)

            def take_qk(m, h):
                for i, dst in enumerate((qT, kT)):
                    act.wait_ge(proj_ready, m.upto(2 * GH, 2 * h + i + 1))
                    nc.scalar.activation(dst[:, :], ps[:, 2 + i, :], ACT.Copy).then_inc(qk_ready, 1)
                for i, e in enumerate((eq, ek)):
                    act.wait_ge(min_ready, m.upto(2 * GH, 2 * h + i + 1))
                    nc.scalar.activation(e[:, :], e[:, :], ACT.Exp).then_inc(exp_ready, 1)

            def take_v(m, k, bank):
                act.wait_ge(v_psum, m.upto(NBLK, k + 1))
                nc.scalar.activation(v[m.par][:, k, :, :].rearrange("p h c -> p (h c)"), ps[:, bank, :], ACT.Copy).then_inc(v_ready, 1)

            def take_keys(m, h):
                act.wait_ge(kn_psum, m.upto(GH, h + 1))
                nc.scalar.activation(kn[m.par][:, h, :, :].rearrange("p a c -> p (a c)"), ps[:, 5, :], ACT.Copy).then_inc(kn_ready, 1)

            def probabilities(m, h):
                act.wait_ge(max_ready, m.upto(GH, h + 1))
                for p in range(NPAIR):
                    last = nc.scalar.activation(pr[:, p, :], ps[:, 6, p * P:(p + 1) * P], ACT.Exp,
                                                bias=negm[:, p:p + 1], scale=float(DK) ** -0.5, accum_out=psum_[:, p:p + 1])
                last.then_inc(p_ready, 1)

            def take_turned_probs(m, h):
                act.wait_ge(pt_psum, m.upto(GH, h + 1))
                nc.scalar.activation(prT[:, :], ps[:, 7, :], ACT.Copy).then_inc(pt_ready, 1)

            def take_local(m, h):
                act.wait_ge(bt_psum, m.upto(GH, h + 1))
                nc.scalar.activation(at[m.g][:, h, :], ps[:, 7, :], ACT.Copy, scale=share[:, 1, m.head(h):m.head(h) + 1]).then_inc(bt_ready, 1)

            def take_read(n, s):
                act.wait_ge(rd_ready, n.upto(NSEG, s + 1))
                half = qhalf(s)
                for h in range(GH):
                    last = nc.scalar.activation(am[n.par][half, s // 2, h, :], region(0, DK, half)[:, h, :], ACT.Copy, scale=rd[half, h:h + 1])
                last.then_inc(read_done, 1)

            def take_out(o):
                act.wait_ge(out_psum, o.upto(1, 1))
                act.wait_ge(stored, o.upto(16 * GH, 16))
                nc.scalar.activation(acc[:, :], ps[:, 4, 0:HID], ACT.Copy).then_inc(acc_ready, 1)

            def window(n, m, o):
                for s in range(NSEG):
                    if n is not None:
                        take_read(n, s)
                    if m is not None:
                        if s % 2 == 0:
                            take_qk(m, s // 2)
                        elif s < 4:
                            take_v(m, s - 1, 4)
                            take_v(m, s, 5)
                    if n is not None and s == 0:
                        take_turned_probs(n, GH - 1)
                    if n is not None and s == 1:
                        take_local(n, GH - 1)
                    if m is not None and s % 2 == 0 and s:
                        take_turned_probs(m, s // 2 - 1)
                    if o is not None and s == NSEG - 1:
                        take_out(o)
                    if m is not None and s % 2:
                        if s > 1:
                            take_local(m, s // 2 - 1)
                        take_keys(m, s // 2)
                        probabilities(m, s // 2)
                if n is not None and n.g == 2 and m is not None and not (isinstance(n.b, int) and n.b == B - 1):
                    take_x(n.b + 1)
                if n is not None and m is None:
                    take_out(n)

            def prologue():
                act.wait_ge(share_clip, 1)
                nc.scalar.activation(se[:, :], se[:, :], ACT.Exp).then_inc(share_exp, 1)
                act.wait_ge(share_ready, 1)
                take_x(0)

            run(act, prologue, window)

        @block.vector
        def _(dve):
            def normalise_x(b):
                dve.wait_ge(rstd_ready, b + 1)
                for k in range(NBLK):
                    last = nc.vector.tensor_scalar(xs[:, k, :], xs[:, k, :], mv[:, k, 0:1], rstd[:, k:k + 1], ALU.subtract, ALU.mult)
                last.then_inc(xn_ready, 1)

            def stats_x(b):
                dve.wait_ge(x_in, b * 16 + 16)
                for k in range(NBLK):
                    last = nc.vector.bn_stats(stats[:, k, :], xs[:, k, :])
                last.then_inc(stat_ready, 1)
                wait_apart(dve, stat_ready, b + 1, seen)
                for k in range(NBLK):
                    last = nc.vector.bn_aggr(mv[:, k, :], stats[:, k, :])
                last.then_inc(var_ready, 1)
                dve.wait_ge(var_ready, b + 1)

            def pairs(x):
                return x[:, :].rearrange("p (a c) -> p a c", a=NPAIR)

            def sigma(m, h):
                for i, (x, e) in enumerate(((qT, eq), (kT, ek))):
                    dve.wait_ge(qk_ready, m.upto(2 * GH, 2 * h + i + 1))
                    nc.vector.tensor_scalar(e[:, :], x[:, :], 0.0, None, ALU.min).then_inc(min_ready, 1)
                dve.wait_ge(exp_ready, m.upto(2 * GH, 2 * h + 1))
                nc.vector.scalar_tensor_tensor(sg[m.par][h][:, :, 1:3, :].rearrange("p a b c -> p a (b c)"), pairs(qT), 1.0,
                                               pairs(eq), ALU.add, ALU.max).then_inc(sigq_ready, 1)
                dve.wait_ge(exp_ready, m.upto(2 * GH, 2 * h + 2))
                if not (m.first and h == 0):
                    dve.wait_ge(sigk_placed, m.upto(GH, h))
                nc.vector.scalar_tensor_tensor(sk[:, :], kT[:, :], 1.0, ek[:, :], ALU.add, ALU.max).then_inc(sigk_ready, 1)

            def maximum(m, h):
                dve.wait_ge(sc_ready, m.upto(GH, h + 1))
                nc.vector.tensor_reduce(negm[:, :], ps[:, 6, :].rearrange("p (a c) -> p a c", a=NPAIR), AXX, ALU.max, negate=True).then_inc(max_raw, 1)
                dve.wait_ge(max_raw, m.upto(GH, h + 1))
                nc.vector.tensor_scalar(negm[:, :], negm[:, :], float(DK) ** -0.5, None, ALU.mult).then_inc(max_ready, 1)

            def inv_sum(m, h):
                dve.wait_ge(p_ready, m.upto(GH, h + 1))
                nc.vector.reciprocal(prec[:, :], psum_[:, :]).then_inc(rs_ready, 1)

            def reset_memory(n):
                if not n.first:
                    dve.wait_ge(read_done, n.upto(NSEG, 0))
                nc.vector.memset(mem[:, :, 0:DK], 0.0)
                nc.vector.memset(mem[:, :, DK:WB], 1.0 / DK).then_inc(mem_ready, 1)

            def change(n, s):
                dve.wait_ge(d_ready, n.upto(NSEG, s + 1))
                nc.vector.reciprocal(rd[:, :], region(DK, WB)[:, :, 0]).then_inc(rd_ready, 1)
                if s == NUPD:
                    return
                half = khalf(s)
                dve.wait_ge(rd_ready, n.upto(NSEG, s + 1))
                nc.vector.tensor_tensor(tmp[half, :, :], region(0, DK, half), rd[half, :].unsqueeze(2).broadcast_to([SEG, GH, DK]), ALU.mult).then_inc(tmp_ready, 1)
                if s == 0:
                    dve.wait_ge(v_ready, n.upto(NBLK, NBLK))
                dve.wait_ge(tmp_ready, n.upto(NUPD, s + 1))
                nc.vector.tensor_tensor(delta[half, :, 0:DK], v[n.par][half, s // 2, :, :], tmp[half, :, :], ALU.subtract).then_inc(delta_ready, 1)

            def update(n, s):
                dve.wait_ge(u_ready, n.upto(NUPD, s + 1))
                dve.wait_ge(mem_ready, n.upto(NSEG, s + 1))
                nc.vector.tensor_tensor(mem[:, :, :], region(0, WB), mem[:, :, :], ALU.add).then_inc(mem_ready, 1)

            def add_read(o, h, bank):
                dve.wait_ge(am_psum, o.upto(GH, h + 1))
                dve.wait_ge(bt_ready, o.upto(GH, h + 1))
                read = ps[:, bank, :].rearrange("p (a b c) -> p a b c", a=NPAIR, b=2)
                sum_ = at[o.g][:, h, :].rearrange("p (a b c) -> p a b c", a=NPAIR, b=2)
                for i in range(2):
                    last = nc.vector.scalar_tensor_tensor(sum_[:, :, i, :], read[:, :, 1 - i, :], share[:, 0, o.head(h):o.head(h) + 1],
                                                          sum_[:, :, i, :], ALU.mult, ALU.add)
                last.then_inc(at_ready, 1)

            def window(n, m, o):
                for s in range(NSEG):
                    if n is not None:
                        change(n, s)
                    if o is not None and s in (0, 2):
                        add_read(o, s, 5)
                        add_read(o, s + 1, 4)
                    if n is not None:
                        if s == 0:
                            inv_sum(n, GH - 1)
                    if m is not None and s % 2 == 0 and s:
                        inv_sum(m, s // 2 - 1)
                    if n is not None and s < NUPD:
                        update(n, s)
                    if m is not None:
                        if s % 2 == 0:
                            sigma(m, s // 2)
                        else:
                            maximum(m, s // 2)
                    if n is not None and n.g in (1, 2) and m is not None and s == 4 and not (isinstance(n.b, int) and n.b == B - 1):
                        if n.g == 1:
                            stats_x(n.b + 1)
                        else:
                            normalise_x(n.b + 1)
                if m is not None:
                    reset_memory(m)
                if n is not None and m is None:
                    for h, bank in enumerate(END_BANKS):
                        add_read(n, h, bank)

            def prologue():
                link = Chain(dve, share_step)
                nc.vector.memset(delta[:, :, DK:WB], 1.0).then_inc(preset, 1)
                dve.wait_ge(w_in, group_in(0))
                nc.vector.tensor_copy(ident_b[:, :], cst[:, slice(*col["ident"])])
                nc.vector.tensor_copy(mask_b[:, :], cst[:, slice(*col["mask_seg"])]).then_inc(preset, 1)
                nc.vector.tensor_scalar(se[:, :], share[:, 0, :], -1.0, 80.0, ALU.mult, ALU.min).then_inc(share_clip, 1)
                dve.wait_ge(share_exp, 1)
                link(nc.vector.tensor_scalar(se[:, :], se[:, :], 1.0, None, ALU.add))
                link(nc.vector.reciprocal(share[:, 0, :], se[:, :]))
                nc.vector.tensor_scalar(share[:, 1, :], share[:, 0, :], -1.0, 1.0, ALU.mult, ALU.add).then_inc(share_ready, 1)
                stats_x(0)
                normalise_x(0)

            run(dve, prologue, window)

def mix_layer1(nc, ps, seen, col, A, x1_dram, s1_dram, out):
    NT = NBLK * NTILE
    TAB = 2 * SLICE * GRID + 3
    U_MAX = float(np.float32(1.0 - 1e-6))
    with ExitStack() as ctx:
        t = Scope(nc, ctx)
        cst = t.sb("cst2", [P, A["consts2"].shape[1]])
        w1, w2 = ([t.sb(f"f_{n}{p}", [P, NBLK, HID]) for p in range(PAR)] for n in ("w1", "w2"))
        xs, xf, s1 = ([t.sb(f"f_{n}{p}", [P, NBLK, HID]) for p in range(PAR)] for n in ("xs", "xf", "s1"))
        xn, sg = (t.sb("f_" + n, [P, NBLK, HID]) for n in ("xn", "sg"))
        xn_all = t.sb("f_xn_all", [P, B, NBLK * HID])
        hot_all = t.sb("f_hot_all", [P, B, NT])
        hotT_all = t.sb("f_hotT_all", [NTILE, B, S])
        sl_all = t.sb("f_sl_all", [P, B, NBLK * SLICE])
        slopes = t.sb("f_slopes", [P, NTILE * SLICE, GRID])
        want = t.sb("f_want", [P, NTILE * SLICE])
        gamma, beta = t.sb("f_gamma", [P, HID]), t.sb("f_beta", [P, HID])
        table = t.sb("f_table", [NTILE, TAB])
        stats, mv = t.sb("f_stats", [P, NBLK, 6]), t.sb("f_mv", [P, NBLK, 2])
        rstd, power = t.sb("f_rstd", [P, NBLK]), t.sb("f_power", [P, NBLK])
        one = t.sb("f_one", [P, 1])
        ts, hot, pen, lo, hi = (t.sb("f_" + n, [P, NT]) for n in ("ts", "hot", "pen", "lo", "hi"))
        cs, ch = t.sb("f_cs", [P, NBLK * NCLUSTER]), t.sb("f_ch", [P, NBLK * NCLUSTER])
        top = t.sb("f_top", [P, NBLK])
        ends = t.sb("f_ends", [P, 2, NBLK])
        least, most = t.sb("f_least", [P, NT]), t.sb("f_most", [P, NT])
        ends64 = t.sb("f_ends64", [P, 2, NTILE])
        hotT = [t.sb(f"f_hotT{p}", [NTILE, S]) for p in range(PAR)]
        sl, dl = t.sb("f_sl", [P, NBLK * SLICE]), t.sb("f_dl", [P, NBLK * SLICE])
        tab = t.sb("f_tab", [P, NBLK, 3])
        rng = t.sb("f_rng", [P, NBLK])
        d, ge, in_, val = (t.sb("f_" + n, [P, NBLK * SLICE, GRID]) for n in ("d", "ge", "in", "val"))

        w_in, preset, want_step = t.sem("f_w_in"), t.sem("f_preset"), t.sem("f_want_step")
        x_in = [t.sem(f"f_x_in{p}") for p in range(PAR)]
        stat_ready, var_ready, pool_step, rstd_ready = (t.sem("f_" + n) for n in ("stat_ready", "var_ready", "pool_step", "rstd_ready"))
        xn_ready, xn_copied, xf_normed, xf_ready = (t.sem("f_" + n) for n in ("xn_ready", "xn_copied", "xf_normed", "xf_ready"))
        sign_ready, agreed, hot_ready, hot_psum, hot_turned, hot_copied = (
            t.sem("f_" + n) for n in ("sign_ready", "agreed", "hot_ready", "hot_psum", "hot_turned", "hot_copied"))
        step = t.sem("f_step")
        norm_in = t.sem("f_norm_in")
        N_W = 5
        first = ExitStack()
        block = first.enter_context(nc.Block())

        def per_block(ap):
            return ap.rearrange("p (k n) -> p k n", k=NBLK)

        def cells(x):
            return x[:, :, :].rearrange("p (k j) g -> p k (j g)", k=NBLK)

        def flat(x):
            return x[:, :, :].rearrange("p k c -> p (k c)")

        def final(turn):
            return isinstance(turn, int) and turn == B // PAR - 1

        class Links:

            def __init__(self, dve, sem, total, turn, p):
                self.dve, self.sem, self.total, self.turn, self.p, self.n = dve, sem, total, turn, p, 0

            def __call__(self, ins):
                self.n += 1
                ins.then_inc(self.sem, 1)
                self.dve.wait_ge(self.sem, upto(self.turn, self.p, self.total, self.n))

            def close(self):
                assert self.n == self.total, (self.n, self.total)

        @block.sync
        def _(sp):
            def load(turn, p):
                sp.dma_start(xs[p % PAR][:, :, :], tokens(x1_dram, turn * PAR + p)).then_inc(x_in[p % PAR], 16)

            load(0, 0)
            for dst, src in ((gamma, A["gamma"]), (beta, A["beta"])):
                sp.dma_start(dst[:, :], src.unsqueeze(0).broadcast_to([P, HID])).then_inc(norm_in, 16)
            load(0, 1)
            for dst, src in (
                (cst[:, :], A["consts2"]),
                (slopes[:, :, :].rearrange("p a g -> p (a g)"), A["slopes"].rearrange("(o t) j g -> o (t j g)", o=1).broadcast_to([P, NTILE * SLICE * GRID])),
                (table[:, 0:SLICE * GRID], A["bases"].rearrange("t j g -> t (j g)")),
                (table[:, SLICE * GRID:2 * SLICE * GRID], A["slopes"].rearrange("t j g -> t (j g)")),
                (table[:, 2 * SLICE * GRID:2 * SLICE * GRID + 1], A["oscale"].unsqueeze(1)),
            ):
                sp.dma_start(dst, src).then_inc(w_in, 16)

            def batch(turn, p, last):
                if not final(turn):
                    sp.wait_ge(xn_ready, upto(turn, p, 1, 1))
                    load(turn, p + PAR)

            by_pairs(sp, None, batch)

        @block.gpsimd
        def _(pool):
            nc.gpsimd.memset(power[:, :], -0.5).then_inc(preset, 1)
            pool.wait_ge(preset, 1)
            pool.wait_ge(norm_in, 32)

            def inputs(turn, p):
                for n in range(2):
                    wait_apart(pool, var_ready, upto(turn, p, 2, n + 1), seen)
                    nc.gpsimd.tensor_scalar(rstd[:, :], mv[:, :, 1], EPS, None, ALU.add).then_inc(pool_step, 1)
                    wait_apart(pool, pool_step, upto(turn, p, 3, n + 1), seen)
                    nc.gpsimd.tensor_tensor(rstd[:, :], rstd[:, :], power[:, :], ALU.pow).then_inc(rstd_ready, 1)
                x = xf[p % PAR]
                wait_apart(pool, xf_normed, upto(turn, p, 1, 1), seen)
                nc.gpsimd.tensor_tensor(x[:, :, :], x[:, :, :], gamma[:, :].unsqueeze(1).broadcast_to([P, NBLK, HID]), ALU.mult).then_inc(pool_step, 1)
                wait_apart(pool, pool_step, upto(turn, p, 3, 3), seen)
                nc.gpsimd.tensor_tensor(x[:, :, :], x[:, :, :], beta[:, :].unsqueeze(1).broadcast_to([P, NBLK, HID]), ALU.add).then_inc(xf_ready, 1)

            def batch(turn, p, last):
                if not last:
                    inputs(turn, p + 1)

            by_pairs(pool, inputs, batch)

        @block.tensor
        def _(pe):
            ident = cst[:, slice(*col["ident"])]
            pe.wait_ge(w_in, 16 * N_W)

            def batch(turn, p, last):
                wait_apart(pe, hot_ready, upto(turn, p, 1, 1), seen)
                if not (early(turn) and p == 0):
                    wait_apart(pe, hot_turned, upto(turn, p, 1, 0), seen)
                for k in range(NBLK):
                    done = nc.tensor.transpose(ps[0:NTILE, 0, k * P:(k + 1) * P], hot[:, k * NTILE:(k + 1) * NTILE], ident)
                done.then_inc(hot_psum, 1)

            by_pairs(pe, None, batch)

        @block.scalar
        def _(act):
            def inputs(turn, p):
                act.wait_ge(xn_ready, upto(turn, p, 1, 1))
                nc.scalar.activation(xn_all[:, bass.ds(turn * PAR + p, 1), :], flat(xn).unsqueeze(1), ACT.Copy).then_inc(xn_copied, 1)
                act.wait_ge(xf_ready, upto(turn, p, 1, 1))
                if not (early(turn) and p == 0):
                    act.wait_ge(agreed, upto(turn, p, 1, 0))
                nc.scalar.activation(sg[:, :, :], xf[p % PAR][:, :, :], ACT.Sign).then_inc(sign_ready, 1)

            def batch(turn, p, last):
                if not last:
                    inputs(turn, p + 1)
                b = bass.ds(turn * PAR + p, 1)
                act.wait_ge(hot_ready, upto(turn, p, 1, 1))
                nc.scalar.activation(hot_all[:, b, :], hot[:, :].unsqueeze(1), ACT.Copy).then_inc(hot_copied, 1)
                act.wait_ge(hot_psum, upto(turn, p, 1, 1))
                nc.scalar.activation(hotT_all[:, b, :], ps[0:NTILE, 0:1, :], ACT.Copy).then_inc(hot_turned, 1)

            def start(turn, p):
                inputs(turn, p)
                act.wait_ge(want_step, 1)
                nc.scalar.activation(want[:, :], want[:, :], ACT.Sign).then_inc(want_step, 1)

            by_pairs(act, start, batch)

        @block.vector
        def _(dve):
            nc.vector.memset(one[:, :], 1.0)
            nc.vector.memset(least[:, :], BIG)
            nc.vector.memset(most[:, :], -BIG)
            def moments(turn, p, x, n):
                for k in range(NBLK):
                    done = nc.vector.bn_stats(stats[:, k, :], x[:, k, :])
                done.then_inc(stat_ready, 1)
                wait_apart(dve, stat_ready, upto(turn, p, 2, n + 1), seen)
                for k in range(NBLK):
                    done = nc.vector.bn_aggr(mv[:, k, :], stats[:, k, :])
                done.then_inc(var_ready, 1)

            def normalised(turn, p, dst, x, n, sem):
                dve.wait_ge(var_ready, upto(turn, p, 2, n + 1))
                dve.wait_ge(rstd_ready, upto(turn, p, 2, n + 1))
                for k in range(NBLK):
                    done = nc.vector.tensor_scalar(dst[:, k, :], x[:, k, :], mv[:, k, 0:1], rstd[:, k:k + 1], ALU.subtract, ALU.mult)
                done.then_inc(sem, 1)

            def inputs(turn, p, piece):
                q = p % PAR
                if piece == 0:
                    dve.wait_ge(x_in[q], (turn + p // PAR) * 16 + 16)
                    moments(turn, p, xs[q], 0)
                elif piece == 1:
                    if not (early(turn) and p == 0):
                        dve.wait_ge(xn_copied, upto(turn, p, 1, 0))
                    normalised(turn, p, xn, xs[q], 0, xn_ready)
                    dve.wait_ge(xn_ready, upto(turn, p, 1, 1))
                    moments(turn, p, xn, 1)
                else:
                    normalised(turn, p, xf[q], xn, 1, xf_normed)

            def batch(turn, p, last):
                if not last:
                    inputs(turn, p + 1, 0)
                link = Links(dve, step, 13, turn, p)
                a = w1[0]
                dve.wait_ge(sign_ready, upto(turn, p, 1, 1))
                nc.vector.tensor_tensor(a[:, :, :], sg[:, :, :], want[:, :].unsqueeze(1).broadcast_to([P, NBLK, HID]), ALU.mult).then_inc(agreed, 1)
                dve.wait_ge(agreed, upto(turn, p, 1, 1))
                link(nc.vector.tensor_reduce(ts[:, :], a[:, :, :].rearrange("p k (t j) -> p (k t) j", j=SLICE), AXX, ALU.add))
                link(nc.vector.tensor_reduce(cs[:, :], ts[:, :].rearrange("p (c t) -> p c t", t=PER_CLUSTER), AXX, ALU.add))
                link(nc.vector.scalar_tensor_tensor(cs[:, :], cs[:, :], float(NCLUSTER), cst[:, slice(*col["cluster"])], ALU.mult, ALU.subtract))
                link(nc.vector.tensor_reduce(top[:, :], per_block(cs[:, :]), AXX, ALU.max))
                link(nc.vector.tensor_tensor(per_block(ch[:, :]), per_block(cs[:, :]), top[:, :].unsqueeze(2).broadcast_to([P, NBLK, NCLUSTER]), ALU.is_equal))
                if not last:
                    inputs(turn, p + 1, 1)
                link(nc.vector.scalar_tensor_tensor(ts[:, :], ts[:, :], float(PER_CLUSTER), cst[:, slice(*col["in_cluster"])], ALU.mult, ALU.subtract))
                tiles = ts[:, :].rearrange("p (c t) -> p c t", t=PER_CLUSTER)
                link(nc.vector.scalar_tensor_tensor(tiles, ch[:, :].unsqueeze(2).broadcast_to([P, NBLK * NCLUSTER, PER_CLUSTER]), 1000.0, tiles, ALU.mult, ALU.add))
                link(nc.vector.tensor_reduce(top[:, :], per_block(ts[:, :]), AXX, ALU.max))
                if not (early(turn) and p == 0):
                    dve.wait_ge(hot_psum, upto(turn, p, 1, 0))
                    dve.wait_ge(hot_copied, upto(turn, p, 1, 0))
                nc.vector.tensor_tensor(per_block(hot[:, :]), per_block(ts[:, :]), top[:, :].unsqueeze(2).broadcast_to([P, NBLK, NTILE]), ALU.is_equal).then_inc(hot_ready, 1)
                dve.wait_ge(hot_ready, upto(turn, p, 1, 1))
                if not last:
                    inputs(turn, p + 1, 2)
                link(nc.vector.tensor_tensor(a[:, :, :].rearrange("p k (t j) -> p (k t) j", j=SLICE), xf[p][:, :, :].rearrange("p k (t j) -> p (k t) j", j=SLICE),
                                             hot[:, :].unsqueeze(2).broadcast_to([P, NT, SLICE]), ALU.mult))
                nc.vector.tensor_scalar(pen[:, :], hot[:, :], -BIG, BIG, ALU.mult, ALU.add)
                link(nc.vector.tensor_reduce(sl[:, :].rearrange("p (k j) -> p k j", k=NBLK), a[:, :, :].rearrange("p k (t j) -> p k j t", j=SLICE), AXX, ALU.add))
                nc.vector.tensor_copy(sl_all[:, bass.ds(turn * PAR + p, 1), :], sl[:, :].unsqueeze(1))
                nc.vector.tensor_reduce(ends[:, 0, :], per_block(sl[:, :]), AXX, ALU.min)
                link(nc.vector.tensor_reduce(ends[:, 1, :], per_block(sl[:, :]), AXX, ALU.max))
                nc.vector.tensor_tensor(per_block(lo[:, :]), per_block(hot[:, :]), ends[:, 0, :].unsqueeze(2).broadcast_to([P, NBLK, NTILE]), ALU.mult)
                link(nc.vector.tensor_tensor(per_block(hi[:, :]), per_block(hot[:, :]), ends[:, 1, :].unsqueeze(2).broadcast_to([P, NBLK, NTILE]), ALU.mult))
                nc.vector.tensor_tensor(lo[:, :], lo[:, :], pen[:, :], ALU.add)
                link(nc.vector.tensor_tensor(hi[:, :], hi[:, :], pen[:, :], ALU.subtract))
                nc.vector.tensor_tensor(least[:, :], least[:, :], lo[:, :], ALU.min)
                nc.vector.tensor_tensor(most[:, :], most[:, :], hi[:, :], ALU.max)
                link.close()

            def start(turn, p):
                for piece in range(3):
                    inputs(turn, p, piece)
                dve.wait_ge(w_in, 16 * N_W)
                nc.vector.tensor_reduce(want[:, :], slopes[:, :, :], AXX, ALU.add).then_inc(want_step, 1)
                dve.wait_ge(want_step, 2)

            by_pairs(dve, start, batch)

        first.close()

        ends_ready, ends_psum, table_ready = t.sem("f2_ends_ready"), t.sem("f2_ends_psum"), t.sem("f2_table_ready")
        hot_placed, tab_psum, splined, shifted, sig_step, log_ready, gated, shared, mixed = (
            t.sem("f2_" + n) for n in ("hot_placed", "tab_psum", "splined", "shifted", "sig_step", "log_ready", "gated", "shared", "mixed"))
        stored = [t.sem(f"f2_stored{p}") for p in range(PAR)]
        FIRST_IN = 16 * (B // PAR)
        step2 = t.sem("f2_step")
        block = ctx.enter_context(nc.Block())
        BASES, SLOPES, SCALE, LEAST, MOST = 0, SLICE * GRID, TAB - 3, TAB - 2, TAB - 1

        @block.sync
        def _(sp):
            def load(turn, p):
                b, q = turn * PAR + p, p % PAR
                sp.dma_start(s1[q][:, :, :], tokens(s1_dram, b)).then_inc(x_in[q], 16)
                sp.dma_start(xs[q][:, :, :], tokens(x1_dram, b)).then_inc(x_in[q], 16)

            def batch(turn, p, last):
                sp.wait_ge(mixed, upto(turn, p, 1, 1))
                sp.dma_start(tokens(out, turn * PAR + p), w1[p][:, :, :]).then_inc(stored[p], 16)
                if not final(turn):
                    load(turn, p + PAR)

            load(0, 0)
            load(0, 1)
            by_pairs(sp, None, batch)
            for p in range(PAR):
                sp.wait_ge(stored[p], 16 * (B // PAR))

        @block.tensor
        def _(pe):
            pe.wait_ge(ends_ready, 2)
            for n in range(2):
                done = nc.tensor.transpose(ps[0:NTILE, 1, n * P:(n + 1) * P], ends64[:, n, :], cst[:, slice(*col["ident"])])
            done.then_inc(ends_psum, 1)
            pe.wait_ge(table_ready, 2)

            def lookup(turn, p):
                q = p % PAR
                pe.wait_ge(hot_placed, upto(turn, p, 1, 1))
                if not early(turn, p):
                    pe.wait_ge(splined, upto(turn, p, 1, 1 - PAR))
                for k in range(NBLK):
                    done = nc.tensor.matmul(ps[:, 2 + 2 * q + k // 2, (k % 2) * HID:(k % 2) * HID + TAB], hotT[q][:, k * P:(k + 1) * P], table[:, :],
                                            start=True, stop=True)
                done.then_inc(tab_psum, 1)

            by_pairs(pe, lookup, lambda turn, p, last: None if last else lookup(turn, p + 1))

        @block.scalar
        def _(act):
            def place(turn, p):
                if not early(turn, p):
                    act.wait_ge(tab_psum, upto(turn, p, 1, 1 - PAR))
                nc.scalar.activation(hotT[p % PAR][:, :].unsqueeze(1), hotT_all[:, bass.ds(turn * PAR + p, 1), :], ACT.Copy).then_inc(hot_placed, 1)

            def batch(turn, p, last):
                if not final(turn):
                    place(turn, p + PAR)
                act.wait_ge(shifted, upto(turn, p, 1, 1))
                if not early(turn):
                    act.wait_ge(stored[p], turn * 16)
                sigmoid(act, nc, flat(w1[p]), flat(w2[p]), one, sig_step, log_ready, turn, p)

            place(0, 0)
            place(0, 1)
            by_pairs(act, None, batch)

        @block.gpsimd
        def _(pool):
            def shift(turn, p):
                x = flat(w2[p % PAR])
                wait_apart(pool, splined, upto(turn, p, 1, 1), seen)
                nc.gpsimd.tensor_tensor(x, x, xn_all[:, bass.ds(turn * PAR + p, 1), :].rearrange("p a n -> p (a n)"), ALU.add).then_inc(shifted, 1)

            def batch(turn, p, last):
                if not last:
                    shift(turn, p + 1)
                x = w1[p]
                wait_apart(pool, x_in[p], turn * 32 + (FIRST_IN + 32), seen)
                wait_apart(pool, gated, upto(turn, p, 1, 1), seen)
                nc.gpsimd.tensor_tensor(x[:, :, :], x[:, :, :], s1[p][:, :, :], ALU.mult).then_inc(shared, 1)
                wait_apart(pool, shared, upto(turn, p, 1, 1), seen)
                nc.gpsimd.tensor_tensor(x[:, :, :], x[:, :, :], xs[p][:, :, :], ALU.add).then_inc(mixed, 1)

            by_pairs(pool, shift, batch)

        @block.vector
        def _(dve):
            for n, (src, op) in enumerate(((least, ALU.min), (most, ALU.max))):
                nc.vector.tensor_reduce(ends64[:, n, :], src[:, :].rearrange("p (k t) -> p t k", k=NBLK), AXX, op).then_inc(ends_ready, 1)
            dve.wait_ge(ends_psum, 1)
            for n, op in enumerate((ALU.min, ALU.max)):
                nc.vector.tensor_reduce(table[:, LEAST + n:LEAST + n + 1], ps[0:NTILE, 1, n * P:(n + 1) * P], AXX, op).then_inc(table_ready, 1)

            def four(ap):
                return ap.rearrange("p (k j) -> p k j", j=SLICE)

            def each(ap):
                return ap.unsqueeze(2).broadcast_to([P, NBLK, SLICE])

            def spline(turn, p):
                b, q = bass.ds(turn * PAR + p, 1), p % PAR
                got = ps[:, 2 + 2 * q:4 + 2 * q, :].rearrange("p a (k c) -> p (a k) c", k=2)
                link = Links(dve, step2, 13, turn, p)
                dve.wait_ge(tab_psum, upto(turn, p, 1, 1))
                link(nc.vector.tensor_copy(tab[:, :, :], got[:, :, SCALE:TAB]))
                scale, least_t, most_t = (tab[:, :, n] for n in range(3))
                nc.vector.tensor_tensor(four(sl[:, :]), sl_all[:, b, :].rearrange("p a (k j) -> p (a k) j", j=SLICE), each(least_t), ALU.subtract)
                link(nc.vector.tensor_tensor(rng[:, :], most_t, least_t, ALU.subtract))
                link(nc.vector.tensor_scalar(rng[:, :], rng[:, :], 1e-8, None, ALU.add))
                link(nc.vector.reciprocal(rng[:, :], rng[:, :]))
                link(nc.vector.tensor_tensor(four(sl[:, :]), four(sl[:, :]), each(rng[:, :]), ALU.mult))
                link(nc.vector.tensor_scalar(sl[:, :], sl[:, :], 0.0, U_MAX, ALU.max, ALU.min))
                link(nc.vector.tensor_scalar(sl[:, :], sl[:, :], float(GRID), None, ALU.mult))
                link(nc.vector.tensor_tensor(d[:, :, :], sl[:, :].unsqueeze(2).broadcast_to([P, NBLK * SLICE, GRID]),
                                             cst[:, col["grid"][0]:col["grid"][0] + GRID].unsqueeze(1).broadcast_to([P, NBLK * SLICE, GRID]), ALU.subtract))
                nc.vector.tensor_tensor(cells(val), got[:, :, SLOPES:SLOPES + SLICE * GRID], cells(d), ALU.mult)
                link(nc.vector.tensor_scalar(ge[:, :, :], d[:, :, :], 0.0, None, ALU.is_ge))
                nc.vector.scalar_tensor_tensor(in_[:, :, :], d[:, :, :], 1.0, ge[:, :, :], ALU.is_lt, ALU.mult)
                link(nc.vector.tensor_tensor(cells(val), got[:, :, BASES:BASES + SLICE * GRID], cells(val), ALU.add))
                link(nc.vector.tensor_tensor(val[:, :, :], val[:, :, :], in_[:, :, :], ALU.mult))
                link(nc.vector.tensor_reduce(dl[:, :], val[:, :, :], AXX, ALU.add))
                link(nc.vector.tensor_tensor(four(dl[:, :]), four(dl[:, :]), each(scale), ALU.mult))
                nc.vector.tensor_tensor(w2[q][:, :, :].rearrange("p k (t j) -> p k t j", j=SLICE),
                                        hot_all[:, b, :].rearrange("p a (k t) -> p (a k) t", k=NBLK).unsqueeze(3).broadcast_to([P, NBLK, NTILE, SLICE]),
                                        four(dl[:, :]).unsqueeze(2).broadcast_to([P, NBLK, NTILE, SLICE]), ALU.mult).then_inc(splined, 1)
                link.close()

            def batch(turn, p, last):
                if not last:
                    spline(turn, p + 1)
                log_sigmoid(dve, nc, flat(w1[p]), flat(w2[p]), sig_step, log_ready, turn, p)
                nc.vector.tensor_tensor(w1[p][:, :, :], w1[p][:, :, :], w2[p][:, :, :], ALU.mult).then_inc(gated, 1)

            by_pairs(dve, spline, batch)


def recurrent_d2_kernel(nc, A, cst_cols, cols1, cols2, out):
    with ExitStack() as ctx:
        t = Scope(nc, ctx)
        ps = ctx.enter_context(nc.psum_tensor("ps", [P, 8, S], F32))
        parts_dram = [nc.dram_tensor(f"parts_{n}", [NPART, HD, B * H, S], BF16, kind="Internal").ap() for n in range(4)]
        v_dram = [nc.dram_tensor(f"values_{n}", [B * NG, P, NBLK * GH * (HD + 1)], F32, kind="Internal").ap() for n in range(2)]
        o_dram = [nc.dram_tensor(f"outs_{n}", [B * H, HD + 1, S], F32, kind="Internal").ap() for n in range(2)]
        inv_dram = [nc.dram_tensor(f"inverse_sums_{n}", [B * H, S], F32, kind="Internal").ap() for n in range(2)]
        x1_dram = nc.dram_tensor("x1_dram", [B, S, HID], F32, kind="Internal").ap()
        s1_dram = nc.dram_tensor("s1_dram", [B, S, HID], F32, kind="Internal").ap()
        seen = t.sem("seen")
        w = {}
        layer0 = ctx.enter_context(ExitStack())
        mids = Scope(nc, layer0)
        cst = mids.sb("cst0", [P, A["consts0"].shape[1]])
        with ExitStack() as early:
            e = Scope(nc, early)
            for name, shape, dt in (
                ("o_a", [P, KC, HID], F32), ("o_f", [P, KC, HID], F32),
                ("ident_b", [P, P], BF16), ("mask_qk", [P, P], BF16), ("mask_kq", [P, P], BF16),
            ):
                w[name] = mids.sb(name, shape, dt)
            for name, shape in (
                ("d", [P, KC, 2 * LAT]), ("q_a", [LAT, HID]), ("q_b", [LAT, HID]), ("k_a", [2 * LAT, HID]),
                ("v_a", [2 * LAT, HID]), ("kr_a", [P, KC, HID]), ("kr_b", [P, KC, HID]),
                ("q_f", [P, KC, HID]), ("k_f", [P, KC, HID]), ("v_f", [P, KC, HID]),
            ):
                w[name] = e.sb("w_" + name, shape)
            load_layer0(nc, e, w, cst, cst_cols, A)
            project_layer0(nc, ps, seen, w, cst, cst_cols, A, parts_dram, v_dram)
        attend_layer0(nc, ps, w, cst, cst_cols, parts_dram, v_dram, o_dram)
        gate_layer0(nc, ps, seen, w, cst, cst_cols, A, o_dram, inv_dram, x1_dram)
        layer0.close()
        recur_layer1(nc, ps, seen, cols1, A, x1_dram, s1_dram)
        mix_layer1(nc, ps, seen, cols2, A, x1_dram, s1_dram, out)


_INS = {
    "L0_attn_hidden_states": "x", "L0_attn_w_kv_d": "w_kv_d", "L0_attn_w_q_d": "w_q_d", "L0_attn_w_k_u": "w_k_u",
    "L0_attn_w_q_u": "w_q_u", "L0_attn_w_v_u": "w_v_u", "L0_attn_w_rope_k": "w_rope_k",
    "L0_attn_w_rope_q": "w_rope_q", "L0_attn_w_o": "w_o", "L0_ffn_Wa": "Wa", "L0_ffn_Wp": "Wp",
    "L0_ffn_w_std": "w_std", "L0_ffn_w_rec": "w_rec", "L1_attn_Wq": "Wq", "L1_attn_Wk": "Wk", "L1_attn_Wv": "Wv",
    "L1_attn_Wo": "Wo", "L1_attn_betas": "betas", "L1_ffn_ln_gamma": "gamma", "L1_ffn_ln_beta": "beta",
    "L1_ffn_spline_bases": "bases", "L1_ffn_spline_slopes": "slopes", "L1_ffn_output_scale": "oscale",
}


def kernel(**inputs):
    import concourse.bacc as bacc
    from concourse.bass_utils import run_bass_kernel_spmd

    nc = bacc.Bacc("TRN2", target_bir_lowering=False, num_devices=1)
    consts0, cols0 = shape_constants(0)
    consts1, cols1 = shape_constants(1)
    consts2, cols2 = shape_constants(2)
    arrays, A = {}, {}
    for long, short in _INS.items():
        a = np.ascontiguousarray(inputs[long])
        arrays[f"in_{short}"] = a
        A[short] = nc.dram_tensor(f"in_{short}", a.shape, mybir.dt.from_np(a.dtype), kind="ExternalInput").ap()
    for name, a in (("consts0", consts0), ("consts1", consts1), ("consts2", consts2)):
        arrays["in_" + name] = a
        A[name] = nc.dram_tensor("in_" + name, a.shape, F32, kind="ExternalInput").ap()
    out = nc.dram_tensor("out", (B, S, HID), F32, kind="ExternalOutput").ap()
    recurrent_d2_kernel(nc, A, cols0, cols1, cols2, out)
    r = run_bass_kernel_spmd(nc, [arrays], core_ids=[0])
    return r.results[0]["out"]
```
